# Optimizing a Trainium2 kernel written in Bass

```python
import numpy as np
import jax
import jax.numpy as jnp

def _softmax(x, axis=-1):
    return jax.nn.softmax(x, axis=axis)

def _gelu(x):
    return jax.nn.gelu(x, approximate=True)

def _silu(x):
    return jax.nn.silu(x)

def _sigmoid(x):
    return jax.nn.sigmoid(x)

def _layernorm(x, axis=-1, eps=1e-05):
    m = jnp.mean(x, axis=axis, keepdims=True)
    v = jnp.var(x, axis=axis, keepdims=True)
    return (x - m) / jnp.sqrt(v + eps)

def _scatter_add(tgt, idx, src, axis=0):
    return tgt.at[idx].add(src)

def _segment_sum(src, seg, n):
    return jax.ops.segment_sum(src, seg, n)
kernel_name = 'mk_gnn_preln_d4_gnn_r8_5d4e81'

def setup_inputs(seed: int=0):
    np.random.seed(seed)
    _w = jnp.asarray

    def _rec_inputs():
        import jax
        import jax.numpy as jnp
        _gk = jax.random.key(seed)
        x = -0.0009044 + 1 * jax.random.normal(jax.random.fold_in(_gk, 1), (12500, 16), jnp.float32)
        src = jax.random.randint(jax.random.fold_in(_gk, 2), (400000,), 0, 12500, jnp.int32)
        dst = jnp.minimum((12500 * jax.random.uniform(jax.random.fold_in(_gk, 3), (400000,)) ** 2.0).astype(jnp.int32), 99999)
        _o = jnp.argsort(dst, stable=True)
        src = src[_o]
        dst = dst[_o]
        edge_attr_16 = -0.00010739 + 0.99994 * jax.random.normal(jax.random.fold_in(_gk, 12), (400000, 16), jnp.float32)
        edge_attr_4 = -0.000192005 + 0.999979 * jax.random.normal(jax.random.fold_in(_gk, 13), (400000, 4), jnp.float32)
        edge_type_90 = jax.random.randint(jax.random.fold_in(_gk, 15), (400000,), 0, 90, jnp.int32)
        edge_weight = jax.random.uniform(jax.random.fold_in(_gk, 16), (400000,), jnp.float32, 0.0, 1)
        return (x, src, dst, edge_attr_16, edge_attr_4, edge_type_90, edge_weight)
    x, src, dst, edge_attr_16, edge_attr_4, edge_type_90, edge_weight = _rec_inputs()

    def _L0_gnn_setup():
        import jax, jax.numpy as jnp
        import numpy as np
        N_NODES = 12500
        N_EDGES = 400000
        F_IN, HID, F_OUT = (16, 64, 16)

        def gcn_conv(x, W, b, src, dst, n):
            x = x @ W
            loops = jnp.arange(n, dtype=src.dtype)
            s = jnp.concatenate([src, loops])
            d = jnp.concatenate([dst, loops])
            deg = jax.ops.segment_sum(jnp.ones_like(d, dtype=x.dtype), d, num_segments=n)
            dinv = jnp.where(deg > 0, jax.lax.rsqrt(deg), 0.0)
            norm = dinv[s] * dinv[d]
            out = jax.ops.segment_sum(x[s] * norm[:, None], d, num_segments=n)
            return out + b
        key = jax.random.key(seed)
        ks = jax.random.split(key, 6)
        x = jax.random.normal(ks[0], (N_NODES, F_IN), jnp.float32)
        edge_index = jax.random.randint(ks[1], (2, N_EDGES), 0, N_NODES, dtype=jnp.int32)
        W1 = jax.random.normal(ks[2], (F_IN, HID), jnp.float32) / np.sqrt(F_IN)
        b1 = jnp.zeros((HID,), jnp.float32)
        W2 = jax.random.normal(ks[3], (HID, F_OUT), jnp.float32) / np.sqrt(HID)
        b2 = jnp.zeros((F_OUT,), jnp.float32)
        return {'x': x, 'edge_index': edge_index, 'W1': W1, 'b1': b1, 'W2': W2, 'b2': b2}
    _L0_gnn_all = _L0_gnn_setup()
    _L0_gnn_in = {k: v for k, v in _L0_gnn_all.items() if k in ('W1', 'b1', 'W2', 'b2')}
    del _L0_gnn_all

    def _L1_gnn_setup():
        import jax, jax.numpy as jnp
        import numpy as np
        N, E, IN, OUT, R, B = (6250, 100000, 16, 16, 90, 30)
        key = jax.random.key(seed)
        ks = jax.random.split(key, 9)
        h = jax.random.normal(ks[0], (N, IN), dtype=jnp.float32)
        he = jax.random.normal(ks[1], (E, IN), dtype=jnp.float32)
        Ws = jax.random.normal(ks[2], (OUT, IN), dtype=jnp.float32) * 0.1
        Wa = jax.random.normal(ks[3], (1, 3 * OUT), dtype=jnp.float32) * 0.1
        weight = jax.random.normal(ks[4], (B, IN, OUT), dtype=jnp.float32) * 0.1
        w_comp = jax.random.normal(ks[5], (R, B), dtype=jnp.float32) * 0.1
        src = jax.random.randint(ks[6], (E,), 0, N)
        dst = jax.random.randint(ks[7], (E,), 0, N)
        rel_type = jax.random.randint(ks[8], (E,), 0, R)
        return {'h': h, 'he': he, 'Ws': Ws, 'Wa': Wa, 'weight': weight, 'w_comp': w_comp, 'src': src, 'dst': dst, 'rel_type': rel_type}
    _L1_gnn_all = _L1_gnn_setup()
    _L1_gnn_in = {k: v for k, v in _L1_gnn_all.items() if k in ('Ws', 'Wa', 'weight', 'w_comp')}
    del _L1_gnn_all

    def _L2_gnn_setup():
        import jax, jax.numpy as jnp
        import numpy as np
        N = 12500
        E = 125000
        IN_V = 16
        OUT_V = 16
        IN_E = 4
        EPS = 1e-05
        SLOPE = 0.01
        key = jax.random.key(seed)
        ks = jax.random.split(key, 9)
        v = jax.random.normal(ks[0], (N, IN_V), jnp.float32)
        e = jax.random.normal(ks[1], (E, IN_E), jnp.float32)
        edge_index = jax.random.randint(ks[2], (2, E), 0, N, jnp.int32)
        enet_w = jax.random.normal(ks[3], (IN_V * OUT_V, IN_E), jnp.float32) / np.sqrt(IN_E)
        enet_b = jax.random.normal(ks[4], (IN_V * OUT_V,), jnp.float32) * 0.01
        root = jax.random.normal(ks[5], (IN_V, OUT_V), jnp.float32) / np.sqrt(IN_V)
        bias = jax.random.normal(ks[6], (OUT_V,), jnp.float32) * 0.01
        gamma = jnp.ones((OUT_V,), jnp.float32) + 0.1 * jax.random.normal(ks[7], (OUT_V,), jnp.float32)
        beta = 0.1 * jax.random.normal(ks[8], (OUT_V,), jnp.float32)
        return {'v': v, 'e': e, 'edge_index': edge_index, 'enet_w': enet_w, 'enet_b': enet_b, 'root': root, 'bias': bias, 'gamma': gamma, 'beta': beta}
    _L2_gnn_all = _L2_gnn_setup()
    _L2_gnn_in = {k: v for k, v in _L2_gnn_all.items() if k in ('enet_w', 'enet_b', 'root', 'bias', 'gamma', 'beta')}
    del _L2_gnn_all

    def _L3_gnn_setup():
        import jax, jax.numpy as jnp
        import numpy as np
        N_NODES = 12500
        N_EDGES = 400000
        DIM = 16
        B, K, C, D, E, H = (0.1, 5.0, 1.0, 5.0, 0.9, 0.1)
        E_ = E
        key = jax.random.key(seed)
        k1, k2, k3, k4 = jax.random.split(key, 4)
        x = jax.random.uniform(k1, (N_NODES, DIM), dtype=jnp.float32)
        edge_src = jax.random.randint(k2, (N_EDGES,), 0, N_NODES, dtype=jnp.int32)
        edge_dst = jax.random.randint(k3, (N_EDGES,), 0, N_NODES, dtype=jnp.int32)
        edge_vals = jax.random.uniform(k4, (N_EDGES,), dtype=jnp.float32)
        return {'x': x, 'edge_src': edge_src, 'edge_dst': edge_dst, 'edge_vals': edge_vals}
    _L3_gnn_all = _L3_gnn_setup()
    _L3_gnn_in = {k: v for k, v in _L3_gnn_all.items() if k in ()}
    del _L3_gnn_all
    return {'x': x, 'src': src, 'dst': dst, 'edge_attr_16': edge_attr_16, 'edge_attr_4': edge_attr_4, 'edge_type_90': edge_type_90, 'edge_weight': edge_weight, 'L0_gnn_W1': _L0_gnn_in['W1'], 'L0_gnn_b1': _L0_gnn_in['b1'], 'L0_gnn_W2': _L0_gnn_in['W2'], 'L0_gnn_b2': _L0_gnn_in['b2'], 'L1_gnn_Ws': _L1_gnn_in['Ws'], 'L1_gnn_Wa': _L1_gnn_in['Wa'], 'L1_gnn_weight': _L1_gnn_in['weight'], 'L1_gnn_w_comp': _L1_gnn_in['w_comp'], 'L2_gnn_enet_w': _L2_gnn_in['enet_w'], 'L2_gnn_enet_b': _L2_gnn_in['enet_b'], 'L2_gnn_root': _L2_gnn_in['root'], 'L2_gnn_bias': _L2_gnn_in['bias'], 'L2_gnn_gamma': _L2_gnn_in['gamma'], 'L2_gnn_beta': _L2_gnn_in['beta']}

def reference(x, src, dst, edge_attr_16, edge_attr_4, edge_type_90, edge_weight, L0_gnn_W1, L0_gnn_b1, L0_gnn_W2, L0_gnn_b2, L1_gnn_Ws, L1_gnn_Wa, L1_gnn_weight, L1_gnn_w_comp, L2_gnn_enet_w, L2_gnn_enet_b, L2_gnn_root, L2_gnn_bias, L2_gnn_gamma, L2_gnn_beta):
    import jax
    import jax.numpy as jnp

    def _L0_gnn_ref(x, edge_index, W1, b1, W2, b2):
        import jax, jax.numpy as jnp
        import numpy as np
        N_NODES = 12500
        N_EDGES = 400000
        F_IN, HID, F_OUT = (16, 64, 16)

        def gcn_conv(x, W, b, src, dst, n):
            x = x @ W
            loops = jnp.arange(n, dtype=src.dtype)
            s = jnp.concatenate([src, loops])
            d = jnp.concatenate([dst, loops])
            deg = jax.ops.segment_sum(jnp.ones_like(d, dtype=x.dtype), d, num_segments=n)
            dinv = jnp.where(deg > 0, jax.lax.rsqrt(deg), 0.0)
            norm = dinv[s] * dinv[d]
            out = jax.ops.segment_sum(x[s] * norm[:, None], d, num_segments=n)
            return out + b
        n = x.shape[0]
        src, dst = (edge_index[0], edge_index[1])
        h = jax.nn.relu(gcn_conv(x, W1, b1, src, dst, n))
        return gcn_conv(h, W2, b2, src, dst, n)

    def _L1_gnn_ref(h, he, Ws, Wa, weight, w_comp, src, dst, rel_type):
        import jax, jax.numpy as jnp
        import numpy as np
        N, E, IN, OUT, R, B = (6250, 100000, 16, 16, 90, 30)
        n_nodes, in_dim = h.shape
        num_bases, _, out_dim = weight.shape
        num_rels = w_comp.shape[0]
        V = weight.reshape(in_dim, num_bases, out_dim)
        W_rel = jnp.matmul(w_comp, V).reshape(num_rels, in_dim, out_dim)
        h_src = h[src]
        z_src = h_src @ Ws.T
        z_dst = h[dst] @ Ws.T
        z_e = he @ Ws.T
        e = jnp.concatenate([z_src, z_e, z_dst], axis=1) @ Wa.T
        msg = jnp.einsum('ei,eio->eo', h_src, W_rel[rel_type]) * e
        h_out = jax.ops.segment_sum(msg, dst, num_segments=n_nodes)
        return h_out

    def _L2_gnn_ref(v, e, edge_index, enet_w, enet_b, root, bias, gamma, beta):
        import jax, jax.numpy as jnp
        import numpy as np
        N = 12500
        E = 125000
        IN_V = 16
        OUT_V = 16
        IN_E = 4
        EPS = 1e-05
        SLOPE = 0.01
        n = v.shape[0]
        src, dst = (edge_index[0], edge_index[1])
        w = (e @ enet_w.T + enet_b).reshape(-1, IN_V, OUT_V)
        msg = jnp.einsum('ei,eio->eo', v[src], w)
        summed = jax.ops.segment_sum(msg, dst, num_segments=n)
        cnt = jax.ops.segment_sum(jnp.ones((msg.shape[0],), v.dtype), dst, num_segments=n)
        out = summed / jnp.clip(cnt, 1.0)[:, None]
        out = out + v @ root + bias
        mu = out.mean(axis=0)
        var = out.var(axis=0)
        out = gamma * (out - mu) * jax.lax.rsqrt(var + EPS) + beta
        return jnp.where(out >= 0, out, SLOPE * out)

    def _L3_gnn_ref(x, edge_src, edge_dst, edge_vals):
        import jax, jax.numpy as jnp
        import numpy as np
        N_NODES = 12500
        N_EDGES = 400000
        DIM = 16
        B, K, C, D, E, H = (0.1, 5.0, 1.0, 5.0, 0.9, 0.1)
        E_ = E
        n = x.shape[0]
        f = B + x * (1.0 - x / K) * (x / C - 1.0)
        xi = x[edge_src]
        xj = x[edge_dst]
        msg = edge_vals[:, None] * xi * xj / (D + E_ * xi + H * xj)
        f = f + jax.ops.segment_sum(msg, edge_src, num_segments=n)
        return f
    edge_index = jnp.stack([src, dst])
    h = jnp.maximum(_layernorm(x, axis=-1), 0.0)
    x = x + _L0_gnn_ref(h, edge_index, L0_gnn_W1, L0_gnn_b1, L0_gnn_W2, L0_gnn_b2)
    h = jnp.maximum(_layernorm(x, axis=-1), 0.0)
    x = x + _L1_gnn_ref(h, edge_attr_16, L1_gnn_Ws, L1_gnn_Wa, L1_gnn_weight, L1_gnn_w_comp, src, dst, edge_type_90)
    h = jnp.maximum(_layernorm(x, axis=-1), 0.0)
    x = x + _L2_gnn_ref(h, edge_attr_4, edge_index, L2_gnn_enet_w, L2_gnn_enet_b, L2_gnn_root, L2_gnn_bias, L2_gnn_gamma, L2_gnn_beta)
    h = jnp.maximum(_layernorm(x, axis=-1), 0.0)
    x = x + _L3_gnn_ref(h, src, dst, edge_weight)
    return x

_drawn_inputs = setup_inputs


def setup_inputs(seed=0):
    import zlib

    import numpy as np

    out = dict(_drawn_inputs(seed))
    spreads = {'L0_gnn_b1': (0.0, 0.1), 'L0_gnn_b2': (0.0, 0.1)}
    factors = {'L2_gnn_enet_b': 8.0, 'L2_gnn_bias': 8.0}
    for name, (base, spread) in spreads.items():
        noise = np.random.default_rng([zlib.crc32(name.encode()), seed]).standard_normal(out[name].shape)
        drawn = base * np.exp(spread * noise) if base else spread * noise
        out[name] = jnp.asarray(drawn.astype(out[name].dtype))
    for name, factor in factors.items():
        out[name] = (out[name] * factor).astype(out[name].dtype)
    return out
```

```python
from contextlib import ExitStack

import concourse.bass as bass
from concourse import mybir

ALU = mybir.AluOpType
ACT = mybir.ActivationFunctionType
AX = mybir.AxisListType
F32 = mybir.dt.float32
F16 = mybir.dt.float16
BF16 = mybir.dt.bfloat16
I32 = mybir.dt.int32

P = 128
F = 16
TILES = 25
WIN = 4
GROUP = 4
COPIES = 5
PARTS = 3
BANK = 512
EPS = 1e-5
SLOPE = 0.01
FB, FK, FC, FD, FE, FH = 0.1, 5.0, 1.0, 5.0, 0.9, 0.1


def build_program(nc, x, src, dst, edge_attr_16, edge_attr_4, edge_type_90, edge_weight, gcn_w1, gcn_b1, gcn_w2,
                  gcn_b2, rel_ws, rel_wa, rel_weight, rel_comp, net_w, net_b, net_root, net_bias, net_gamma,
                  net_beta, out):
    N = x.shape[0]
    E = src.shape[0]
    CE = P * TILES
    CHUNKS = E // CE
    NWIN = (N + P - 1) // P
    NGRP = (NWIN + GROUP - 1) // GROUP
    NW = NGRP * GROUP
    NROW = NW * P
    AW = NW + WIN
    LAST = N - (NWIN - 1) * P
    HID = gcn_w1.shape[1]
    BASES = rel_weight.shape[0]
    RELS = rel_comp.shape[0]
    KE = edge_attr_4.shape[1]
    RW = F + 1
    RPB = BANK // RW
    RBANKS = RELS // RPB
    NETW = (KE + 1) * F
    NODEW = NETW + F
    assert E == CE * CHUNKS and CHUNKS % 2 == 1 and RELS == RPB * RBANKS and TILES % COPIES == 0
    PAIRS = CHUNKS // 2
    SPAN = WIN * P
    LAND = 16 * TILES

    tab1 = nc.dram_tensor("tab1", [NROW, F], F32).ap()
    tab2 = nc.dram_tensor("tab2", [NROW, F], F32).ap()
    tab_rel = nc.dram_tensor("tab_rel", [NROW * RELS, RW], F32).ap()
    tab_net = nc.dram_tensor("tab_net", [NROW, NETW], F32).ap()
    tab3 = nc.dram_tensor("tab3", [NROW, F], F32).ap()
    rel_index = nc.dram_tensor("rel_index", [E], I32).ap()
    w_rel_flat = nc.dram_tensor("w_rel_flat", [RELS * F * F], F32).ap()
    meta_dram = nc.dram_tensor("meta_dram", [CHUNKS, 4], I32).ap()
    base_dram = nc.dram_tensor("base_dram", [CHUNKS], F32).ap()
    sums = [nc.dram_tensor(f"sums{k}", [N + P, F], F32).ap() for k in range(COPIES)]

    def by_window(t):
        return t.rearrange("(w r) f -> r w f", r=P)

    def by_chunk(t):
        return t.rearrange("(c p j) -> c p j", p=P, j=TILES)

    def resident(t):
        return t.rearrange("(c p j) -> p c j", p=P, j=TILES)

    ctx = ExitStack()
    with ctx:
        def sb(name, shape, dt=F32):
            return ctx.enter_context(nc.sbuf_tensor(name, shape, dt))

        def sem(name):
            return ctx.enter_context(nc.semaphore(name))

        ctx.enter_context(nc.allow_non_contiguous_dma("rows of 64 bytes, small weights"))

        xs = sb("xs", [P, NW, F])
        h = sb("h", [P, NW, F])
        g = sb("g", [P, NW, F])
        tmp = sb("tmp", [P, NW, F])
        own = sb("own", [P, NW, F])
        acc = sb("acc", [P, AW, 2 * F])
        deg = sb("deg", [P, AW, 1])
        dinv = sb("dinv", [P, NW])
        row_a = sb("row_a", [P, NW])
        row_b = sb("row_b", [P, NW])
        valid = sb("valid", [P, NW])
        dst_f = sb("dst_f", [P, CHUNKS * TILES])
        wt = sb("wt", [P, CHUNKS * TILES])
        span = sb("span", [CHUNKS, 4], I32)
        meta = sb("meta", [CHUNKS, 4], I32)
        passes_f = sb("passes_f", [CHUNKS, 1])
        base_f = sb("base_f", [CHUNKS, 1])
        meta_row = sb("meta_row", [1, CHUNKS * 4], I32)
        base_all = sb("base_all", [P, CHUNKS])
        before = sb("before", [P, P])
        earlier = sb("earlier", [P, P], BF16)
        identity = sb("identity", [P, P])
        ones_f = sb("ones_f", [P, P])
        ones_b = sb("ones_b", [P, 1], BF16)
        iota_span = sb("iota_span", [P, SPAN], F16)
        spare = sb("spare", [P, 1])
        hot = sb("hot", [P, TILES, SPAN], BF16)
        ints = hot[:, :, :].rearrange("p j n -> p (j n)").bitcast(I32)
        int_a = ints[:, 0:CHUNKS * TILES]
        int_b = ints[:, CHUNKS * TILES:2 * CHUNKS * TILES]
        parts = sb("parts", [P, TILES, PARTS, 2 * F], BF16)
        dst_rel = sb("dst_rel", [P, TILES])
        index = [sb(f"index{s}", [P, TILES], I32) for s in range(2)]
        index_j = [sb(f"index_j{s}", [P, TILES], I32) for s in range(2)]
        rows = [sb(f"rows{s}", [P, TILES, NETW]) for s in range(2)]
        attr = [sb(f"attr{s}", [P, TILES, F]) for s in range(2)]
        msg = sb("msg", [P, TILES, 2 * F])
        work = sb("work", [P, TILES, KE * F])
        rest = sb("rest", [P, TILES, 2 * F])
        score = sb("score", [P, TILES])
        part_sum = sb("part_sum", [P, WIN, 2 * F])
        src_row = [sb(f"src_row{s}", [P, CE], I32) for s in range(2)]
        span_in = src_row[0][0:CHUNKS, :]
        seen = sb("seen", [P, TILES])
        scat = [sb(f"scat{s}", [P, TILES, F]) for s in range(2)]
        scat_index = [sb(f"scat_index{s}", [P, TILES], I32) for s in range(2)]
        stage = sb("stage", [P, GROUP, F])
        turned = sb("turned", [F, GROUP, P])
        hid = sb("hid", [HID, GROUP * P])
        rel_out = [r[:, 0:RELS * RW].bitcast(F32) for r in src_row]
        net_out = sb("net_out", [P, GROUP, NETW])
        w1 = sb("w1", [F, HID])
        w2 = sb("w2", [HID, F])
        b1 = sb("b1", [HID, 1])
        b2 = sb("b2", [P, F])
        ws = sb("ws", [F, F])
        wa = sb("wa", [F, 3])
        wa_wide = sb("wa_wide", [F, 3, P])
        a_rows = sb("a_rows", [P, 3, F])
        a_col = sb("a_col", [F, 1])
        comp = sb("comp", [BASES, RELS])
        bases = sb("bases", [BASES, F, F])
        w_rel_sb = sb("w_rel_sb", [RELS, F * F])
        rel_rhs = sb("rel_rhs", [F, RELS, RW])
        net_rhs = sb("net_rhs", [F, NODEW // F, F])
        bias = sb("bias", [P, F])
        gamma = sb("gamma", [P, F])
        beta = sb("beta", [P, F])
        col_sum = sb("col_sum", [P, F])
        mean = sb("mean", [P, F])
        scale = sb("scale", [P, F])

        pass_ps = ctx.enter_context(nc.psum_tensor("pass_ps", [P, BANK], F32))
        turn_ps = ctx.enter_context(nc.psum_tensor("turn_ps", [P, BANK], F32))
        big_ps = [ctx.enter_context(nc.psum_tensor(f"big_ps{k}", [P, RBANKS, BANK], F32)) for k in range(2)]

        pool_turns = sem("pool_turns")
        consts = sem("consts")
        in_x = sem("in_x")
        in_small = sem("in_small")
        in_span = sem("in_span")
        in_dst = sem("in_dst")
        in_srctype = sem("in_srctype")
        in_wt = sem("in_wt")
        setup = sem("setup")
        setup_pe = sem("setup_pe")
        meta_out = sem("meta_out")
        meta_in = sem("meta_in")
        relidx_out = sem("relidx_out")
        w_rel_out = sem("w_rel_out")
        w_rel_in = sem("w_rel_in")
        zeroed = sem("zeroed")
        var_ready = sem("var_ready")
        root_done = sem("root_done")
        table_ready = sem("table_ready")
        table_out = [sem(f"table_out{k}") for k in range(5)]
        hot_ready = {s: sem(f"hot_ready_{s}") for s in ("deg", "conv1", "conv2", "rel", "net")}
        pass_done = {s: sem(f"pass_done_{s}") for s in hot_ready}
        gathering = ("conv1", "conv2", "rel", "net", "rat")
        index_in = {s: [sem(f"index_in_{s}{k}") for k in range(2)] for s in gathering}
        gathered = {s: [sem(f"gathered_{s}{k}") for k in range(2)] for s in gathering}
        rows_free = {s: [sem(f"rows_free_{s}{k}") for k in range(2)] for s in gathering}
        attr_in = {s: [sem(f"attr_in_{s}{k}") for k in range(2)] for s in ("rel", "net")}
        src_row_in = [sem(f"src_row_in{k}") for k in range(2)]
        equal_ready = sem("equal_ready")
        equal_done = sem("equal_done")
        scat_ready = [sem(f"scat_ready{k}") for k in range(2)]
        scattered = [sem(f"scattered{k}") for k in range(COPIES)]
        staged = {s: sem(f"staged_{s}") for s in ("hidden", "rel", "net")}
        turned_ps_ready = {s: sem(f"turned_ps_ready_{s}") for s in staged}
        turned_ready = {s: sem(f"turned_ready_{s}") for s in staged}
        product_ready = {s: sem(f"product_ready_{s}") for s in staged}
        hid_ready = sem("hid_ready")
        hid_ps_ready = sem("hid_ps_ready")
        node_ready = sem("node_ready")
        rel_copied = [sem(f"rel_copied{k}") for k in range(2)]
        rel_stored = [sem(f"rel_stored{k}") for k in range(2)]
        net_copied = sem("net_copied")
        net_stored = sem("net_stored")
        node_done = sem("node_done")
        bn_ready = sem("bn_ready")
        bn_sum = sem("bn_sum")
        sums_ready = sem("sums_ready")
        sums_in = sem("sums_in")
        out_ready = sem("out_ready")
        stored = sem("stored")

        def chunks(eng, body):
            with eng.Fori(0, PAIRS) as i:
                body(i * 2, 0, i)
                body(i * 2 + 1, 1, i)
            body(CHUNKS - 1, 0, PAIRS)

        def parts_view(width):
            return parts[:, :, :, :].rearrange("p j s f -> p (j s f)")[:, 0:TILES * PARTS * width]

        block = ctx.enter_context(nc.Block())

        @block.sync
        def _(sp):
            sp.dma_start(span_in, dst.rearrange("(c e) -> c e", e=CE)).then_inc(in_span, 16)
            sp.dma_start(int_a.rearrange("p (c j) -> p c j", j=TILES), resident(dst)).then_inc(in_dst, 16)
            sp.wait_ge(setup, 1)
            sp.dma_start(xs[:, 0:NWIN - 1, :], by_window(x[0:(NWIN - 1) * P, :])).then_inc(in_x, 16)
            sp.dma_start(xs[0:LAST, NWIN - 1, :], x[(NWIN - 1) * P:N, :]).then_inc(in_x, 16)
            for to, of in (
                (w1[:, :], gcn_w1), (w2[:, :], gcn_w2), (b1[:, :], gcn_b1.rearrange("(k a) -> k a", a=1)),
                (b2[:, :], gcn_b2.rearrange("(a f) -> a f", a=1).broadcast_to([P, F])),
                (ws[:, :], rel_ws), (wa[:, :], rel_wa.rearrange("a (t k) -> k (a t)", k=F)),
                (comp[:, :], rel_comp.rearrange("r b -> b r")),
                (bases[:, :, :], rel_weight.rearrange("b i o -> (b i o)").rearrange("(i b o) -> b i o", b=BASES, o=F)),
                (net_rhs[:, KE, :], net_b.rearrange("(i o) -> i o", o=F)), (net_rhs[:, KE + 1, :], net_root),
                (bias[:, :], net_bias.rearrange("(a f) -> a f", a=1).broadcast_to([P, F])),
                (gamma[:, :], net_gamma.rearrange("(a f) -> a f", a=1).broadcast_to([P, F])),
                (beta[:, :], net_beta.rearrange("(a f) -> a f", a=1).broadcast_to([P, F])),
            ):
                sp.dma_start(to, of).then_inc(in_small, 16)
            for k in range(KE):
                sp.dma_start(net_rhs[:, k, :], net_w[:, k].rearrange("(i o) -> i o", o=F)).then_inc(in_small, 16)
            sp.wait_ge(setup, 2)
            sp.dma_start(int_a.rearrange("p (c j) -> p c j", j=TILES), resident(src)).then_inc(in_srctype, 16)
            sp.dma_start(int_b.rearrange("p (c j) -> p c j", j=TILES),
                         resident(edge_type_90)).then_inc(in_srctype, 16)
            sp.dma_start(wt[:, :].rearrange("p (c j) -> p c j", j=TILES), resident(edge_weight)).then_inc(in_wt, 16)
            sp.wait_ge(setup, 3)
            sp.dma_start(meta_dram, meta[:, :]).then_inc(meta_out, 16)
            sp.dma_start(base_dram.rearrange("(c a) -> c a", a=1), base_f[:, :]).then_inc(meta_out, 16)
            sp.wait_ge(meta_out, 32)
            sp.dma_start(meta_row[:, :], meta_dram.rearrange("c k -> (c k)").rearrange("(a n) -> a n", a=1))\
                .then_inc(meta_in, 16)
            sp.dma_start(base_all[:, :], base_dram.rearrange("(a c) -> a c", a=1).broadcast_to([P, CHUNKS]))\
                .then_inc(meta_in, 16)
            sp.wait_ge(setup, 4)
            sp.dma_start(resident(rel_index), int_b.rearrange("p (c j) -> p c j", j=TILES))\
                .then_inc(relidx_out, 16)
            sp.wait_ge(setup, 5)
            sp.dma_start(w_rel_flat.rearrange("(i r o) -> r i o", r=RELS, o=F),
                         w_rel_sb[:, :].rearrange("r (i o) -> r i o", o=F)).then_inc(w_rel_out, 16)
            sp.wait_ge(w_rel_out, 16)
            sp.dma_start(rel_rhs[:, :, 0:F], w_rel_flat.rearrange("(r i o) -> i r o", i=F, o=F)).then_inc(w_rel_in, 16)
            sp.wait_ge(zeroed, 1)
            for k in range(COPIES):
                sp.dma_start(by_window(sums[k][0:(NWIN - 1) * P, :]), acc[:, 0:NWIN - 1, 0:F]).then_inc(zeroed, 16)
                sp.dma_start(sums[k][(NWIN - 1) * P:N, :], acc[0:LAST, NWIN - 1, 0:F]).then_inc(zeroed, 16)
                sp.dma_start(sums[k][N:N + P, :], acc[:, 0, 0:F]).then_inc(zeroed, 16)
            sp.wait_ge(zeroed, 1 + 48 * COPIES)
            sp.sem_inc(zeroed, 1)

            def table(k, to):
                sp.wait_ge(table_ready, k + 1)
                sp.dma_start(by_window(to), g[:, :, :]).then_inc(table_out[k], 16)

            def feed(name, index_of, attr_of=None, width=F):
                def body(c, s, use):
                    sp.wait_ge(rows_free[name][s], use + 1)
                    sp.dma_start(index[s][:, :], by_chunk(index_of)[bass.ds(c, 1), :, :]
                                 .rearrange("a p j -> (a p) j")).then_inc(index_in[name][s], 16)
                    if attr_of is not None:
                        sp.dma_start(attr[s][:, :, 0:width], attr_of.rearrange("(c p j) k -> c p j k", p=P, j=TILES)
                                     [bass.ds(c, 1), :, :, :].rearrange("a p j k -> (a p) j k"))\
                            .then_inc(attr_in[name][s], 16)
                chunks(sp, body)

            table(0, tab1)
            feed("conv1", src)
            table(1, tab2)
            feed("conv2", src)

            with sp.Fori(0, NGRP) as i:
                for w in range(GROUP):
                    s = w % 2
                    sp.wait_ge(rel_copied[s], i * 4 + (w // 2) * 2 + 3)
                    sp.dma_start(tab_rel.rearrange("(n r) f -> n (r f)", r=RELS)[bass.ds((i * GROUP + w) * P, P), :],
                                 rel_out[s]).then_inc(rel_stored[s], 16)
            for s in range(2):
                sp.wait_ge(rel_stored[s], 16 * NW // 2 + 16)
            sp.wait_ge(relidx_out, 16)
            sp.sem_inc(table_out[2], 16)
            feed("rel", rel_index, edge_attr_16)

            with sp.Fori(0, NGRP) as i:
                sp.wait_ge(net_copied, i + 1)
                sp.dma_start(by_window(tab_net)[:, bass.ds(i * GROUP, GROUP), :], net_out[:, :, :])\
                    .then_inc(net_stored, 16)
            sp.wait_ge(net_stored, 16 * NGRP + 16)
            sp.sem_inc(table_out[3], 16)
            feed("net", src, edge_attr_4, KE)

            sp.wait_ge(table_ready, 3)
            sp.dma_start(by_window(tab3), g[:, :, :]).then_inc(table_out[4], 16)

            def feed_rational(c, s, use):
                sp.wait_ge(rows_free["rat"][s], use + 1)
                sp.dma_start(index[s][:, :], by_chunk(src)[bass.ds(c, 1), :, :]
                             .rearrange("a p j -> (a p) j")).then_inc(index_in["rat"][s], 16)
                sp.dma_start(index_j[s][:, :], by_chunk(dst)[bass.ds(c, 1), :, :]
                             .rearrange("a p j -> (a p) j")).then_inc(index_in["rat"][s], 16)
                sp.dma_start(src_row[s][:, :], src.rearrange("(c e) -> c e", e=CE)[bass.ds(c, 1), :]
                             .broadcast_to([P, CE])).then_inc(src_row_in[s], 16)
            chunks(sp, feed_rational)

            sp.wait_ge(sums_ready, 1)
            for k in range(COPIES):
                sp.wait_ge(scattered[k], 16 * CHUNKS * TILES // COPIES)
            loads = (acc[:, 0:NW, 0:F], acc[:, 0:NW, F:2 * F], tmp[:, :, :], h[:, :, :], g[:, :, :])
            for k in range(COPIES):
                sp.dma_start(loads[k][:, 0:NWIN - 1, :], by_window(sums[k][0:(NWIN - 1) * P, :])).then_inc(sums_in, 16)
                sp.dma_start(loads[k][0:LAST, NWIN - 1, :], sums[k][(NWIN - 1) * P:N, :]).then_inc(sums_in, 16)
            sp.wait_ge(out_ready, 1)
            sp.dma_start(by_window(out[0:(NWIN - 1) * P, :]), xs[:, 0:NWIN - 1, :]).then_inc(stored, 16)
            sp.dma_start(out[(NWIN - 1) * P:N, :], xs[0:LAST, NWIN - 1, :]).then_inc(stored, 16)
            sp.wait_ge(stored, 32)

        @block.gpsimd
        def _(pool):
            pool.memset(before[:, :], 1.0)
            pool.memset(earlier[:, :], 1.0)
            pool.memset(identity[:, :], 0.0)
            pool.memset(ones_f[:, :], 1.0)
            pool.memset(ones_b[:, :], 1.0)
            pool.iota(iota_span[:, :], pattern=[[1, SPAN]], base=0, channel_multiplier=0,
                      allow_small_or_imprecise_dtypes=True)
            pool.iota(spare[:, :], pattern=[[0, 1]], base=N, channel_multiplier=1,
                      allow_small_or_imprecise_dtypes=True)
            pool.iota(valid[:, :], pattern=[[P, NW]], base=0, channel_multiplier=1,
                      allow_small_or_imprecise_dtypes=True)
            pool.drain()
            pool.affine_select(out=before[:, :], in_=before[:, :], compare_op=ALU.is_gt, fill=0.0, base=0,
                               pattern=[[1, P]], channel_multiplier=-1)
            pool.affine_select(out=earlier[:, :], in_=earlier[:, :], compare_op=ALU.is_gt, fill=0.0, base=0,
                               pattern=[[-1, P]], channel_multiplier=1)
            pool.affine_select(out=identity[:, :], in_=identity[:, :], compare_op=ALU.not_equal, fill=1.0, base=0,
                               pattern=[[-1, P]], channel_multiplier=1)
            pool.drain().then_inc(consts, 1)

            def alone():
                pool.sem_inc(pool_turns, 1)

            def gather(name, table, width, number):
                pool.wait_ge(table_out[number], 16)

                def body(c, s, use):
                    pool.wait_ge(index_in[name][s], use * 16 + 16)
                    pool.wait_ge(rows_free[name][s], use + 1)
                    alone()
                    for j in range(TILES):
                        pool.indirect_dma_start(
                            out=rows[s][:, j, 0:width], out_offset=None, in_=table,
                            in_offset=bass.IndirectOffsetOnAxis(ap=index[s][:, j:j + 1], axis=0),
                        ).then_inc(gathered[name][s], 16)
                chunks(pool, body)

            gather("conv1", tab1, F, 0)
            gather("conv2", tab2, F, 1)
            gather("rel", tab_rel, RW, 2)
            gather("net", tab_net, NETW, 3)

            pool.wait_ge(table_out[4], 16)
            pool.wait_ge(zeroed, 2 + 48 * COPIES)

            def gather_both(s, use):
                pool.wait_ge(index_in["rat"][s], use * 32 + 32)
                pool.wait_ge(rows_free["rat"][s], use + 1)
                alone()
                for j in range(TILES):
                    for k, ix in enumerate((index[s], index_j[s])):
                        pool.indirect_dma_start(
                            out=rows[s][:, j, k * F:k * F + F], out_offset=None, in_=tab3,
                            in_offset=bass.IndirectOffsetOnAxis(ap=ix[:, j:j + 1], axis=0),
                        ).then_inc(gathered["rat"][s], 16)

            def scatter(c, s, use, first=False):
                pool.wait_ge(scat_ready[s], use + 1)
                for j in range(TILES):
                    k = j % COPIES
                    if not (first and j < COPIES):
                        pool.wait_ge(scattered[k], c * (16 * TILES // COPIES) + 16 * (j // COPIES))
                    alone()
                    pool.indirect_dma_start(
                        out=sums[k], out_offset=bass.IndirectOffsetOnAxis(ap=scat_index[s][:, j:j + 1], axis=0),
                        in_=scat[s][:, j, :], in_offset=None, compute_op=ALU.add,
                        bounds_check=N + P - 1,
                    ).then_inc(scattered[k], 16)

            gather_both(0, 0)
            gather_both(1, 0)
            scatter(0, 0, 0, first=True)
            gather_both(0, 1)
            scatter(1, 1, 0)
            with pool.Fori(1, PAIRS) as i:
                gather_both(1, i)
                scatter(i * 2, 0, i)
                gather_both(0, i + 1)
                scatter(i * 2 + 1, 1, i)
            scatter(CHUNKS - 1, 0, PAIRS)

        @block.scalar
        def _(act):
            def root(k):
                act.wait_ge(var_ready, k)
                act.activation(row_b[:, :], row_a[:, :], ACT.Sqrt)
                act.drain().then_inc(root_done, 1)

            def turn(name, i):
                of = g if name == "hidden" else h
                act.activation(stage[:, :, :], of[:, bass.ds(i * GROUP, GROUP), :], ACT.Copy)
                act.drain().then_inc(staged[name], 1)
                act.wait_ge(turned_ps_ready[name], i + 1)
                act.activation(turned[:, :, :].rearrange("k w r -> k (w r)"), turn_ps[0:F, :], ACT.Copy)
                act.drain().then_inc(turned_ready[name], 1)

            root(1)
            root(2)
            act.wait_ge(node_ready, 1)
            act.wait_ge(in_small, 16 * (13 + KE))
            with act.Fori(0, NGRP) as i:
                turn("hidden", i)
                act.wait_ge(hid_ps_ready, i + 1)
                act.activation(hid[:, :], big_ps[0][0:HID, 0, :], ACT.Relu, bias=b1[:, 0:1])
                act.drain().then_inc(hid_ready, 1)
                act.wait_ge(product_ready["hidden"], i + 1)
                act.activation(tmp[:, bass.ds(i * GROUP, GROUP), :],
                               big_ps[1][:, 0, 0:GROUP * F].rearrange("p (w f) -> p w f", f=F), ACT.Copy)
                act.drain()
            act.drain().then_inc(node_done, 1)
            root(3)
            act.wait_ge(node_ready, 2)
            for s in range(2):
                act.sem_inc(rel_stored[s], 16)
            with act.Fori(0, NGRP) as i:
                turn("rel", i)
                for w in range(GROUP):
                    s = w % 2
                    act.wait_ge(product_ready["rel"], i * GROUP + w + 1)
                    act.wait_ge(rel_stored[s], (i * 2 + w // 2) * 16 + 16)
                    for b in range(RBANKS - 1 - s):
                        act.activation(rel_out[s][:, b * RPB * RW:(b + 1) * RPB * RW], big_ps[s][:, b, 0:RPB * RW],
                                       ACT.Copy)
                    act.drain().then_inc(rel_copied[s], 1)
            root(4)
            act.wait_ge(node_ready, 3)
            act.sem_inc(net_stored, 16)
            with act.Fori(0, NGRP) as i:
                turn("net", i)
                act.wait_ge(product_ready["net"], i + 1)
                act.wait_ge(net_stored, i * 16 + 16)
                ps = big_ps[0][:, 0, 0:GROUP * NODEW].rearrange("p (w k) -> p w k", k=NODEW)
                act.activation(net_out[:, :, :], ps[:, :, 0:NETW], ACT.Copy)
                act.activation(own[:, bass.ds(i * GROUP, GROUP), :], ps[:, :, NETW:NODEW], ACT.Copy)
                act.drain().then_inc(net_copied, 1)
            act.drain().then_inc(node_done, 1)
            act.wait_ge(bn_ready, 3)
            act.activation(scale[:, :], col_sum[:, :], ACT.Sqrt)
            act.drain().then_inc(root_done, 1)
            root(5)

        @block.tensor
        def _(pe):
            pe.wait_ge(consts, 1)
            pe.wait_ge(setup_pe, 1)
            pe.matmul(turn_ps[0:CHUNKS, 0:1], before[0:CHUNKS, 0:CHUNKS], passes_f[:, :], start=True, stop=True)
            pe.drain().then_inc(setup_pe, 1)
            pe.wait_ge(in_small, 16 * (13 + KE))
            pe.wait_ge(setup_pe, 3)
            pe.matmul(big_ps[0][0:RELS, 0, 0:F * F], comp[:, :], bases[:, :, :].rearrange("b i o -> b (i o)"),
                      start=True, stop=True)
            for t in range(3):
                pe.matmul(big_ps[0][:, 1, t * F:t * F + F], wa_wide[:, t, :], ws[:, :], start=(t == 0), stop=(t == 2),
                          skip_group_check=True)
            pe.matmul(big_ps[0][0:F, 2, 0:1], ws[:, :], wa[:, 0:1], start=True, stop=True)
            pe.drain().then_inc(setup_pe, 1)
            pe.wait_ge(meta_in, 32)

            def sum_windows(name, width):
                with pe.Fori(0, CHUNKS) as c:
                    passes = pe.value_load(meta_row[0:1, bass.ds(c * 4 + 1, 1)], min_val=1, max_val=NWIN)
                    first = pe.value_load(meta_row[0:1, bass.ds(c * 4 + 2, 1)], min_val=0, max_val=NWIN * CHUNKS)
                    with pe.Fori(0, passes) as k:
                        pe.wait_ge(hot_ready[name], first + k + 1)
                        for j in range(TILES):
                            for w in range(WIN):
                                rhs = ones_b[:, :] if name == "deg" else \
                                    parts_view(width)[:, j * PARTS * width:(j + 1) * PARTS * width]
                                n = rhs.shape[1]
                                pe.matmul(pass_ps[:, w * n:w * n + n], hot[:, j, w * P:w * P + P], rhs,
                                          start=(j == 0 and w == 0), stop=(j == TILES - 1),
                                          skip_group_check=True)
                        pe.drain().then_inc(pass_done[name], 1)

            def turn(name, i):
                pe.wait_ge(staged[name], i + 1)
                for w in range(GROUP):
                    pe.transpose(turn_ps[0:F, w * P:w * P + P], stage[:, w, :], identity[:, :])
                pe.drain().then_inc(turned_ps_ready[name], 1)
                pe.wait_ge(turned_ready[name], i + 1)

            sum_windows("deg", 0)
            sum_windows("conv1", F)
            with pe.Fori(0, NGRP) as i:
                turn("hidden", i)
                pe.matmul(big_ps[0][0:HID, 0, :], w1[:, :], turned[:, :, :].rearrange("k w r -> k (w r)"),
                          start=True, stop=True)
                pe.drain().then_inc(hid_ps_ready, 1)
                pe.wait_ge(hid_ready, i + 1)
                for w in range(GROUP):
                    pe.matmul(big_ps[1][:, 0, w * F:w * F + F], hid[:, w * P:w * P + P], w2[:, :],
                              start=(w == 0), stop=(w == GROUP - 1), skip_group_check=True)
                pe.drain().then_inc(product_ready["hidden"], 1)
            sum_windows("conv2", F)
            rel_flat = rel_rhs[:, :, :].rearrange("i r o -> i (r o)")
            with pe.Fori(0, NGRP) as i:
                turn("rel", i)
                for w in range(GROUP):
                    if w < 2:
                        pe.wait_ge(rel_copied[w], i * 4 + 1)
                    else:
                        pe.wait_ge(rel_copied[w - 2], i * 4 + 3)
                    for b in range(RBANKS):
                        pe.matmul(big_ps[w % 2][:, b, 0:RPB * RW], turned[:, w, :],
                                  rel_flat[:, b * RPB * RW:(b + 1) * RPB * RW], start=True, stop=True)
                    pe.drain().then_inc(product_ready["rel"], 1)
            sum_windows("rel", 2 * F)
            net_flat = net_rhs[:, :, :].rearrange("i k o -> i (k o)")
            with pe.Fori(0, NGRP) as i:
                turn("net", i)
                for w in range(GROUP):
                    pe.matmul(big_ps[0][:, 0, w * NODEW:w * NODEW + NODEW], turned[:, w, :], net_flat,
                              start=(w == 0), stop=(w == GROUP - 1), skip_group_check=True)
                pe.drain().then_inc(product_ready["net"], 1)
            sum_windows("net", F)
            for k in range(2):
                pe.wait_ge(bn_ready, k + 1)
                pe.matmul(turn_ps[:, 0:F], ones_f[:, :], col_sum[:, :], start=True, stop=True)
                pe.drain().then_inc(bn_sum, 1)
            with pe.Fori(0, CHUNKS) as c:
                pe.wait_ge(equal_ready, c + 1)
                width = PARTS * F
                per = BANK // width
                for j in range(TILES):
                    b, a = j // per, j % per
                    pe.matmul(big_ps[0][:, b, a * width:(a + 1) * width], hot[:, j, 0:P],
                              parts_view(F)[:, j * width:(j + 1) * width],
                              start=(a == 0), stop=(a == per - 1 or j == TILES - 1), skip_group_check=True)
                pe.drain().then_inc(equal_done, 1)

        @block.vector
        def _(dve):
            dve.memset(xs[:, NWIN - 1:NW, :], 0.0)
            dve.drain().then_inc(setup, 1)
            dve.memset(acc[:, :, :], 0.0)
            dve.memset(deg[:, :, :], 0.0)
            dve.drain().then_inc(zeroed, 1)
            dve.wait_ge(in_dst, 16)
            dve.tensor_copy(dst_f[:, :], int_a)
            dve.drain().then_inc(setup, 1)
            dve.wait_ge(in_span, 16)
            dve.tensor_reduce(span[:, 0:1], span_in, AX.X, ALU.min)
            dve.tensor_reduce(span[:, 1:2], span_in, AX.X, ALU.max)
            dve.memset(meta[:, :], 0)
            dve.drain()
            shift = P.bit_length() - 1
            dve.tensor_scalar(span[:, 2:4], span[:, 0:2], shift, None, ALU.logical_shift_right)
            dve.drain()
            dve.tensor_copy(meta[:, 0:1], span[:, 2:3])
            dve.tensor_scalar(base_f[:, :], span[:, 2:3], float(P), None, ALU.mult)
            dve.tensor_tensor(span[:, 0:1], span[:, 3:4], span[:, 2:3], ALU.subtract)
            dve.drain()
            dve.tensor_scalar(span[:, 1:2], span[:, 0:1], float(WIN), None, ALU.add)
            dve.drain()
            dve.tensor_scalar(meta[:, 1:2], span[:, 1:2], WIN.bit_length() - 1, None, ALU.logical_shift_right)
            dve.drain()
            dve.tensor_copy(passes_f[:, :], meta[:, 1:2])
            dve.drain().then_inc(setup_pe, 1)
            dve.wait_ge(setup_pe, 2)
            dve.tensor_copy(meta[:, 2:3], turn_ps[0:CHUNKS, 0:1])
            dve.drain().then_inc(setup, 1)
            dve.wait_ge(in_srctype, 32)
            dve.scalar_tensor_tensor(out=int_b, in0=int_a, scalar=float(RELS), in1=int_b,
                                     op0=ALU.mult, op1=ALU.add)
            dve.drain().then_inc(setup, 1)
            dve.wait_ge(in_small, 16 * (13 + KE))
            dve.tensor_copy(wa_wide[:, :, :], wa[:, :].unsqueeze(2).broadcast_to([F, 3, P]))
            dve.drain().then_inc(setup_pe, 1)
            dve.wait_ge(setup_pe, 4)
            dve.tensor_copy(w_rel_sb[:, :], big_ps[0][0:RELS, 0, 0:F * F])
            dve.drain().then_inc(setup, 1)
            dve.tensor_copy(a_rows[:, :, :].rearrange("p t f -> p (t f)"), big_ps[0][:, 1, 0:3 * F])
            dve.tensor_copy(a_col[:, :], big_ps[0][0:F, 2, 0:1])
            dve.wait_ge(w_rel_in, 16)
            dve.drain()
            dve.tensor_copy(rel_rhs[:, :, F:RW], a_col[:, :].unsqueeze(2).broadcast_to([F, RELS, 1]))
            dve.wait_ge(consts, 1)
            dve.tensor_scalar(valid[:, :], valid[:, :], float(N), None, ALU.is_lt)
            dve.drain()

            def wide(v):
                return v.unsqueeze(2).broadcast_to([P, NW, F])

            def per_feature(v):
                return v.unsqueeze(1).broadcast_to([P, NW, F])

            def norm(k):
                dve.tensor_reduce(row_a[:, :], xs[:, :, :], AX.X, ALU.add)
                dve.drain()
                dve.tensor_scalar(row_a[:, :], row_a[:, :], 1.0 / F, None, ALU.mult)
                dve.drain()
                dve.tensor_tensor(h[:, :, :], xs[:, :, :], wide(row_a[:, :]), ALU.subtract)
                dve.drain()
                dve.tensor_tensor(tmp[:, :, :], h[:, :, :], h[:, :, :], ALU.mult)
                dve.drain()
                dve.tensor_reduce(row_a[:, :], tmp[:, :, :], AX.X, ALU.add)
                dve.drain()
                dve.tensor_scalar(row_a[:, :], row_a[:, :], 1.0 / F, EPS, ALU.mult, ALU.add)
                dve.drain().then_inc(var_ready, 1)
                dve.wait_ge(root_done, k)
                dve.reciprocal(row_a[:, :], row_b[:, :])
                dve.drain()
                dve.tensor_tensor(h[:, :, :], h[:, :, :], wide(row_a[:, :]), ALU.mult)
                dve.drain()
                dve.tensor_scalar(h[:, :, :], h[:, :, :], 0.0, None, ALU.max)
                dve.drain()

            def split(of, width):
                v = parts_view(width).rearrange("p (j s f) -> p j s f", j=TILES, s=PARTS)
                r = rest[:, :, 0:width]
                dve.tensor_copy(v[:, :, 0, :], of)
                dve.drain()
                dve.tensor_tensor(r, of, v[:, :, 0, :], ALU.subtract)
                dve.drain()
                dve.tensor_copy(v[:, :, 1, :], r)
                dve.drain()
                dve.tensor_tensor(v[:, :, 2, :], r, v[:, :, 1, :], ALU.subtract)
                dve.drain()

            def passes_of(name, c, width, to):
                low = dve.value_load(meta_row[0:1, bass.ds(c * 4, 1)], min_val=0, max_val=NWIN - 1)
                passes = dve.value_load(meta_row[0:1, bass.ds(c * 4 + 1, 1)], min_val=1, max_val=NWIN)
                first = dve.value_load(meta_row[0:1, bass.ds(c * 4 + 2, 1)], min_val=0, max_val=NWIN * CHUNKS)
                dve.tensor_tensor(dst_rel[:, :], dst_f[:, bass.ds(c * TILES, TILES)],
                                  base_all[:, bass.ds(c, 1)].broadcast_to([P, TILES]), ALU.subtract)
                dve.drain()
                with dve.Fori(0, passes) as k:
                    for j in range(TILES):
                        dve.tensor_scalar(hot[:, j, :], iota_span[:, :], dst_rel[:, j:j + 1], None, ALU.is_equal)
                    dve.drain().then_inc(hot_ready[name], 1)
                    dve.tensor_scalar(dst_rel[:, :], dst_rel[:, :], -float(SPAN), None, ALU.add)
                    dve.wait_ge(pass_done[name], first + k + 1)
                    place = nc.s_assert_within(low + k * WIN, 0, NW, skip_runtime_bounds_check_because=
                                               "a pass begins at a window that the chunk touches")
                    if name == "deg":
                        now = pass_ps[:, 0:WIN].unsqueeze(2)
                    else:
                        dve.tensor_reduce(part_sum[:, :, 0:width],
                                          pass_ps[:, 0:WIN * PARTS * width]
                                          .rearrange("p (w s f) -> p w f s", w=WIN, s=PARTS), AX.X, ALU.add)
                        dve.drain()
                        now = part_sum[:, :, 0:width]
                    at = to[:, bass.ds(place, WIN), 0:width]
                    dve.tensor_tensor(at, at, now, ALU.add)
                    dve.drain()

            def clear_sums(width):
                dve.memset(acc[:, :, 0:width], 0.0)
                dve.drain()

            def edges(name, width, message):
                for s in range(2):
                    dve.sem_inc(rows_free[name][s], 1)

                def body(c, s, use):
                    dve.wait_ge(gathered[name][s], use * LAND + LAND)
                    message(s, use)
                    dve.drain().then_inc(rows_free[name][s], 1)
                    passes_of(name, c, width, acc)
                chunks(dve, body)

            def plain(s, use):
                split(rows[s][:, :, 0:F], F)

            dve.wait_ge(in_x, 32)
            norm(1)
            dve.wait_ge(meta_in, 32)
            dve.wait_ge(relidx_out, 16)
            with dve.Fori(0, CHUNKS) as c:
                passes_of("deg", c, 1, deg)
            dve.tensor_scalar(row_a[:, :], deg[:, 0:NW, 0], 1.0, None, ALU.add)
            dve.drain().then_inc(var_ready, 1)
            dve.wait_ge(root_done, 2)
            dve.reciprocal(dinv[:, :], row_b[:, :])
            dve.drain()
            dve.tensor_tensor(g[:, :, :], h[:, :, :], wide(dinv[:, :]), ALU.mult)
            dve.drain().then_inc(table_ready, 1)
            dve.wait_ge(zeroed, 2 + 48 * COPIES)
            edges("conv1", F, plain)
            dve.tensor_tensor(g[:, :, :], g[:, :, :], acc[:, 0:NW, 0:F], ALU.add)
            dve.drain()
            dve.tensor_tensor(g[:, :, :], g[:, :, :], wide(dinv[:, :]), ALU.mult)
            dve.drain().then_inc(node_ready, 1)
            dve.wait_ge(node_done, 1)
            dve.tensor_tensor(g[:, :, :], tmp[:, :, :], wide(dinv[:, :]), ALU.mult)
            dve.drain().then_inc(table_ready, 1)
            clear_sums(F)
            edges("conv2", F, plain)
            dve.tensor_tensor(g[:, :, :], g[:, :, :], acc[:, 0:NW, 0:F], ALU.add)
            dve.drain()
            dve.tensor_tensor(g[:, :, :], g[:, :, :], wide(dinv[:, :]), ALU.mult)
            dve.drain()
            dve.tensor_tensor(xs[:, :, :], xs[:, :, :], g[:, :, :], ALU.add)
            dve.drain()
            dve.tensor_tensor(xs[:, :, :], xs[:, :, :], per_feature(b2[:, :]), ALU.add)
            dve.drain()

            norm(3)
            for s in range(2):
                dve.sem_inc(rel_copied[s], 1)
            dve.drain().then_inc(node_ready, 1)
            with dve.Fori(0, NGRP) as i:
                for w in range(GROUP):
                    s = w % 2
                    dve.wait_ge(product_ready["rel"], i * GROUP + w + 1)
                    dve.wait_ge(rel_stored[s], (i * 2 + w // 2) * 16 + 16)
                    for b in range(RBANKS - 1 - s, RBANKS):
                        dve.tensor_copy(rel_out[s][:, b * RPB * RW:(b + 1) * RPB * RW], big_ps[s][:, b, 0:RPB * RW])
                    dve.drain().then_inc(rel_copied[s], 1)
            clear_sums(2 * F)

            def relational(s, use):
                dve.wait_ge(attr_in["rel"][s], use * 16 + 16)
                dve.tensor_tensor(msg[:, :, 0:F], attr[s][:, :, :],
                                  a_rows[:, 1, :].unsqueeze(1).broadcast_to([P, TILES, F]), ALU.mult)
                dve.drain()
                dve.tensor_reduce(score[:, :], msg[:, :, 0:F], AX.X, ALU.add)
                dve.drain()
                dve.tensor_tensor(score[:, :], score[:, :], rows[s][:, :, F], ALU.add)
                dve.drain()
                dve.tensor_tensor(msg[:, :, 0:F], rows[s][:, :, 0:F],
                                  score[:, :].unsqueeze(2).broadcast_to([P, TILES, F]), ALU.mult)
                dve.tensor_copy(msg[:, :, F:2 * F], rows[s][:, :, 0:F])
                dve.drain()
                split(msg[:, :, :], 2 * F)
            edges("rel", 2 * F, relational)
            dve.tensor_tensor(tmp[:, :, :], h[:, :, :], per_feature(a_rows[:, 2, :]), ALU.mult)
            dve.drain()
            dve.tensor_reduce(row_a[:, :], tmp[:, :, :], AX.X, ALU.add)
            dve.drain()
            dve.tensor_tensor(tmp[:, :, :], acc[:, 0:NW, F:2 * F], wide(row_a[:, :]), ALU.mult)
            dve.drain()
            dve.tensor_tensor(tmp[:, :, :], tmp[:, :, :], acc[:, 0:NW, 0:F], ALU.add)
            dve.drain()
            dve.tensor_tensor(xs[:, :, :], xs[:, :, :], tmp[:, :, :], ALU.add)
            dve.drain()

            norm(4)
            dve.drain().then_inc(node_ready, 1)
            clear_sums(F)

            def network(s, use):
                dve.wait_ge(attr_in["net"][s], use * 16 + 16)
                for k in range(KE):
                    dve.tensor_tensor(work[:, :, k * F:k * F + F], rows[s][:, :, k * F:k * F + F],
                                      attr[s][:, :, k:k + 1].broadcast_to([P, TILES, F]), ALU.mult)
                dve.drain()
                dve.tensor_tensor(work[:, :, 0:2 * F], work[:, :, 0:2 * F], work[:, :, 2 * F:4 * F], ALU.add)
                dve.drain()
                dve.tensor_tensor(work[:, :, 0:F], work[:, :, 0:F], work[:, :, F:2 * F], ALU.add)
                dve.drain()
                dve.tensor_tensor(msg[:, :, 0:F], work[:, :, 0:F], rows[s][:, :, KE * F:NETW], ALU.add)
                dve.drain()
                split(msg[:, :, 0:F], F)
            edges("net", F, network)
            dve.tensor_scalar(row_a[:, :], deg[:, 0:NW, 0], 1.0, None, ALU.max)
            dve.drain()
            dve.reciprocal(row_a[:, :], row_a[:, :])
            dve.drain()
            dve.tensor_tensor(tmp[:, :, :], acc[:, 0:NW, 0:F], wide(row_a[:, :]), ALU.mult)
            dve.wait_ge(node_done, 2)
            dve.drain()
            dve.tensor_tensor(tmp[:, :, :], tmp[:, :, :], own[:, :, :], ALU.add)
            dve.drain()
            dve.tensor_tensor(tmp[:, :, :], tmp[:, :, :], per_feature(bias[:, :]), ALU.add)
            dve.drain()

            def over_nodes(k):
                dve.tensor_reduce(col_sum[:, :], g[:, :, :].rearrange("p w f -> p f w"), AX.X, ALU.add)
                dve.drain().then_inc(bn_ready, 1)
                dve.wait_ge(bn_sum, k)
            dve.tensor_tensor(g[:, :, :], tmp[:, :, :], wide(valid[:, :]), ALU.mult)
            dve.drain()
            over_nodes(1)
            dve.tensor_scalar(mean[:, :], turn_ps[:, 0:F], 1.0 / N, None, ALU.mult)
            dve.drain()
            dve.tensor_tensor(tmp[:, :, :], tmp[:, :, :], per_feature(mean[:, :]), ALU.subtract)
            dve.drain()
            dve.tensor_tensor(g[:, :, :], tmp[:, :, :], wide(valid[:, :]), ALU.mult)
            dve.drain()
            dve.tensor_tensor(g[:, :, :], g[:, :, :], g[:, :, :], ALU.mult)
            dve.drain()
            over_nodes(2)
            dve.tensor_scalar(col_sum[:, :], turn_ps[:, 0:F], 1.0 / N, EPS, ALU.mult, ALU.add)
            dve.drain().then_inc(bn_ready, 1)
            dve.wait_ge(root_done, 4 + 1)
            dve.reciprocal(scale[:, :], scale[:, :])
            dve.drain()
            dve.tensor_tensor(scale[:, :], scale[:, :], gamma[:, :], ALU.mult)
            dve.drain()
            dve.tensor_tensor(tmp[:, :, :], tmp[:, :, :], per_feature(scale[:, :]), ALU.mult)
            dve.drain()
            dve.tensor_tensor(tmp[:, :, :], tmp[:, :, :], per_feature(beta[:, :]), ALU.add)
            dve.drain()
            dve.tensor_scalar(g[:, :, :], tmp[:, :, :], SLOPE, None, ALU.mult)
            dve.drain()
            dve.tensor_tensor(tmp[:, :, :], tmp[:, :, :], g[:, :, :], ALU.max)
            dve.drain()
            dve.tensor_tensor(xs[:, :, :], xs[:, :, :], tmp[:, :, :], ALU.add)
            dve.drain()

            norm(6)
            dve.tensor_copy(g[:, :, :], h[:, :, :])
            dve.drain().then_inc(table_ready, 1)
            dve.tensor_scalar(tmp[:, :, :], h[:, :, :], -1.0 / FK, 1.0, ALU.mult, ALU.add)
            dve.tensor_scalar(own[:, :, :], h[:, :, :], 1.0 / FC, -1.0, ALU.mult, ALU.add)
            dve.drain()
            dve.tensor_tensor(tmp[:, :, :], tmp[:, :, :], h[:, :, :], ALU.mult)
            dve.drain()
            dve.tensor_tensor(own[:, :, :], tmp[:, :, :], own[:, :, :], ALU.mult)
            dve.drain()
            dve.tensor_scalar(own[:, :, :], own[:, :, :], FB, None, ALU.add)
            dve.drain()
            dve.tensor_tensor(xs[:, :, :], xs[:, :, :], own[:, :, :], ALU.add)
            dve.wait_ge(in_wt, 16)
            for s in range(2):
                dve.sem_inc(rows_free["rat"][s], 1)

            def rational(c, s, use, first=False):
                dve.wait_ge(gathered["rat"][s], use * (2 * LAND) + 2 * LAND)
                xi, xj = rows[s][:, :, 0:F], rows[s][:, :, F:2 * F]
                den, top = work[:, :, 0:F], work[:, :, F:2 * F]
                dve.tensor_scalar(den, xi, FE, FD, ALU.mult, ALU.add)
                dve.tensor_tensor(top, xi, xj, ALU.mult)
                dve.drain()
                dve.scalar_tensor_tensor(out=den, in0=xj, scalar=FH, in1=den, op0=ALU.mult, op1=ALU.add)
                dve.tensor_tensor(top, top, wt[:, bass.ds(c * TILES, TILES)].unsqueeze(2)
                                  .broadcast_to([P, TILES, F]), ALU.mult)
                dve.drain()
                dve.reciprocal(msg[:, :, 0:F], den)
                dve.drain()
                dve.tensor_tensor(msg[:, :, 0:F], msg[:, :, 0:F], top, ALU.mult)
                dve.drain()
                split(msg[:, :, 0:F], F)
                dve.wait_ge(src_row_in[s], use * 16 + 16)
                equal = hot[:, :, 0:P]
                dve.tensor_tensor(equal, src_row[s][:, :].rearrange("q (p j) -> q j p", j=TILES),
                                  index[s][:, :].unsqueeze(2).broadcast_to([P, TILES, P]), ALU.is_equal)
                dve.drain().then_inc(equal_ready, 1)
                dve.tensor_tensor(hot[:, :, P:2 * P], equal,
                                  earlier[:, :].unsqueeze(1).broadcast_to([P, TILES, P]), ALU.mult)
                dve.drain()
                dve.tensor_reduce(seen[:, :], hot[:, :, P:2 * P], AX.X, ALU.add)
                dve.drain()
                dve.tensor_scalar(seen[:, :], seen[:, :], 0.5, None, ALU.is_gt)
                dve.tensor_scalar(score[:, :], index[s][:, :], -1.0, spare[:, 0:1], ALU.mult, ALU.add)
                dve.drain()
                dve.tensor_tensor(score[:, :], score[:, :], seen[:, :], ALU.mult)
                dve.drain()
                if not first:
                    for k in range(COPIES):
                        dve.wait_ge(scattered[k], (c - 1) * (16 * TILES // COPIES))
                dve.tensor_tensor(scat_index[s][:, :], score[:, :], index[s][:, :], ALU.add)
                dve.drain().then_inc(rows_free["rat"][s], 1)
                dve.wait_ge(equal_done, c + 1)
                width = PARTS * F
                per = BANK // width
                for b in range((TILES + per - 1) // per):
                    n = min(per, TILES - b * per)
                    dve.tensor_reduce(scat[s][:, b * per:b * per + n, :],
                                      big_ps[0][:, b, 0:n * width].rearrange("p (a q f) -> p a f q", a=n, q=PARTS),
                                      AX.X, ALU.add)
                dve.drain().then_inc(scat_ready[s], 1)
            rational(0, 0, 0, first=True)
            rational(1, 1, 0, first=True)
            with dve.Fori(1, PAIRS) as i:
                rational(i * 2, 0, i)
                rational(i * 2 + 1, 1, i)
            rational(CHUNKS - 1, 0, PAIRS)
            dve.drain().then_inc(sums_ready, 1)
            dve.wait_ge(sums_in, 32 * COPIES)
            for v in (acc[:, 0:NW, 0:F], acc[:, 0:NW, F:2 * F], tmp[:, :, :], h[:, :, :], g[:, :, :]):
                dve.tensor_tensor(xs[:, 0:NWIN, :], xs[:, 0:NWIN, :], v[:, 0:NWIN, :], ALU.add)
                dve.drain()
            dve.drain().then_inc(out_ready, 1)


_INS = ['x', 'src', 'dst', 'edge_attr_16', 'edge_attr_4', 'edge_type_90', 'edge_weight', 'L0_gnn_W1', 'L0_gnn_b1',
        'L0_gnn_W2', 'L0_gnn_b2', 'L1_gnn_Ws', 'L1_gnn_Wa', 'L1_gnn_weight', 'L1_gnn_w_comp', 'L2_gnn_enet_w',
        'L2_gnn_enet_b', 'L2_gnn_root', 'L2_gnn_bias', 'L2_gnn_gamma', 'L2_gnn_beta']


def kernel(**inputs):
    import numpy as np
    import concourse.bacc as bacc
    from concourse.bass_utils import run_bass_kernel_spmd

    nc = bacc.Bacc("TRN2", target_bir_lowering=False, num_devices=1)
    arrays, args = {}, []
    for name in _INS:
        a = np.ascontiguousarray(inputs[name])
        arrays[f"in_{name}"] = a
        args.append(nc.dram_tensor(f"in_{name}", a.shape, mybir.dt.from_np(a.dtype), kind="ExternalInput").ap())
    result = nc.dram_tensor("out_x", inputs["x"].shape, F32, kind="ExternalOutput").ap()
    build_program(nc, *args, result)
    r = run_bass_kernel_spmd(nc, [arrays], core_ids=[0])
    return r.results[0]["out_x"]
```

```python
from contextlib import ExitStack

import concourse.bass as bass
from concourse import mybir

ALU = mybir.AluOpType
ACT = mybir.ActivationFunctionType
AX = mybir.AxisListType
F32 = mybir.dt.float32
F16 = mybir.dt.float16
BF16 = mybir.dt.bfloat16
I32 = mybir.dt.int32

P = 128
F = 16
TILES = 25
WIN = 4
POOL_TILES = 8
PAIR_ORDER = (0, 0, 1, 0, 2, 1, 1, 2)
MATE_ORDER = (0, 1, 0, 2, 0, 1, 2, 1)
GROUP = 4
COPIES = 5
PARTS = 3
BANK = 512
EPS = 1e-5
SLOPE = 0.01
FB, FK, FC, FD, FE, FH = 0.1, 5.0, 1.0, 5.0, 0.9, 0.1


def build_program(nc, x, src, dst, edge_attr_16, edge_attr_4, edge_type_90, edge_weight, gcn_w1, gcn_b1, gcn_w2,
                  gcn_b2, rel_ws, rel_wa, rel_weight, rel_comp, net_w, net_b, net_root, net_bias, net_gamma,
                  net_beta, out):
    N = x.shape[0]
    E = src.shape[0]
    CE = P * TILES
    CHUNKS = E // CE
    NWIN = (N + P - 1) // P
    NGRP = (NWIN + GROUP - 1) // GROUP
    NW = NGRP * GROUP
    NROW = NW * P
    AW = NW + WIN
    LAST = N - (NWIN - 1) * P
    HID = gcn_w1.shape[1]
    BASES = rel_weight.shape[0]
    RELS = rel_comp.shape[0]
    KE = edge_attr_4.shape[1]
    RW = F + 1
    RPB = BANK // RW
    RBANKS = RELS // RPB
    NETW = (KE + 1) * F
    NODEW = NETW + F
    assert E == CE * CHUNKS and CHUNKS % 2 == 1 and RELS == RPB * RBANKS and TILES % COPIES == 0
    PAIRS = CHUNKS // 2
    SPAN = WIN * P
    LAND = 16 * TILES

    tab1 = nc.dram_tensor("tab1", [NROW, F], F32).ap()
    tab2 = nc.dram_tensor("tab2", [NROW, F], F32).ap()
    tab_rel = nc.dram_tensor("tab_rel", [NROW * RELS, RW], F32).ap()
    tab_net = nc.dram_tensor("tab_net", [NROW, NETW], F32).ap()
    tab3 = nc.dram_tensor("tab3", [NROW, F], F32).ap()
    rel_index = nc.dram_tensor("rel_index", [E], I32).ap()
    w_rel_flat = nc.dram_tensor("w_rel_flat", [RELS * F * F], F32).ap()
    meta_dram = nc.dram_tensor("meta_dram", [CHUNKS, 4], I32).ap()
    base_dram = nc.dram_tensor("base_dram", [CHUNKS], F32).ap()
    sums = [nc.dram_tensor(f"sums{k}", [N + P, F], F32).ap() for k in range(COPIES)]

    def by_window(t):
        return t.rearrange("(w r) f -> r w f", r=P)

    def by_chunk(t):
        return t.rearrange("(c p j) -> c p j", p=P, j=TILES)

    def resident(t):
        return t.rearrange("(c p j) -> p c j", p=P, j=TILES)

    ctx = ExitStack()
    with ctx:
        def sb(name, shape, dt=F32):
            return ctx.enter_context(nc.sbuf_tensor(name, shape, dt))

        def sem(name):
            return ctx.enter_context(nc.semaphore(name))

        ctx.enter_context(nc.allow_non_contiguous_dma("rows of 64 bytes, small weights"))

        xs = sb("xs", [P, NW, F])
        h = sb("h", [P, NW, F])
        g = sb("g", [P, NW, F])
        tmp = sb("tmp", [P, NW, F])
        own = sb("own", [P, NW, F])
        acc = sb("acc", [P, AW, 2 * F])
        deg = sb("deg", [P, NW])
        dinv = sb("dinv", [P, NW])
        row_a = sb("row_a", [P, NW])
        row_b = sb("row_b", [P, NW])
        valid = sb("valid", [P, NW])
        dst_f = sb("dst_f", [P, CHUNKS * TILES])
        weight = [sb(f"weight{s}", [P, TILES]) for s in range(2)]
        dst_row = sb("dst_row", [P, CE], I32)
        span = sb("span", [CHUNKS, 4], I32)
        meta = sb("meta", [CHUNKS, 4], I32)
        passes_f = sb("passes_f", [CHUNKS, 1])
        base_f = sb("base_f", [CHUNKS, 1])
        meta_row = sb("meta_row", [1, CHUNKS * 4], I32)
        base_all = sb("base_all", [P, CHUNKS])
        before = sb("before", [P, P])
        earlier = sb("earlier", [P, P], BF16)
        identity_b = sb("identity_b", [P, P], BF16)
        identity = sb("identity", [P, P])
        ones_f = sb("ones_f", [P, P])
        ones_b = sb("ones_b", [P, 1], BF16)
        iota_span = sb("iota_span", [P, SPAN], F16)
        spare = sb("spare", [P, 1])
        hot = sb("hot", [P, TILES, SPAN], BF16)
        ints = hot[:, :, :].rearrange("p j n -> p (j n)").bitcast(I32)
        int_a = ints[:, 0:CHUNKS * TILES]
        int_b = ints[:, CHUNKS * TILES:2 * CHUNKS * TILES]
        parts = sb("parts", [P, TILES, PARTS, 2 * F], BF16)
        dst_rel = sb("dst_rel", [P, TILES])
        index = [sb(f"index{s}", [P, TILES], I32) for s in range(2)]
        xj = sb("xj", [P, TILES, F])
        node_of = sb("node_of", [P, WIN])
        node_ids = sb("node_ids", [P, WIN])
        rows = [sb(f"rows{s}", [P, TILES, NETW]) for s in range(2)]
        attr = [sb(f"attr{s}", [P, TILES, F]) for s in range(2)]
        msg = sb("msg", [P, TILES, 2 * F])
        work = sb("work", [P, TILES, KE * F])
        rest = sb("rest", [P, TILES, 2 * F])
        score = sb("score", [P, TILES])
        hot_flat = hot[:, :, :].rearrange("p j n -> p (j n)")
        h_stack = hot_flat.rearrange("p (w q f) -> p w q f", w=NW, q=P // F)
        hot_t = hot_flat.rearrange("p (w e) -> p w e", w=WIN)
        mat_parts = dst_row[0:F, :].bitcast(BF16)[:, 0:PARTS * RELS * RW].rearrange("i (q n) -> i q n", q=PARTS)
        LOW = PAIR_ORDER.index(2) * F
        h_parts = acc[:, :, :].rearrange("p w f -> p (w f)").bitcast(BF16).rearrange("p (w f) -> p w f", w=AW)
        equal = own[:, :, :].rearrange("p w f -> p (w f)").bitcast(BF16)[:, 0:CE].rearrange("p (j q) -> p j q", q=P)
        part_sum = sb("part_sum", [P, WIN, 2 * F])
        src_row = [sb(f"src_row{s}", [P, CE], I32) for s in range(2)]
        dst_window = src_row[0][:, 0:CHUNKS * TILES].bitcast(F32)
        dst_place = src_row[1][:, 0:CHUNKS * TILES].bitcast(F32)
        span_in = src_row[0][0:CHUNKS, :]
        seen = sb("seen", [P, TILES])
        scat = [sb(f"scat{s}", [P, TILES, F]) for s in range(2)]
        scat_index = [sb(f"scat_index{s}", [P, TILES], I32) for s in range(2)]
        stage = sb("stage", [P, GROUP, F])
        turned = sb("turned", [F, GROUP, P])
        turned_b = [sb(f"turned_b{k}", [P, P], BF16) for k in range(2)]
        hid = sb("hid", [HID, GROUP * P])
        rel_out = [r[:, 0:RELS * RW].bitcast(F32) for r in src_row]
        net_out = sb("net_out", [P, GROUP, NETW])
        w1 = sb("w1", [F, HID])
        w2 = sb("w2", [HID, F])
        b1 = sb("b1", [HID, 1])
        b2 = sb("b2", [P, F])
        ws = sb("ws", [F, F])
        wa = sb("wa", [F, 3])
        wa_wide = sb("wa_wide", [F, 3, P])
        a_rows = sb("a_rows", [P, 3, F])
        a_col = sb("a_col", [F, 1])
        comp = sb("comp", [BASES, RELS])
        bases = sb("bases", [BASES, F, F])
        w_rel_sb = sb("w_rel_sb", [RELS, F * F])
        rel_rhs = sb("rel_rhs", [F, RELS, RW])
        rel_stack = sb("rel_stack", [P, RELS * RW], BF16)
        rel_low = sb("rel_low", [P, RELS * RW], BF16)
        net_rhs = sb("net_rhs", [F, NODEW // F, F])
        bias = sb("bias", [P, F])
        gamma = sb("gamma", [P, F])
        beta = sb("beta", [P, F])
        col_sum = sb("col_sum", [P, F])
        mean = sb("mean", [P, F])
        scale = sb("scale", [P, F])

        pass_ps = ctx.enter_context(nc.psum_tensor("pass_ps", [P, BANK], F32))
        turn_ps = ctx.enter_context(nc.psum_tensor("turn_ps", [P, BANK], F32))
        big_ps = [ctx.enter_context(nc.psum_tensor(f"big_ps{k}", [P, RBANKS, BANK], F32)) for k in range(2)]

        stack_ps = [t[:, 0:P // 2].bitcast(BF16) for t in (turn_ps, pass_ps)]

        pool_turns = sem("pool_turns")
        consts = sem("consts")
        in_x = sem("in_x")
        in_small = sem("in_small")
        in_span = sem("in_span")
        in_dst = sem("in_dst")
        in_srctype = sem("in_srctype")
        split_dst = sem("split_dst")
        window_copied = [sem(f"window_copied{k}") for k in range(2)]
        window_ready = [sem(f"window_ready{k}") for k in range(2)]
        place_ready = [sem(f"place_ready{k}") for k in range(2)]
        degree_done = [sem(f"degree_done{k}") for k in range(2)]
        weight_in = [sem(f"weight_in{k}") for k in range(2)]
        dst_row_in = sem("dst_row_in")
        dst_row_free = sem("dst_row_free")
        setup = sem("setup")
        setup_pe = sem("setup_pe")
        meta_out = sem("meta_out")
        meta_in = sem("meta_in")
        relidx_out = sem("relidx_out")
        w_rel_out = sem("w_rel_out")
        w_rel_in = sem("w_rel_in")
        zeroed = sem("zeroed")
        var_ready = sem("var_ready")
        root_done = sem("root_done")
        table_ready = sem("table_ready")
        table_out = [sem(f"table_out{k}") for k in range(5)]
        hot_ready = {s: sem(f"hot_ready_{s}") for s in ("conv1", "conv2", "rel", "net", "rat")}
        pass_done = {s: sem(f"pass_done_{s}") for s in hot_ready}
        gathering = ("conv1", "conv2", "rel", "net", "rat")
        index_in = {s: [sem(f"index_in_{s}{k}") for k in range(2)] for s in gathering}
        gathered = {s: [sem(f"gathered_{s}{k}") for k in range(2)] for s in gathering}
        rows_free = {s: [sem(f"rows_free_{s}{k}") for k in range(2)] for s in gathering}
        attr_in = {s: [sem(f"attr_in_{s}{k}") for k in range(2)] for s in ("rel", "net")}
        src_row_in = [sem(f"src_row_in{k}") for k in range(2)]
        equal_ready = sem("equal_ready")
        equal_done = sem("equal_done")
        scat_ready = [sem(f"scat_ready{k}") for k in range(2)]
        scattered = [sem(f"scattered{k}") for k in range(COPIES)]
        staged = {s: sem(f"staged_{s}") for s in ("hidden", "net")}
        stack_ps_ready = [sem(f"stack_ps_ready{k}") for k in range(2)]
        stack_ready = [sem(f"stack_ready{k}") for k in range(2)]
        rel_ready = [sem(f"rel_ready{k}") for k in range(2)]
        rel_split = sem("rel_split")
        rel_stacked = sem("rel_stacked")
        turned_ps_ready = {s: sem(f"turned_ps_ready_{s}") for s in staged}
        turned_ready = {s: sem(f"turned_ready_{s}") for s in staged}
        product_ready = {s: sem(f"product_ready_{s}") for s in staged}
        hid_ready = sem("hid_ready")
        hid_ps_ready = sem("hid_ps_ready")
        node_ready = sem("node_ready")
        rel_copied = [sem(f"rel_copied{k}") for k in range(2)]
        rel_stored = [sem(f"rel_stored{k}") for k in range(2)]
        net_copied = sem("net_copied")
        net_stored = sem("net_stored")
        node_done = sem("node_done")
        bn_ready = sem("bn_ready")
        bn_sum = sem("bn_sum")
        sums_ready = sem("sums_ready")
        sums_in = sem("sums_in")
        out_ready = sem("out_ready")
        stored = sem("stored")

        def chunks(eng, body):
            with eng.Fori(0, PAIRS) as i:
                body(i * 2, 0, i)
                body(i * 2 + 1, 1, i)
            body(CHUNKS - 1, 0, PAIRS)

        def chunks_after_first(eng, body):
            body(0, 0, 0, first=True)
            body(1, 1, 0, first=True)
            with eng.Fori(1, PAIRS) as i:
                body(i * 2, 0, i)
                body(i * 2 + 1, 1, i)
            body(CHUNKS - 1, 0, PAIRS)

        half = TILES * (P + NWIN)

        def hot_place(s):
            return hot_flat[:, s * half:s * half + TILES * P].rearrange("p (j n) -> p j n", n=P)

        def hot_window(s):
            return hot_flat[:, s * half + TILES * P:(s + 1) * half].rearrange("p (j n) -> p j n", n=NWIN)

        def parts_view(width):
            return parts[:, :, :, :].rearrange("p j s f -> p (j s f)")[:, 0:TILES * PARTS * width]

        block = ctx.enter_context(nc.Block())

        @block.sync
        def _(sp):
            sp.dma_start(span_in, dst.rearrange("(c e) -> c e", e=CE)).then_inc(in_span, 16)
            sp.dma_start(int_a.rearrange("p (c j) -> p c j", j=TILES), resident(dst)).then_inc(in_dst, 16)
            sp.wait_ge(setup, 1)
            sp.dma_start(xs[:, 0:NWIN - 1, :], by_window(x[0:(NWIN - 1) * P, :])).then_inc(in_x, 16)
            sp.dma_start(xs[0:LAST, NWIN - 1, :], x[(NWIN - 1) * P:N, :]).then_inc(in_x, 16)
            for to, of in (
                (w1[:, :], gcn_w1), (w2[:, :], gcn_w2), (b1[:, :], gcn_b1.rearrange("(k a) -> k a", a=1)),
                (b2[:, :], gcn_b2.rearrange("(a f) -> a f", a=1).broadcast_to([P, F])),
                (ws[:, :], rel_ws), (wa[:, :], rel_wa.rearrange("a (t k) -> k (a t)", k=F)),
                (comp[:, :], rel_comp.rearrange("r b -> b r")),
                (bases[:, :, :], rel_weight.rearrange("b i o -> (b i o)").rearrange("(i b o) -> b i o", b=BASES, o=F)),
                (net_rhs[:, KE, :], net_b.rearrange("(i o) -> i o", o=F)), (net_rhs[:, KE + 1, :], net_root),
                (bias[:, :], net_bias.rearrange("(a f) -> a f", a=1).broadcast_to([P, F])),
                (gamma[:, :], net_gamma.rearrange("(a f) -> a f", a=1).broadcast_to([P, F])),
                (beta[:, :], net_beta.rearrange("(a f) -> a f", a=1).broadcast_to([P, F])),
            ):
                sp.dma_start(to, of).then_inc(in_small, 16)
            for k in range(KE):
                sp.dma_start(net_rhs[:, k, :], net_w[:, k].rearrange("(i o) -> i o", o=F)).then_inc(in_small, 16)
            sp.wait_ge(setup, 2)
            sp.dma_start(int_a.rearrange("p (c j) -> p c j", j=TILES), resident(src)).then_inc(in_srctype, 16)
            sp.dma_start(int_b.rearrange("p (c j) -> p c j", j=TILES),
                         resident(edge_type_90)).then_inc(in_srctype, 16)
            sp.wait_ge(setup, 3)
            sp.dma_start(meta_dram, meta[:, :]).then_inc(meta_out, 16)
            sp.dma_start(base_dram.rearrange("(c a) -> c a", a=1), base_f[:, :]).then_inc(meta_out, 16)
            sp.wait_ge(meta_out, 32)
            sp.dma_start(meta_row[:, :], meta_dram.rearrange("c k -> (c k)").rearrange("(a n) -> a n", a=1))\
                .then_inc(meta_in, 16)
            sp.dma_start(base_all[:, :], base_dram.rearrange("(a c) -> a c", a=1).broadcast_to([P, CHUNKS]))\
                .then_inc(meta_in, 16)
            sp.wait_ge(setup, 4)
            sp.dma_start(resident(rel_index), int_b.rearrange("p (c j) -> p c j", j=TILES))\
                .then_inc(relidx_out, 16)
            sp.wait_ge(setup, 5)
            sp.dma_start(w_rel_flat.rearrange("(i r o) -> r i o", r=RELS, o=F),
                         w_rel_sb[:, :].rearrange("r (i o) -> r i o", o=F)).then_inc(w_rel_out, 16)
            sp.wait_ge(w_rel_out, 16)
            sp.dma_start(rel_rhs[:, :, 0:F], w_rel_flat.rearrange("(r i o) -> i r o", i=F, o=F)).then_inc(w_rel_in, 16)
            sp.wait_ge(rel_split, 1)
            flat_parts = mat_parts.rearrange("i q n -> i (q n)")
            for q, part in enumerate(MATE_ORDER):
                sp.dma_start(rel_stack[q * F:q * F + F, :], flat_parts[:, part * RELS * RW:(part + 1) * RELS * RW])\
                    .then_inc(rel_stacked, 16)
            sp.dma_start(rel_low[LOW:LOW + F, :], flat_parts[:, 2 * RELS * RW:3 * RELS * RW]).then_inc(rel_stacked, 16)
            sp.wait_ge(zeroed, 1)
            for k in range(COPIES):
                sp.dma_start(by_window(sums[k][0:(NWIN - 1) * P, :]), acc[:, 0:NWIN - 1, 0:F]).then_inc(zeroed, 16)
                sp.dma_start(sums[k][(NWIN - 1) * P:N, :], acc[0:LAST, NWIN - 1, 0:F]).then_inc(zeroed, 16)
                sp.dma_start(sums[k][N:N + P, :], acc[:, 0, 0:F]).then_inc(zeroed, 16)
            sp.wait_ge(zeroed, 1 + 48 * COPIES)
            sp.sem_inc(zeroed, 1)

            def table(k, to):
                sp.wait_ge(table_ready, k + 1)
                sp.dma_start(by_window(to), g[:, :, :]).then_inc(table_out[k], 16)

            def feed(name, index_of, attr_of=None, width=F):
                def body(c, s, use):
                    sp.wait_ge(rows_free[name][s], use + 1)
                    sp.dma_start(index[s][:, :], by_chunk(index_of)[bass.ds(c, 1), :, :]
                                 .rearrange("a p j -> (a p) j")).then_inc(index_in[name][s], 16)
                    if attr_of is not None:
                        sp.dma_start(attr[s][:, :, 0:width], attr_of.rearrange("(c p j) k -> c p j k", p=P, j=TILES)
                                     [bass.ds(c, 1), :, :, :].rearrange("a p j k -> (a p) j k"))\
                            .then_inc(attr_in[name][s], 16)
                chunks(sp, body)

            table(0, tab1)
            feed("conv1", src)
            table(1, tab2)
            feed("conv2", src)

            with sp.Fori(0, NW // 2) as i:
                for s in range(2):
                    sp.wait_ge(rel_copied[s], i * 2 + 3)
                    sp.dma_start(tab_rel.rearrange("(n r) f -> n (r f)", r=RELS)[bass.ds((i * 2 + s) * P, P), :],
                                 rel_out[s]).then_inc(rel_stored[s], 16)
            for s in range(2):
                sp.wait_ge(rel_stored[s], 16 * NW // 2 + 16)
            sp.wait_ge(relidx_out, 16)
            sp.sem_inc(table_out[2], 16)
            feed("rel", rel_index, edge_attr_16)

            with sp.Fori(0, NGRP) as i:
                sp.wait_ge(net_copied, i + 1)
                sp.dma_start(by_window(tab_net)[:, bass.ds(i * GROUP, GROUP), :], net_out[:, :, :])\
                    .then_inc(net_stored, 16)
            sp.wait_ge(net_stored, 16 * NGRP + 16)
            sp.sem_inc(table_out[3], 16)
            feed("net", src, edge_attr_4, KE)

            sp.wait_ge(table_ready, 3)
            sp.dma_start(by_window(tab3), g[:, :, :]).then_inc(table_out[4], 16)

            def feed_rational(c, s, use):
                sp.wait_ge(rows_free["rat"][s], use + 1)
                sp.dma_start(index[s][:, :], by_chunk(src)[bass.ds(c, 1), :, :]
                             .rearrange("a p j -> (a p) j")).then_inc(index_in["rat"][s], 16)
                sp.dma_start(weight[s][:, :], by_chunk(edge_weight)[bass.ds(c, 1), :, :]
                             .rearrange("a p j -> (a p) j")).then_inc(weight_in[s], 16)
                sp.dma_start(src_row[s][:, :], src.rearrange("(c e) -> c e", e=CE)[bass.ds(c, 1), :]
                             .broadcast_to([P, CE])).then_inc(src_row_in[s], 16)
                sp.wait_ge(dst_row_free, c + 1)
                sp.dma_start(dst_row[:, :], dst.rearrange("(c e) -> c e", e=CE)[bass.ds(c, 1), :]
                             .broadcast_to([P, CE])).then_inc(dst_row_in, 16)
            chunks(sp, feed_rational)

            sp.wait_ge(sums_ready, 1)
            for k in range(COPIES):
                sp.wait_ge(scattered[k], 16 * CHUNKS * TILES // COPIES)
            loads = (acc[:, 0:NW, 0:F], acc[:, 0:NW, F:2 * F], tmp[:, :, :], h[:, :, :], g[:, :, :])
            for k in range(COPIES):
                sp.dma_start(loads[k][:, 0:NWIN - 1, :], by_window(sums[k][0:(NWIN - 1) * P, :])).then_inc(sums_in, 16)
                sp.dma_start(loads[k][0:LAST, NWIN - 1, :], sums[k][(NWIN - 1) * P:N, :]).then_inc(sums_in, 16)
            sp.wait_ge(out_ready, 1)
            sp.dma_start(by_window(out[0:(NWIN - 1) * P, :]), xs[:, 0:NWIN - 1, :]).then_inc(stored, 16)
            sp.dma_start(out[(NWIN - 1) * P:N, :], xs[0:LAST, NWIN - 1, :]).then_inc(stored, 16)
            sp.wait_ge(stored, 32)

        @block.gpsimd
        def _(pool):
            pool.memset(before[:, :], 1.0)
            pool.memset(earlier[:, :], 1.0)
            pool.memset(identity[:, :], 0.0)
            pool.memset(ones_f[:, :], 1.0)
            pool.memset(ones_b[:, :], 1.0)
            pool.iota(iota_span[:, :], pattern=[[1, SPAN]], base=0, channel_multiplier=0,
                      allow_small_or_imprecise_dtypes=True)
            pool.iota(spare[:, :], pattern=[[0, 1]], base=N, channel_multiplier=1,
                      allow_small_or_imprecise_dtypes=True)
            pool.iota(node_ids[:, :], pattern=[[P, WIN]], base=0, channel_multiplier=1,
                      allow_small_or_imprecise_dtypes=True)
            pool.iota(valid[:, :], pattern=[[P, NW]], base=0, channel_multiplier=1,
                      allow_small_or_imprecise_dtypes=True)
            pool.drain()
            pool.affine_select(out=before[:, :], in_=before[:, :], compare_op=ALU.is_gt, fill=0.0, base=0,
                               pattern=[[1, P]], channel_multiplier=-1)
            pool.affine_select(out=earlier[:, :], in_=earlier[:, :], compare_op=ALU.is_gt, fill=0.0, base=0,
                               pattern=[[-1, P]], channel_multiplier=1)
            pool.affine_select(out=identity[:, :], in_=identity[:, :], compare_op=ALU.not_equal, fill=1.0, base=0,
                               pattern=[[-1, P]], channel_multiplier=1)
            pool.memset(identity_b[:, :], 0.0)
            pool.drain()
            pool.affine_select(out=identity_b[:, :], in_=identity_b[:, :], compare_op=ALU.not_equal, fill=1.0, base=0,
                               pattern=[[-1, P]], channel_multiplier=1)
            pool.drain().then_inc(consts, 1)

            def alone():
                pool.sem_inc(pool_turns, 1)

            def gather(name, table, width, number):
                pool.wait_ge(table_out[number], 16)

                def body(c, s, use):
                    pool.wait_ge(index_in[name][s], use * 16 + 16)
                    pool.wait_ge(rows_free[name][s], use + 1)
                    alone()
                    for j in range(TILES):
                        pool.indirect_dma_start(
                            out=rows[s][:, j, 0:width], out_offset=None, in_=table,
                            in_offset=bass.IndirectOffsetOnAxis(ap=index[s][:, j:j + 1], axis=0),
                        ).then_inc(gathered[name][s], 16)
                chunks(pool, body)

            pool.wait_ge(relidx_out, 16)
            pool.wait_ge(split_dst, 1)

            def windows(c, s, use, first=False):
                if not first:
                    pool.wait_ge(degree_done[s], use)
                pool.wait_ge(window_copied[s], use + 1)
                alone()
                for j in range(TILES - POOL_TILES, TILES):
                    pool.tensor_scalar(hot_window(s)[:, j, :], iota_span[:, 0:NWIN],
                                       weight[s][:, j:j + 1], None, ALU.is_equal)
                pool.drain().then_inc(window_ready[s], 1)
            chunks_after_first(pool, windows)

            gather("conv1", tab1, F, 0)
            gather("conv2", tab2, F, 1)
            gather("rel", tab_rel, RW, 2)
            gather("net", tab_net, NETW, 3)

            pool.wait_ge(table_out[4], 16)
            pool.wait_ge(zeroed, 2 + 48 * COPIES)

            def gather_sources(s, use):
                pool.wait_ge(index_in["rat"][s], use * 16 + 16)
                pool.wait_ge(rows_free["rat"][s], use + 1)
                alone()
                for j in range(TILES):
                    pool.indirect_dma_start(
                        out=rows[s][:, j, 0:F], out_offset=None, in_=tab3,
                        in_offset=bass.IndirectOffsetOnAxis(ap=index[s][:, j:j + 1], axis=0),
                    ).then_inc(gathered["rat"][s], 16)

            def scatter(c, s, use, first=False):
                pool.wait_ge(scat_ready[s], use + 1)
                for j in range(TILES):
                    k = j % COPIES
                    if not (first and j < COPIES):
                        pool.wait_ge(scattered[k], c * (16 * TILES // COPIES) + 16 * (j // COPIES))
                    alone()
                    pool.indirect_dma_start(
                        out=sums[k], out_offset=bass.IndirectOffsetOnAxis(ap=scat_index[s][:, j:j + 1], axis=0),
                        in_=scat[s][:, j, :], in_offset=None, compute_op=ALU.add,
                        bounds_check=N + P - 1,
                    ).then_inc(scattered[k], 16)

            gather_sources(0, 0)
            gather_sources(1, 0)
            scatter(0, 0, 0, first=True)
            gather_sources(0, 1)
            scatter(1, 1, 0)
            with pool.Fori(1, PAIRS) as i:
                gather_sources(1, i)
                scatter(i * 2, 0, i)
                gather_sources(0, i + 1)
                scatter(i * 2 + 1, 1, i)
            scatter(CHUNKS - 1, 0, PAIRS)

        @block.scalar
        def _(act):
            def root(k):
                act.wait_ge(var_ready, k)
                act.activation(row_b[:, :], row_a[:, :], ACT.Sqrt)
                act.drain().then_inc(root_done, 1)

            def turn(name, i):
                of = g if name == "hidden" else h
                act.activation(stage[:, :, :], of[:, bass.ds(i * GROUP, GROUP), :], ACT.Copy)
                act.drain().then_inc(staged[name], 1)
                act.wait_ge(turned_ps_ready[name], i + 1)
                act.activation(turned[:, :, :].rearrange("k w r -> k (w r)"), turn_ps[0:F, :], ACT.Copy)
                act.drain().then_inc(turned_ready[name], 1)

            root(1)
            act.wait_ge(split_dst, 1)

            def windows(c, s, use, first=False):
                if not first:
                    act.wait_ge(window_ready[s], use)
                act.activation(weight[s][:, :], dst_window[:, bass.ds(c * TILES, TILES)], ACT.Copy)
                act.drain().then_inc(window_copied[s], 1)
            chunks_after_first(act, windows)
            root(2)
            act.wait_ge(node_ready, 1)
            act.wait_ge(in_small, 16 * (13 + KE))
            with act.Fori(0, NGRP) as i:
                turn("hidden", i)
                act.wait_ge(hid_ps_ready, i + 1)
                act.activation(hid[:, :], big_ps[0][0:HID, 0, :], ACT.Relu, bias=b1[:, 0:1])
                act.drain().then_inc(hid_ready, 1)
                act.wait_ge(product_ready["hidden"], i + 1)
                act.activation(tmp[:, bass.ds(i * GROUP, GROUP), :],
                               big_ps[1][:, 0, 0:GROUP * F].rearrange("p (w f) -> p w f", f=F), ACT.Copy)
                act.drain()
            act.drain().then_inc(node_done, 1)
            root(3)
            act.wait_ge(node_ready, 2)
            for s in range(2):
                act.sem_inc(rel_stored[s], 16)

            def take_turned(s, i):
                act.wait_ge(stack_ps_ready[s], i + 1)
                act.activation(turned_b[s][:, :], stack_ps[s], ACT.Copy)
                act.drain().then_inc(stack_ready[s], 1)
            take_turned(0, 0)
            take_turned(1, 0)

            def empty(i, more=True):
                for s in range(2):
                    act.wait_ge(rel_ready[s], i + 1)
                    act.wait_ge(rel_stored[s], i * 16 + 16)
                    for b in range(RBANKS - 1 - s):
                        act.activation(rel_out[s][:, b * RPB * RW:(b + 1) * RPB * RW], big_ps[s][:, b, 0:RPB * RW],
                                       ACT.Copy)
                    act.drain().then_inc(rel_copied[s], 1)
                    if more:
                        take_turned(s, i + 1)
            with act.Fori(0, NW // 2 - 1) as i:
                empty(i)
            empty(NW // 2 - 1, more=False)
            root(4)
            act.wait_ge(node_ready, 3)
            act.sem_inc(net_stored, 16)
            with act.Fori(0, NGRP) as i:
                turn("net", i)
                act.wait_ge(product_ready["net"], i + 1)
                act.wait_ge(net_stored, i * 16 + 16)
                ps = big_ps[0][:, 0, 0:GROUP * NODEW].rearrange("p (w k) -> p w k", k=NODEW)
                act.activation(net_out[:, :, :], ps[:, :, 0:NETW], ACT.Copy)
                act.activation(own[:, bass.ds(i * GROUP, GROUP), :], ps[:, :, NETW:NODEW], ACT.Copy)
                act.drain().then_inc(net_copied, 1)
            act.drain().then_inc(node_done, 1)
            act.wait_ge(bn_ready, 3)
            act.activation(scale[:, :], col_sum[:, :], ACT.Sqrt)
            act.drain().then_inc(root_done, 1)
            root(5)

        @block.tensor
        def _(pe):
            pe.wait_ge(consts, 1)
            pe.wait_ge(setup_pe, 1)
            pe.matmul(turn_ps[0:CHUNKS, 0:1], before[0:CHUNKS, 0:CHUNKS], passes_f[:, :], start=True, stop=True)
            pe.drain().then_inc(setup_pe, 1)
            pe.wait_ge(in_small, 16 * (13 + KE))
            pe.wait_ge(setup_pe, 3)
            pe.matmul(big_ps[0][0:RELS, 0, 0:F * F], comp[:, :], bases[:, :, :].rearrange("b i o -> b (i o)"),
                      start=True, stop=True)
            for t in range(3):
                pe.matmul(big_ps[0][:, 1, t * F:t * F + F], wa_wide[:, t, :], ws[:, :], start=(t == 0), stop=(t == 2),
                          skip_group_check=True)
            pe.matmul(big_ps[0][0:F, 2, 0:1], ws[:, :], wa[:, 0:1], start=True, stop=True)
            pe.drain().then_inc(setup_pe, 1)
            pe.wait_ge(meta_in, 32)

            def sum_windows(name, width):
                with pe.Fori(0, CHUNKS) as c:
                    passes = pe.value_load(meta_row[0:1, bass.ds(c * 4 + 1, 1)], min_val=1, max_val=NWIN)
                    first = pe.value_load(meta_row[0:1, bass.ds(c * 4 + 2, 1)], min_val=0, max_val=NWIN * CHUNKS)
                    with pe.Fori(0, passes) as k:
                        pe.wait_ge(hot_ready[name], first + k + 1)
                        for j in range(TILES):
                            for w in range(WIN):
                                rhs = parts_view(width)[:, j * PARTS * width:(j + 1) * PARTS * width]
                                n = rhs.shape[1]
                                pe.matmul(pass_ps[:, w * n:w * n + n], hot[:, j, w * P:w * P + P], rhs,
                                          start=(j == 0 and w == 0), stop=(j == TILES - 1),
                                          skip_group_check=True)
                        pe.drain().then_inc(pass_done[name], 1)

            def turn(name, i):
                pe.wait_ge(staged[name], i + 1)
                for w in range(GROUP):
                    pe.transpose(turn_ps[0:F, w * P:w * P + P], stage[:, w, :], identity[:, :])
                pe.drain().then_inc(turned_ps_ready[name], 1)
                pe.wait_ge(turned_ready[name], i + 1)

            def degrees(c, s, use, first=False):
                pe.wait_ge(window_ready[s], use + 1)
                pe.wait_ge(place_ready[s], use + 1)
                for j in range(TILES):
                    pe.matmul(pass_ps[:, 0:NWIN], hot_place(s)[:, j, :], hot_window(s)[:, j, :],
                              start=(first and s == 0 and j == 0), stop=True, skip_group_check=True)
                pe.drain().then_inc(degree_done[s], 1)
            chunks_after_first(pe, degrees)
            sum_windows("conv1", F)
            with pe.Fori(0, NGRP) as i:
                turn("hidden", i)
                pe.matmul(big_ps[0][0:HID, 0, :], w1[:, :], turned[:, :, :].rearrange("k w r -> k (w r)"),
                          start=True, stop=True)
                pe.drain().then_inc(hid_ps_ready, 1)
                pe.wait_ge(hid_ready, i + 1)
                for w in range(GROUP):
                    pe.matmul(big_ps[1][:, 0, w * F:w * F + F], hid[:, w * P:w * P + P], w2[:, :],
                              start=(w == 0), stop=(w == GROUP - 1), skip_group_check=True)
                pe.drain().then_inc(product_ready["hidden"], 1)
            sum_windows("conv2", F)
            def turn_stack(s, i):
                pe.transpose(stack_ps[s], h_stack[:, bass.ds(i * 2 + s, 1), :, :].rearrange("p a q f -> p (a q f)"),
                             identity_b[:, :])
                pe.drain().then_inc(stack_ps_ready[s], 1)

            def rows_by_relations(i, more=True):
                for s in range(2):
                    pe.wait_ge(stack_ready[s], i + 1)
                    pe.wait_ge(rel_copied[s], i * 2 + 1)
                    for b in range(RBANKS):
                        at = slice(b * RPB * RW, (b + 1) * RPB * RW)
                        pe.matmul(big_ps[s][:, b, 0:RPB * RW], turned_b[s][:, :], rel_stack[:, at],
                                  start=True, stop=False)
                    for b in range(RBANKS):
                        at = slice(b * RPB * RW, (b + 1) * RPB * RW)
                        pe.matmul(big_ps[s][:, b, 0:RPB * RW], turned_b[s][LOW:LOW + F, :], rel_low[LOW:LOW + F, at],
                                  start=False, stop=True)
                    pe.drain().then_inc(rel_ready[s], 1)
                    if more:
                        turn_stack(s, i + 1)
            pe.wait_ge(node_ready, 2)
            pe.wait_ge(rel_stacked, 16 * (len(MATE_ORDER) + 1))
            turn_stack(0, 0)
            turn_stack(1, 0)
            with pe.Fori(0, NW // 2 - 1) as i:
                rows_by_relations(i)
            rows_by_relations(NW // 2 - 1, more=False)
            sum_windows("rel", 2 * F)
            net_flat = net_rhs[:, :, :].rearrange("i k o -> i (k o)")
            with pe.Fori(0, NGRP) as i:
                turn("net", i)
                for w in range(GROUP):
                    pe.matmul(big_ps[0][:, 0, w * NODEW:w * NODEW + NODEW], turned[:, w, :], net_flat,
                              start=(w == 0), stop=(w == GROUP - 1), skip_group_check=True)
                pe.drain().then_inc(product_ready["net"], 1)
            sum_windows("net", F)
            for k in range(2):
                pe.wait_ge(bn_ready, k + 1)
                pe.matmul(turn_ps[:, 0:F], ones_f[:, :], col_sum[:, :], start=True, stop=True)
                pe.drain().then_inc(bn_sum, 1)
            width = PARTS * F
            per = BANK // width
            with pe.Fori(0, CHUNKS) as c:
                low = pe.value_load(meta_row[0:1, bass.ds(c * 4, 1)], min_val=0, max_val=NWIN - 1)
                passes = pe.value_load(meta_row[0:1, bass.ds(c * 4 + 1, 1)], min_val=1, max_val=NWIN)
                before_c = pe.value_load(meta_row[0:1, bass.ds(c * 4 + 2, 1)], min_val=0, max_val=NWIN * CHUNKS)
                with pe.Fori(0, passes) as k:
                    place = nc.s_assert_within(low + k * WIN, 0, NW, skip_runtime_bounds_check_because=
                                               "a pass begins at a window that the chunk touches")
                    pe.wait_ge(hot_ready["rat"], before_c + k + 1)
                    for j in range(TILES):
                        b, a = j // per, j % per
                        for w in range(WIN):
                            pe.matmul(big_ps[1][:, b, a * width:(a + 1) * width],
                                      hot_t[:, w, j:CE:TILES],
                                      h_parts[:, bass.ds(place + w, 1), 0:width].rearrange("p a f -> p (a f)"),
                                      start=(a == 0 and w == 0), stop=(w == WIN - 1), skip_group_check=True)
                    pe.drain().then_inc(pass_done["rat"], 1)
                pe.wait_ge(equal_ready, c + 1)
                for j in range(TILES):
                    b, a = j // per, j % per
                    pe.matmul(big_ps[0][:, b, a * width:(a + 1) * width], equal[:, j, :],
                              parts_view(F)[:, j * width:(j + 1) * width],
                              start=(a == 0), stop=(a == per - 1 or j == TILES - 1), skip_group_check=True)
                pe.drain().then_inc(equal_done, 1)

        @block.vector
        def _(dve):
            dve.memset(xs[:, NWIN - 1:NW, :], 0.0)
            dve.drain().then_inc(setup, 1)
            dve.memset(acc[:, :, :], 0.0)
            dve.drain().then_inc(zeroed, 1)
            dve.wait_ge(in_dst, 16)
            dve.tensor_copy(dst_f[:, :], int_a)
            dve.drain().then_inc(setup, 1)
            dve.wait_ge(in_span, 16)
            dve.tensor_reduce(span[:, 0:1], span_in, AX.X, ALU.min)
            dve.tensor_reduce(span[:, 1:2], span_in, AX.X, ALU.max)
            dve.memset(meta[:, :], 0)
            dve.drain()
            shift = P.bit_length() - 1
            dve.tensor_scalar(span[:, 2:4], span[:, 0:2], shift, None, ALU.logical_shift_right)
            dve.drain()
            dve.tensor_copy(meta[:, 0:1], span[:, 2:3])
            dve.tensor_scalar(base_f[:, :], span[:, 2:3], float(P), None, ALU.mult)
            dve.tensor_tensor(span[:, 0:1], span[:, 3:4], span[:, 2:3], ALU.subtract)
            dve.drain()
            dve.tensor_scalar(span[:, 1:2], span[:, 0:1], float(WIN), None, ALU.add)
            dve.drain()
            dve.tensor_scalar(meta[:, 1:2], span[:, 1:2], WIN.bit_length() - 1, None, ALU.logical_shift_right)
            dve.drain()
            dve.tensor_copy(passes_f[:, :], meta[:, 1:2])
            dve.drain().then_inc(setup_pe, 1)
            dve.wait_ge(setup_pe, 2)
            dve.tensor_copy(meta[:, 2:3], turn_ps[0:CHUNKS, 0:1])
            dve.drain().then_inc(setup, 1)
            dve.wait_ge(in_srctype, 32)
            dve.scalar_tensor_tensor(out=int_b, in0=int_a, scalar=float(RELS), in1=int_b,
                                     op0=ALU.mult, op1=ALU.add)
            dve.drain().then_inc(setup, 1)
            dve.tensor_copy(int_a, dst_f[:, :])
            dve.drain()
            dve.tensor_scalar(int_a, int_a, shift, None, ALU.logical_shift_right)
            dve.drain()
            dve.tensor_copy(dst_window, int_a)
            dve.drain()
            dve.scalar_tensor_tensor(out=dst_place, in0=dst_window, scalar=-float(P), in1=dst_f[:, :],
                                     op0=ALU.mult, op1=ALU.add)
            dve.drain().then_inc(split_dst, 1)
            dve.wait_ge(in_small, 16 * (13 + KE))
            dve.tensor_copy(wa_wide[:, :, :], wa[:, :].unsqueeze(2).broadcast_to([F, 3, P]))
            dve.drain().then_inc(setup_pe, 1)
            dve.wait_ge(setup_pe, 4)
            dve.tensor_copy(w_rel_sb[:, :], big_ps[0][0:RELS, 0, 0:F * F])
            dve.drain().then_inc(setup, 1)
            dve.tensor_copy(a_rows[:, :, :].rearrange("p t f -> p (t f)"), big_ps[0][:, 1, 0:3 * F])
            dve.tensor_copy(a_col[:, :], big_ps[0][0:F, 2, 0:1])
            dve.wait_ge(w_rel_in, 16)
            dve.drain()
            dve.tensor_copy(rel_rhs[:, :, F:RW], a_col[:, :].unsqueeze(2).broadcast_to([F, RELS, 1]))
            dve.drain()
            flat = rel_rhs[:, :, :].rearrange("i r o -> i (r o)")
            dve.tensor_copy(mat_parts[:, 0, :], flat)
            dve.drain()
            dve.tensor_tensor(flat, flat, mat_parts[:, 0, :], ALU.subtract)
            dve.drain()
            dve.tensor_copy(mat_parts[:, 1, :], flat)
            dve.drain()
            dve.tensor_tensor(mat_parts[:, 2, :], flat, mat_parts[:, 1, :], ALU.subtract)
            dve.drain().then_inc(rel_split, 1)
            dve.wait_ge(consts, 1)
            dve.tensor_scalar(valid[:, :], valid[:, :], float(N), None, ALU.is_lt)
            dve.drain()

            def wide(v):
                return v.unsqueeze(2).broadcast_to([P, NW, F])

            def per_feature(v):
                return v.unsqueeze(1).broadcast_to([P, NW, F])

            def norm(k):
                dve.tensor_reduce(row_a[:, :], xs[:, :, :], AX.X, ALU.add)
                dve.drain()
                dve.tensor_scalar(row_a[:, :], row_a[:, :], 1.0 / F, None, ALU.mult)
                dve.drain()
                dve.tensor_tensor(h[:, :, :], xs[:, :, :], wide(row_a[:, :]), ALU.subtract)
                dve.drain()
                dve.tensor_tensor(tmp[:, :, :], h[:, :, :], h[:, :, :], ALU.mult)
                dve.drain()
                dve.tensor_reduce(row_a[:, :], tmp[:, :, :], AX.X, ALU.add)
                dve.drain()
                dve.tensor_scalar(row_a[:, :], row_a[:, :], 1.0 / F, EPS, ALU.mult, ALU.add)
                dve.drain().then_inc(var_ready, 1)
                dve.wait_ge(root_done, k)
                dve.reciprocal(row_a[:, :], row_b[:, :])
                dve.drain()
                dve.tensor_tensor(h[:, :, :], h[:, :, :], wide(row_a[:, :]), ALU.mult)
                dve.drain()
                dve.tensor_scalar(h[:, :, :], h[:, :, :], 0.0, None, ALU.max)
                dve.drain()

            def split(of, width):
                v = parts_view(width).rearrange("p (j s f) -> p j s f", j=TILES, s=PARTS)
                r = rest[:, :, 0:width]
                dve.tensor_copy(v[:, :, 0, :], of)
                dve.drain()
                dve.tensor_tensor(r, of, v[:, :, 0, :], ALU.subtract)
                dve.drain()
                dve.tensor_copy(v[:, :, 1, :], r)
                dve.drain()
                dve.tensor_tensor(v[:, :, 2, :], r, v[:, :, 1, :], ALU.subtract)
                dve.drain()

            def passes_of(name, c, width):
                low = dve.value_load(meta_row[0:1, bass.ds(c * 4, 1)], min_val=0, max_val=NWIN - 1)
                passes = dve.value_load(meta_row[0:1, bass.ds(c * 4 + 1, 1)], min_val=1, max_val=NWIN)
                first = dve.value_load(meta_row[0:1, bass.ds(c * 4 + 2, 1)], min_val=0, max_val=NWIN * CHUNKS)
                dve.tensor_tensor(dst_rel[:, :], dst_f[:, bass.ds(c * TILES, TILES)],
                                  base_all[:, bass.ds(c, 1)].broadcast_to([P, TILES]), ALU.subtract)
                dve.drain()
                with dve.Fori(0, passes) as k:
                    for j in range(TILES):
                        dve.tensor_scalar(hot[:, j, :], iota_span[:, :], dst_rel[:, j:j + 1], None, ALU.is_equal)
                    dve.drain().then_inc(hot_ready[name], 1)
                    dve.tensor_scalar(dst_rel[:, :], dst_rel[:, :], -float(SPAN), None, ALU.add)
                    dve.wait_ge(pass_done[name], first + k + 1)
                    place = nc.s_assert_within(low + k * WIN, 0, NW, skip_runtime_bounds_check_because=
                                               "a pass begins at a window that the chunk touches")
                    dve.tensor_reduce(part_sum[:, :, 0:width],
                                      pass_ps[:, 0:WIN * PARTS * width]
                                      .rearrange("p (w s f) -> p w f s", w=WIN, s=PARTS), AX.X, ALU.add)
                    dve.drain()
                    at = acc[:, bass.ds(place, WIN), 0:width]
                    dve.tensor_tensor(at, at, part_sum[:, :, 0:width], ALU.add)
                    dve.drain()

            def clear_sums(width):
                dve.memset(acc[:, :, 0:width], 0.0)
                dve.drain()

            def edges(name, width, message):
                for s in range(2):
                    dve.sem_inc(rows_free[name][s], 1)

                def body(c, s, use):
                    dve.wait_ge(gathered[name][s], use * LAND + LAND)
                    message(s, use)
                    dve.drain().then_inc(rows_free[name][s], 1)
                    passes_of(name, c, width)
                chunks(dve, body)

            def plain(s, use):
                split(rows[s][:, :, 0:F], F)

            dve.wait_ge(in_x, 32)
            norm(1)
            dve.wait_ge(meta_in, 32)
            dve.wait_ge(relidx_out, 16)

            def places(c, s, use, first=False):
                if not first:
                    dve.wait_ge(degree_done[s], use)
                for j in range(TILES):
                    dve.tensor_scalar(hot_place(s)[:, j, :], iota_span[:, 0:P],
                                      dst_place[:, bass.ds(c * TILES + j, 1)], None, ALU.is_equal)
                for j in range(TILES - POOL_TILES):
                    dve.tensor_scalar(hot_window(s)[:, j, :], iota_span[:, 0:NWIN],
                                      dst_window[:, bass.ds(c * TILES + j, 1)], None, ALU.is_equal)
                dve.drain().then_inc(place_ready[s], 1)
            chunks_after_first(dve, places)
            dve.memset(deg[:, :], 0.0)
            for s in range(2):
                dve.wait_ge(degree_done[s], PAIRS + 1 - s)
            dve.drain()
            dve.tensor_copy(deg[:, 0:NWIN], pass_ps[:, 0:NWIN])
            dve.drain()
            dve.tensor_scalar(row_a[:, :], deg[:, :], 1.0, None, ALU.add)
            dve.drain().then_inc(var_ready, 1)
            dve.wait_ge(root_done, 2)
            dve.reciprocal(dinv[:, :], row_b[:, :])
            dve.drain()
            dve.tensor_tensor(g[:, :, :], h[:, :, :], wide(dinv[:, :]), ALU.mult)
            dve.drain().then_inc(table_ready, 1)
            dve.wait_ge(zeroed, 2 + 48 * COPIES)
            edges("conv1", F, plain)
            dve.tensor_tensor(g[:, :, :], g[:, :, :], acc[:, 0:NW, 0:F], ALU.add)
            dve.drain()
            dve.tensor_tensor(g[:, :, :], g[:, :, :], wide(dinv[:, :]), ALU.mult)
            dve.drain().then_inc(node_ready, 1)
            dve.wait_ge(node_done, 1)
            dve.tensor_tensor(g[:, :, :], tmp[:, :, :], wide(dinv[:, :]), ALU.mult)
            dve.drain().then_inc(table_ready, 1)
            clear_sums(F)
            edges("conv2", F, plain)
            dve.tensor_tensor(g[:, :, :], g[:, :, :], acc[:, 0:NW, 0:F], ALU.add)
            dve.drain()
            dve.tensor_tensor(g[:, :, :], g[:, :, :], wide(dinv[:, :]), ALU.mult)
            dve.drain()
            dve.tensor_tensor(xs[:, :, :], xs[:, :, :], g[:, :, :], ALU.add)
            dve.drain()
            dve.tensor_tensor(xs[:, :, :], xs[:, :, :], per_feature(b2[:, :]), ALU.add)
            dve.drain()

            norm(3)
            for s in range(2):
                dve.sem_inc(rel_copied[s], 1)
            hi, mid, lo = (PAIR_ORDER.index(q) for q in range(PARTS))
            dve.tensor_copy(h_stack[:, :, hi, :], h[:, :, :])
            dve.drain()
            dve.tensor_tensor(tmp[:, :, :], h[:, :, :], h_stack[:, :, hi, :], ALU.subtract)
            dve.drain()
            dve.tensor_copy(h_stack[:, :, mid, :], tmp[:, :, :])
            dve.drain()
            dve.tensor_tensor(h_stack[:, :, lo, :], tmp[:, :, :], h_stack[:, :, mid, :], ALU.subtract)
            dve.drain()
            for q, part in enumerate(PAIR_ORDER):
                if q != PAIR_ORDER.index(part):
                    dve.tensor_copy(h_stack[:, :, q, :], h_stack[:, :, PAIR_ORDER.index(part), :])
            dve.drain().then_inc(node_ready, 1)
            with dve.Fori(0, NW // 2) as i:
                for s in range(2):
                    dve.wait_ge(rel_ready[s], i + 1)
                    dve.wait_ge(rel_stored[s], i * 16 + 16)
                    for b in range(RBANKS - 1 - s, RBANKS):
                        dve.tensor_copy(rel_out[s][:, b * RPB * RW:(b + 1) * RPB * RW], big_ps[s][:, b, 0:RPB * RW])
                    dve.drain().then_inc(rel_copied[s], 1)
            clear_sums(2 * F)

            def relational(s, use):
                dve.wait_ge(attr_in["rel"][s], use * 16 + 16)
                dve.tensor_tensor(msg[:, :, 0:F], attr[s][:, :, :],
                                  a_rows[:, 1, :].unsqueeze(1).broadcast_to([P, TILES, F]), ALU.mult)
                dve.drain()
                dve.tensor_reduce(score[:, :], msg[:, :, 0:F], AX.X, ALU.add)
                dve.drain()
                dve.tensor_tensor(score[:, :], score[:, :], rows[s][:, :, F], ALU.add)
                dve.drain()
                dve.tensor_tensor(msg[:, :, 0:F], rows[s][:, :, 0:F],
                                  score[:, :].unsqueeze(2).broadcast_to([P, TILES, F]), ALU.mult)
                dve.tensor_copy(msg[:, :, F:2 * F], rows[s][:, :, 0:F])
                dve.drain()
                split(msg[:, :, :], 2 * F)
            edges("rel", 2 * F, relational)
            dve.tensor_tensor(tmp[:, :, :], h[:, :, :], per_feature(a_rows[:, 2, :]), ALU.mult)
            dve.drain()
            dve.tensor_reduce(row_a[:, :], tmp[:, :, :], AX.X, ALU.add)
            dve.drain()
            dve.tensor_tensor(tmp[:, :, :], acc[:, 0:NW, F:2 * F], wide(row_a[:, :]), ALU.mult)
            dve.drain()
            dve.tensor_tensor(tmp[:, :, :], tmp[:, :, :], acc[:, 0:NW, 0:F], ALU.add)
            dve.drain()
            dve.tensor_tensor(xs[:, :, :], xs[:, :, :], tmp[:, :, :], ALU.add)
            dve.drain()

            norm(4)
            dve.drain().then_inc(node_ready, 1)
            clear_sums(F)

            def network(s, use):
                dve.wait_ge(attr_in["net"][s], use * 16 + 16)
                for k in range(KE):
                    dve.tensor_tensor(work[:, :, k * F:k * F + F], rows[s][:, :, k * F:k * F + F],
                                      attr[s][:, :, k:k + 1].broadcast_to([P, TILES, F]), ALU.mult)
                dve.drain()
                dve.tensor_tensor(work[:, :, 0:2 * F], work[:, :, 0:2 * F], work[:, :, 2 * F:4 * F], ALU.add)
                dve.drain()
                dve.tensor_tensor(work[:, :, 0:F], work[:, :, 0:F], work[:, :, F:2 * F], ALU.add)
                dve.drain()
                dve.tensor_tensor(msg[:, :, 0:F], work[:, :, 0:F], rows[s][:, :, KE * F:NETW], ALU.add)
                dve.drain()
                split(msg[:, :, 0:F], F)
            edges("net", F, network)
            dve.tensor_scalar(row_a[:, :], deg[:, :], 1.0, None, ALU.max)
            dve.drain()
            dve.reciprocal(row_a[:, :], row_a[:, :])
            dve.drain()
            dve.tensor_tensor(tmp[:, :, :], acc[:, 0:NW, 0:F], wide(row_a[:, :]), ALU.mult)
            dve.wait_ge(node_done, 2)
            dve.drain()
            dve.tensor_tensor(tmp[:, :, :], tmp[:, :, :], own[:, :, :], ALU.add)
            dve.drain()
            dve.tensor_tensor(tmp[:, :, :], tmp[:, :, :], per_feature(bias[:, :]), ALU.add)
            dve.drain()

            def over_nodes(k):
                dve.tensor_reduce(col_sum[:, :], g[:, :, :].rearrange("p w f -> p f w"), AX.X, ALU.add)
                dve.drain().then_inc(bn_ready, 1)
                dve.wait_ge(bn_sum, k)
            dve.tensor_tensor(g[:, :, :], tmp[:, :, :], wide(valid[:, :]), ALU.mult)
            dve.drain()
            over_nodes(1)
            dve.tensor_scalar(mean[:, :], turn_ps[:, 0:F], 1.0 / N, None, ALU.mult)
            dve.drain()
            dve.tensor_tensor(tmp[:, :, :], tmp[:, :, :], per_feature(mean[:, :]), ALU.subtract)
            dve.drain()
            dve.tensor_tensor(g[:, :, :], tmp[:, :, :], wide(valid[:, :]), ALU.mult)
            dve.drain()
            dve.tensor_tensor(g[:, :, :], g[:, :, :], g[:, :, :], ALU.mult)
            dve.drain()
            over_nodes(2)
            dve.tensor_scalar(col_sum[:, :], turn_ps[:, 0:F], 1.0 / N, EPS, ALU.mult, ALU.add)
            dve.drain().then_inc(bn_ready, 1)
            dve.wait_ge(root_done, 4 + 1)
            dve.reciprocal(scale[:, :], scale[:, :])
            dve.drain()
            dve.tensor_tensor(scale[:, :], scale[:, :], gamma[:, :], ALU.mult)
            dve.drain()
            dve.tensor_tensor(tmp[:, :, :], tmp[:, :, :], per_feature(scale[:, :]), ALU.mult)
            dve.drain()
            dve.tensor_tensor(tmp[:, :, :], tmp[:, :, :], per_feature(beta[:, :]), ALU.add)
            dve.drain()
            dve.tensor_scalar(g[:, :, :], tmp[:, :, :], SLOPE, None, ALU.mult)
            dve.drain()
            dve.tensor_tensor(tmp[:, :, :], tmp[:, :, :], g[:, :, :], ALU.max)
            dve.drain()
            dve.tensor_tensor(xs[:, :, :], xs[:, :, :], tmp[:, :, :], ALU.add)
            dve.drain()

            norm(6)
            dve.tensor_copy(g[:, :, :], h[:, :, :])
            dve.drain().then_inc(table_ready, 1)
            dve.tensor_scalar(tmp[:, :, :], h[:, :, :], -1.0 / FK, 1.0, ALU.mult, ALU.add)
            dve.tensor_scalar(own[:, :, :], h[:, :, :], 1.0 / FC, -1.0, ALU.mult, ALU.add)
            dve.drain()
            dve.tensor_tensor(tmp[:, :, :], tmp[:, :, :], h[:, :, :], ALU.mult)
            dve.drain()
            dve.tensor_tensor(own[:, :, :], tmp[:, :, :], own[:, :, :], ALU.mult)
            dve.drain()
            dve.tensor_scalar(own[:, :, :], own[:, :, :], FB, None, ALU.add)
            dve.drain()
            dve.tensor_tensor(xs[:, :, :], xs[:, :, :], own[:, :, :], ALU.add)
            dve.memset(h_parts, 0.0)
            dve.drain()
            hi, mid, lo = (h_parts[:, 0:NW, q * F:q * F + F] for q in range(PARTS))
            dve.tensor_copy(hi, h[:, :, :])
            dve.drain()
            dve.tensor_tensor(tmp[:, :, :], h[:, :, :], hi, ALU.subtract)
            dve.drain()
            dve.tensor_copy(mid, tmp[:, :, :])
            dve.drain()
            dve.tensor_tensor(lo, tmp[:, :, :], mid, ALU.subtract)
            dve.drain()
            for s in range(2):
                dve.sem_inc(rows_free["rat"][s], 1)
            dve.sem_inc(dst_row_free, 1)
            per = BANK // (PARTS * F)

            def tile_rows(ps, to):
                for b in range((TILES + per - 1) // per):
                    n = min(per, TILES - b * per)
                    dve.tensor_reduce(to[:, b * per:b * per + n, :], ps[:, b, 0:n * PARTS * F]
                                      .rearrange("p (a q f) -> p a f q", a=n, q=PARTS), AX.X, ALU.add)

            def targets(c):
                passes = dve.value_load(meta_row[0:1, bass.ds(c * 4 + 1, 1)], min_val=1, max_val=NWIN)
                before_c = dve.value_load(meta_row[0:1, bass.ds(c * 4 + 2, 1)], min_val=0, max_val=NWIN * CHUNKS)
                dve.wait_ge(dst_row_in, c * 16 + 16)
                dve.memset(xj[:, :, :], 0.0)
                dve.tensor_tensor(node_of[:, :], node_ids[:, :], base_all[:, bass.ds(c, 1)].broadcast_to([P, WIN]),
                                  ALU.add)
                dve.drain()
                with dve.Fori(0, passes) as k:
                    for w in range(WIN):
                        dve.tensor_scalar(hot_t[:, w, :], dst_row[:, :], node_of[:, w:w + 1], None, ALU.is_equal)
                    dve.drain().then_inc(hot_ready["rat"], 1)
                    dve.tensor_scalar(node_of[:, :], node_of[:, :], float(SPAN), None, ALU.add)
                    dve.wait_ge(pass_done["rat"], before_c + k + 1)
                    tile_rows(big_ps[1], rest[:, :, 0:F])
                    dve.drain()
                    dve.tensor_tensor(xj[:, :, :], xj[:, :, :], rest[:, :, 0:F], ALU.add)
                    dve.drain()
                dve.drain().then_inc(dst_row_free, 1)

            def rational(c, s, use, first=False):
                targets(c)
                dve.wait_ge(gathered["rat"][s], use * LAND + LAND)
                dve.wait_ge(weight_in[s], use * 16 + 16)
                xi = rows[s][:, :, 0:F]
                den, top = work[:, :, 0:F], work[:, :, F:2 * F]
                dve.tensor_scalar(den, xi, FE, FD, ALU.mult, ALU.add)
                dve.tensor_tensor(top, xi, xj[:, :, :], ALU.mult)
                dve.drain()
                dve.scalar_tensor_tensor(out=den, in0=xj[:, :, :], scalar=FH, in1=den, op0=ALU.mult, op1=ALU.add)
                dve.tensor_tensor(top, top, weight[s][:, :].unsqueeze(2)
                                  .broadcast_to([P, TILES, F]), ALU.mult)
                dve.drain()
                dve.reciprocal(msg[:, :, 0:F], den)
                dve.drain()
                dve.tensor_tensor(msg[:, :, 0:F], msg[:, :, 0:F], top, ALU.mult)
                dve.drain()
                split(msg[:, :, 0:F], F)
                dve.wait_ge(src_row_in[s], use * 16 + 16)
                dve.tensor_tensor(equal, src_row[s][:, :].rearrange("q (p j) -> q j p", j=TILES),
                                  index[s][:, :].unsqueeze(2).broadcast_to([P, TILES, P]), ALU.is_equal)
                dve.drain().then_inc(equal_ready, 1)
                before_row = src_row[s][:, 0:CE // 2].bitcast(BF16).rearrange("p (j q) -> p j q", q=P)
                dve.tensor_tensor(before_row, equal,
                                  earlier[:, :].unsqueeze(1).broadcast_to([P, TILES, P]), ALU.mult)
                dve.drain()
                dve.tensor_reduce(seen[:, :], before_row, AX.X, ALU.add)
                dve.drain()
                dve.tensor_scalar(seen[:, :], seen[:, :], 0.5, None, ALU.is_gt)
                dve.tensor_scalar(score[:, :], index[s][:, :], -1.0, spare[:, 0:1], ALU.mult, ALU.add)
                dve.drain()
                dve.tensor_tensor(score[:, :], score[:, :], seen[:, :], ALU.mult)
                dve.drain()
                if not first:
                    for k in range(COPIES):
                        dve.wait_ge(scattered[k], (c - 1) * (16 * TILES // COPIES))
                dve.tensor_tensor(scat_index[s][:, :], score[:, :], index[s][:, :], ALU.add)
                dve.drain().then_inc(rows_free["rat"][s], 1)
                dve.wait_ge(equal_done, c + 1)
                tile_rows(big_ps[0], scat[s])
                dve.drain().then_inc(scat_ready[s], 1)
            chunks_after_first(dve, rational)
            dve.drain().then_inc(sums_ready, 1)
            dve.wait_ge(sums_in, 32 * COPIES)
            for v in (acc[:, 0:NW, 0:F], acc[:, 0:NW, F:2 * F], tmp[:, :, :], h[:, :, :], g[:, :, :]):
                dve.tensor_tensor(xs[:, 0:NWIN, :], xs[:, 0:NWIN, :], v[:, 0:NWIN, :], ALU.add)
                dve.drain()
            dve.drain().then_inc(out_ready, 1)


_INS = ['x', 'src', 'dst', 'edge_attr_16', 'edge_attr_4', 'edge_type_90', 'edge_weight', 'L0_gnn_W1', 'L0_gnn_b1',
        'L0_gnn_W2', 'L0_gnn_b2', 'L1_gnn_Ws', 'L1_gnn_Wa', 'L1_gnn_weight', 'L1_gnn_w_comp', 'L2_gnn_enet_w',
        'L2_gnn_enet_b', 'L2_gnn_root', 'L2_gnn_bias', 'L2_gnn_gamma', 'L2_gnn_beta']


def kernel(**inputs):
    import numpy as np
    import concourse.bacc as bacc
    from concourse.bass_utils import run_bass_kernel_spmd

    nc = bacc.Bacc("TRN2", target_bir_lowering=False, num_devices=1)
    arrays, args = {}, []
    for name in _INS:
        a = np.ascontiguousarray(inputs[name])
        arrays[f"in_{name}"] = a
        args.append(nc.dram_tensor(f"in_{name}", a.shape, mybir.dt.from_np(a.dtype), kind="ExternalInput").ap())
    result = nc.dram_tensor("out_x", inputs["x"].shape, F32, kind="ExternalOutput").ap()
    build_program(nc, *args, result)
    r = run_bass_kernel_spmd(nc, [arrays], core_ids=[0])
    return r.results[0]["out_x"]
```

```python
from contextlib import ExitStack

import concourse.bass as bass
from concourse import mybir

ALU = mybir.AluOpType
ACT = mybir.ActivationFunctionType
AX = mybir.AxisListType
F32 = mybir.dt.float32
F16 = mybir.dt.float16
BF16 = mybir.dt.bfloat16
I32 = mybir.dt.int32

P = 128
F = 16
TILES = 25
WIN = 4
DENSE = {"conv1": 3, "rat": 7}
FPB = 4
FAR = 2.0 ** 100
PADDED = TILES + 1
NOWHERE = 200
PAIR_ORDER = (0, 0, 1, 0, 2, 1, 1, 2)
MATE_ORDER = (0, 1, 0, 2, 0, 1, 2, 1)
GROUP = 4
COPIES = 5
PARTS = 3
BANK = 512
EPS = 1e-5
SLOPE = 0.01
FB, FK, FC, FD, FE, FH = 0.1, 5.0, 1.0, 5.0, 0.9, 0.1


def build_program(nc, x, src, dst, edge_attr_16, edge_attr_4, edge_type_90, edge_weight, gcn_w1, gcn_b1, gcn_w2,
                  gcn_b2, rel_ws, rel_wa, rel_weight, rel_comp, net_w, net_b, net_root, net_bias, net_gamma,
                  net_beta, out):
    N = x.shape[0]
    E = src.shape[0]
    CE = P * TILES
    CHUNKS = E // CE
    NWIN = (N + P - 1) // P
    NGRP = (NWIN + GROUP - 1) // GROUP
    NW = NGRP * GROUP
    NROW = NW * P
    AW = NW + WIN
    LAST = N - (NWIN - 1) * P
    HID = gcn_w1.shape[1]
    BASES = rel_weight.shape[0]
    RELS = rel_comp.shape[0]
    KE = edge_attr_4.shape[1]
    RW = F + 1
    RPB = BANK // RW
    RBANKS = RELS // RPB
    NETW = (KE + 1) * F
    NODEW = NETW + F
    assert NW == 4 * TILES
    assert E == CE * CHUNKS and CHUNKS % 2 == 1 and RELS == RPB * RBANKS and TILES % COPIES == 0
    PAIRS = CHUNKS // 2
    SPAN = WIN * P

    def land(name):
        return 16 * (TILES - DENSE.get(name, 0))

    tab1 = nc.dram_tensor("tab1", [NROW, F], F32).ap()
    tab2 = nc.dram_tensor("tab2", [NROW, F], F32).ap()
    tab_rel = nc.dram_tensor("tab_rel", [NROW * RELS, RW], F32).ap()
    tab_net = nc.dram_tensor("tab_net", [NROW, NETW], F32).ap()
    tab3 = nc.dram_tensor("tab3", [NROW, F], F32).ap()
    rel_index = nc.dram_tensor("rel_index", [E], I32).ap()
    w_rel_flat = nc.dram_tensor("w_rel_flat", [RELS * F * F], F32).ap()
    meta_dram = nc.dram_tensor("meta_dram", [CHUNKS, 4], I32).ap()
    base_dram = nc.dram_tensor("base_dram", [CHUNKS], F32).ap()
    sums = [nc.dram_tensor(f"sums{k}", [N + P, F], F32).ap() for k in range(COPIES)]

    def by_window(t):
        return t.rearrange("(w r) f -> r w f", r=P)

    def by_chunk(t):
        return t.rearrange("(c p j) -> c p j", p=P, j=TILES)

    def resident(t):
        return t.rearrange("(c p j) -> p c j", p=P, j=TILES)

    ctx = ExitStack()
    with ctx:
        def sb(name, shape, dt=F32):
            return ctx.enter_context(nc.sbuf_tensor(name, shape, dt))

        def sem(name):
            return ctx.enter_context(nc.semaphore(name))

        ctx.enter_context(nc.allow_non_contiguous_dma("rows of 64 bytes, small weights"))

        xs = sb("xs", [P, NW, F])
        h = sb("h", [P, NW, F])
        g = sb("g", [P, NW, F])
        tmp = sb("tmp", [P, NW, F])
        own = sb("own", [P, NW, F])
        acc = sb("acc", [P, AW, 2 * F])
        deg = sb("deg", [P, NW])
        dinv = sb("dinv", [P, NW])
        row_a = sb("row_a", [P, NW])
        row_b = sb("row_b", [P, NW])
        valid = sb("valid", [P, NW])
        dst_f = sb("dst_f", [P, CHUNKS * TILES])
        weight = [sb(f"weight{s}", [P, TILES]) for s in range(2)]
        dst_row = sb("dst_row", [P, CE], I32)
        span = sb("span", [CHUNKS, 4], I32)
        meta = sb("meta", [CHUNKS, 4], I32)
        passes_f = sb("passes_f", [CHUNKS, 1])
        base_f = sb("base_f", [CHUNKS, 1])
        meta_row = sb("meta_row", [1, CHUNKS * 4], I32)
        base_all = sb("base_all", [P, CHUNKS])
        before = sb("before", [P, P])
        earlier = sb("earlier", [P, P], BF16)
        identity_b = sb("identity_b", [P, P], BF16)
        identity = sb("identity", [P, P])
        ones_f = sb("ones_f", [P, P])
        ones_b = sb("ones_b", [P, 1], BF16)
        iota_span = sb("iota_span", [P, SPAN], F16)
        spare = sb("spare", [P, 1])
        hot = sb("hot", [P, TILES, SPAN], BF16)
        ints = hot[:, :, :].rearrange("p j n -> p (j n)").bitcast(I32)
        int_a = ints[:, 0:CHUNKS * TILES]
        int_b = ints[:, CHUNKS * TILES:2 * CHUNKS * TILES]
        parts = sb("parts", [P, TILES, PARTS, 2 * F], BF16)
        dst_rel = sb("dst_rel", [P, TILES])
        index = [sb(f"index{s}", [P, TILES], I32) for s in range(2)]
        xj = sb("xj", [P, TILES, F])
        node_of = sb("node_of", [P, WIN])
        node_ids = sb("node_ids", [P, WIN])
        rows = [sb(f"rows{s}", [P, TILES, NETW]) for s in range(2)]
        attr = [sb(f"attr{s}", [P, TILES, F]) for s in range(2)]
        msg = sb("msg", [P, TILES, 2 * F])
        work = sb("work", [P, TILES, KE * F])
        rest = sb("rest", [P, TILES, 2 * F])
        score = sb("score", [P, TILES])
        hot_flat = hot[:, :, :].rearrange("p j n -> p (j n)")
        h_stack = hot_flat.rearrange("p (w q f) -> p w q f", w=NW, q=P // F)
        near_hot = sb("near_hot", [P, max(DENSE.values()), 2, P], BF16)
        near_int = sb("near_int", [P, 2, max(DENSE.values())], I32)
        near_b = sb("near_b", [P, 2, max(DENSE.values())], BF16)
        near_mask = sb("near_mask", [P, FPB, NWIN], BF16)
        unused = sb("unused", [P, FPB, NWIN])
        hot_t = hot_flat.rearrange("p (w e) -> p w e", w=WIN)
        net_parts = dst_row[0:F, :].bitcast(BF16)[:, 0:PARTS * NODEW].rearrange("i (q n) -> i q n", q=PARTS)
        mat_parts = dst_row[0:F, :].bitcast(BF16)[:, 0:PARTS * RELS * RW].rearrange("i (q n) -> i q n", q=PARTS)
        LOW = PAIR_ORDER.index(2) * F
        equal = own[:, :, :].rearrange("p w f -> p (w f)").bitcast(BF16)[:, 0:CE].rearrange("p (j q) -> p j q", q=P)
        part_sum = sb("part_sum", [P, WIN, 2 * F])
        src_row = [sb(f"src_row{s}", [P, CE], I32) for s in range(2)]
        near_table = {"conv1": src_row[0][:, :].bitcast(BF16),
                      "rat": acc[:, :, :].rearrange("p w f -> p (w f)").bitcast(BF16)}
        near_table = {n: t[:, 0:PARTS * F * AW].rearrange("p (q w) -> p q w", w=AW) for n, t in near_table.items()}
        int_c = dst_row[:, 0:CHUNKS * TILES]
        half_row = CHUNKS * PADDED
        dst_window = src_row[1][:, :].bitcast(F16)[:, 0:half_row].rearrange("p (c j) -> p c j", j=PADDED)
        dst_place = src_row[0][:, :].bitcast(F16)[:, 0:half_row].rearrange("p (c j) -> p c j", j=PADDED)
        counting = rows[0][:, :, :].rearrange("p j f -> p (j f)").bitcast(F16)[:, 0:P * PADDED]\
            .rearrange("p (n j) -> p n j", j=PADDED)
        span_in = src_row[0][0:CHUNKS, :]
        seen = sb("seen", [P, TILES])
        scat = [sb(f"scat{s}", [P, TILES, F]) for s in range(2)]
        scat_index = [sb(f"scat_index{s}", [P, TILES], I32) for s in range(2)]
        stage = sb("stage", [P, GROUP, F])
        turned = sb("turned", [F, GROUP, P])
        turned_b = [sb(f"turned_b{k}", [P, P], BF16) for k in range(2)]
        hid = sb("hid", [HID, GROUP * P])
        rel_out = [r[:, 0:RELS * RW].bitcast(F32) for r in src_row]
        w1 = sb("w1", [F, HID])
        w2 = sb("w2", [HID, F])
        b1 = sb("b1", [HID, 1])
        b2 = sb("b2", [P, F])
        ws = sb("ws", [F, F])
        wa = sb("wa", [F, 3])
        wa_wide = sb("wa_wide", [F, 3, P])
        a_rows = sb("a_rows", [P, 3, F])
        a_col = sb("a_col", [F, 1])
        comp = sb("comp", [BASES, RELS])
        bases = sb("bases", [BASES, F, F])
        w_rel_sb = sb("w_rel_sb", [RELS, F * F])
        rel_rhs = sb("rel_rhs", [F, RELS, RW])
        rel_stack = sb("rel_stack", [P, RELS * RW], BF16)
        net_stack = sb("net_stack", [P, NODEW], BF16)
        net_low = sb("net_low", [P, NODEW], BF16)
        rel_low = sb("rel_low", [P, RELS * RW], BF16)
        net_rhs = sb("net_rhs", [F, NODEW // F, F])
        bias = sb("bias", [P, F])
        gamma = sb("gamma", [P, F])
        beta = sb("beta", [P, F])
        col_sum = sb("col_sum", [P, F])
        mean = sb("mean", [P, F])
        scale = sb("scale", [P, F])

        pass_ps = ctx.enter_context(nc.psum_tensor("pass_ps", [P, BANK], F32))
        turn_ps = ctx.enter_context(nc.psum_tensor("turn_ps", [P, BANK], F32))
        big_ps = [ctx.enter_context(nc.psum_tensor(f"big_ps{k}", [P, RBANKS, BANK], F32)) for k in range(2)]

        stack_ps = [t[:, 0:P // 2].bitcast(BF16) for t in (turn_ps, pass_ps)]

        near_banks = {"conv1": [big_ps[0][:, b, :] for b in range(3)] + [big_ps[1][:, 0, :]],
                      "rat": [big_ps[0][:, b, :] for b in range(3)] + [pass_ps[:, :]]}

        pool_turns = sem("pool_turns")
        near_table_ready = {n: sem(f"near_table_ready_{n}") for n in DENSE}
        consts = sem("consts")
        in_x = sem("in_x")
        in_small = sem("in_small")
        in_span = sem("in_span")
        in_dst = sem("in_dst")
        in_srctype = sem("in_srctype")
        place_ready = [sem(f"place_ready{k}") for k in range(2)]
        degree_done = [sem(f"degree_done{k}") for k in range(2)]
        weight_in = [sem(f"weight_in{k}") for k in range(2)]
        dst_row_in = sem("dst_row_in")
        dst_row_free = sem("dst_row_free")
        setup = sem("setup")
        setup_pe = sem("setup_pe")
        meta_out = sem("meta_out")
        meta_in = sem("meta_in")
        relidx_out = sem("relidx_out")
        w_rel_out = sem("w_rel_out")
        w_rel_in = sem("w_rel_in")
        zeroed = sem("zeroed")
        var_ready = sem("var_ready")
        root_done = sem("root_done")
        table_ready = sem("table_ready")
        table_out = [sem(f"table_out{k}") for k in range(5)]
        hot_ready = {s: sem(f"hot_ready_{s}") for s in ("conv1", "conv2", "rel", "net", "rat")}
        pass_done = {s: sem(f"pass_done_{s}") for s in hot_ready}
        gathering = ("conv1", "conv2", "rel", "net", "rat")
        index_in = {s: [sem(f"index_in_{s}{k}") for k in range(2)] for s in gathering}
        gathered = {s: [sem(f"gathered_{s}{k}") for k in range(2)] for s in gathering}
        rows_free = {s: [sem(f"rows_free_{s}{k}") for k in range(2)] for s in gathering}
        attr_in = {s: [sem(f"attr_in_{s}{k}") for k in range(2)] for s in ("rel", "net")}
        near_split = {n: sem(f"near_split_{n}") for n in DENSE}
        near_rows_ps = {n: sem(f"near_rows_ps_{n}") for n in DENSE}
        near_hot_ready = {n: sem(f"near_hot_ready_{n}") for n in DENSE}
        near_ready = {n: [sem(f"near_ready_{n}{b}") for b in range(F // FPB)] for n in DENSE}
        near_free = {n: [sem(f"near_free_{n}{b}") for b in range(F // FPB)] for n in DENSE}
        picked = {n: [sem(f"picked_{n}{k}") for k in range(2)] for n in DENSE}
        src_row_in = [sem(f"src_row_in{k}") for k in range(2)]
        equal_ready = sem("equal_ready")
        equal_done = sem("equal_done")
        scat_ready = [sem(f"scat_ready{k}") for k in range(2)]
        scattered = [sem(f"scattered{k}") for k in range(COPIES)]
        staged = {s: sem(f"staged_{s}") for s in ("hidden",)}
        stacked_stages = ("rel", "net")
        stack_ps_ready = {n: [sem(f"stack_ps_ready_{n}{k}") for k in range(2)] for n in stacked_stages}
        stack_ready = {n: [sem(f"stack_ready_{n}{k}") for k in range(2)] for n in stacked_stages}
        rows_ready = {n: [sem(f"rows_ready_{n}{k}") for k in range(2)] for n in stacked_stages}
        mat_split = {n: sem(f"mat_split_{n}") for n in stacked_stages}
        mat_stacked = {n: sem(f"mat_stacked_{n}") for n in stacked_stages}
        turned_ps_ready = {s: sem(f"turned_ps_ready_{s}") for s in staged}
        turned_ready = {s: sem(f"turned_ready_{s}") for s in staged}
        product_ready = {s: sem(f"product_ready_{s}") for s in staged}
        hid_ready = sem("hid_ready")
        hid_ps_ready = sem("hid_ps_ready")
        node_ready = sem("node_ready")
        rel_copied = [sem(f"rel_copied{k}") for k in range(2)]
        net_copied = [sem(f"net_copied{k}") for k in range(2)]
        rel_stored = [sem(f"rel_stored{k}") for k in range(2)]
        net_stored = sem("net_stored")
        node_done = sem("node_done")
        bn_ready = sem("bn_ready")
        bn_sum = sem("bn_sum")
        sums_ready = sem("sums_ready")
        sums_in = sem("sums_in")
        out_ready = sem("out_ready")
        stored = sem("stored")

        def chunks(eng, body):
            with eng.Fori(0, PAIRS) as i:
                body(i * 2, 0, i)
                body(i * 2 + 1, 1, i)
            body(CHUNKS - 1, 0, PAIRS)

        def chunks_after_first(eng, body):
            body(0, 0, 0, first=True)
            body(1, 1, 0, first=True)
            with eng.Fori(1, PAIRS) as i:
                body(i * 2, 0, i)
                body(i * 2 + 1, 1, i)
            body(CHUNKS - 1, 0, PAIRS)

        half = PADDED * (P + NWIN)

        def hot_place(s):
            return hot_flat[:, s * half:s * half + PADDED * P].rearrange("p (n j) -> p n j", j=PADDED)

        def hot_window(s):
            return hot_flat[:, s * half + PADDED * P:(s + 1) * half].rearrange("p (n j) -> p n j", j=PADDED)

        def parts_view(width):
            return parts[:, :, :, :].rearrange("p j s f -> p (j s f)")[:, 0:TILES * PARTS * width]

        block = ctx.enter_context(nc.Block())

        @block.sync
        def _(sp):
            sp.dma_start(span_in, dst.rearrange("(c e) -> c e", e=CE)).then_inc(in_span, 16)
            sp.dma_start(int_a.rearrange("p (c j) -> p c j", j=TILES), resident(dst)).then_inc(in_dst, 16)
            sp.wait_ge(setup, 1)
            sp.dma_start(xs[:, 0:NWIN - 1, :], by_window(x[0:(NWIN - 1) * P, :])).then_inc(in_x, 16)
            sp.dma_start(xs[0:LAST, NWIN - 1, :], x[(NWIN - 1) * P:N, :]).then_inc(in_x, 16)
            for to, of in (
                (w1[:, :], gcn_w1), (w2[:, :], gcn_w2), (b1[:, :], gcn_b1.rearrange("(k a) -> k a", a=1)),
                (b2[:, :], gcn_b2.rearrange("(a f) -> a f", a=1).broadcast_to([P, F])),
                (ws[:, :], rel_ws), (wa[:, :], rel_wa.rearrange("a (t k) -> k (a t)", k=F)),
                (comp[:, :], rel_comp.rearrange("r b -> b r")),
                (bases[:, :, :], rel_weight.rearrange("b i o -> (b i o)").rearrange("(i b o) -> b i o", b=BASES, o=F)),
                (net_rhs[:, KE, :], net_b.rearrange("(i o) -> i o", o=F)), (net_rhs[:, KE + 1, :], net_root),
                (bias[:, :], net_bias.rearrange("(a f) -> a f", a=1).broadcast_to([P, F])),
                (gamma[:, :], net_gamma.rearrange("(a f) -> a f", a=1).broadcast_to([P, F])),
                (beta[:, :], net_beta.rearrange("(a f) -> a f", a=1).broadcast_to([P, F])),
            ):
                sp.dma_start(to, of).then_inc(in_small, 16)
            for k in range(KE):
                sp.dma_start(net_rhs[:, k, :], net_w[:, k].rearrange("(i o) -> i o", o=F)).then_inc(in_small, 16)
            sp.wait_ge(setup, 2)
            sp.dma_start(int_a.rearrange("p (c j) -> p c j", j=TILES), resident(src)).then_inc(in_srctype, 16)
            sp.dma_start(int_b.rearrange("p (c j) -> p c j", j=TILES),
                         resident(edge_type_90)).then_inc(in_srctype, 16)
            sp.wait_ge(setup, 3)
            sp.dma_start(meta_dram, meta[:, :]).then_inc(meta_out, 16)
            sp.dma_start(base_dram.rearrange("(c a) -> c a", a=1), base_f[:, :]).then_inc(meta_out, 16)
            sp.wait_ge(meta_out, 32)
            sp.dma_start(meta_row[:, :], meta_dram.rearrange("c k -> (c k)").rearrange("(a n) -> a n", a=1))\
                .then_inc(meta_in, 16)
            sp.dma_start(base_all[:, :], base_dram.rearrange("(a c) -> a c", a=1).broadcast_to([P, CHUNKS]))\
                .then_inc(meta_in, 16)
            sp.wait_ge(setup, 4)
            sp.dma_start(resident(rel_index), int_b.rearrange("p (c j) -> p c j", j=TILES))\
                .then_inc(relidx_out, 16)
            sp.wait_ge(setup, 5)
            sp.dma_start(w_rel_flat.rearrange("(i r o) -> r i o", r=RELS, o=F),
                         w_rel_sb[:, :].rearrange("r (i o) -> r i o", o=F)).then_inc(w_rel_out, 16)
            sp.wait_ge(w_rel_out, 16)
            sp.dma_start(rel_rhs[:, :, 0:F], w_rel_flat.rearrange("(r i o) -> i r o", i=F, o=F)).then_inc(w_rel_in, 16)
            def stack(name, parts_of, width, to, low):
                sp.wait_ge(mat_split[name], 1)
                for q, part in enumerate(MATE_ORDER):
                    sp.dma_start(to[q * F:q * F + F, :], parts_of[:, part, :]).then_inc(mat_stacked[name], 16)
                sp.dma_start(low[LOW:LOW + F, :], parts_of[:, 2, :]).then_inc(mat_stacked[name], 16)
            stack("rel", mat_parts, RELS * RW, rel_stack, rel_low)
            stack("net", net_parts, NODEW, net_stack, net_low)
            sp.wait_ge(zeroed, 1)
            for k in range(COPIES):
                sp.dma_start(by_window(sums[k][0:(NWIN - 1) * P, :]), acc[:, 0:NWIN - 1, 0:F]).then_inc(zeroed, 16)
                sp.dma_start(sums[k][(NWIN - 1) * P:N, :], acc[0:LAST, NWIN - 1, 0:F]).then_inc(zeroed, 16)
                sp.dma_start(sums[k][N:N + P, :], acc[:, 0, 0:F]).then_inc(zeroed, 16)
            sp.wait_ge(zeroed, 1 + 48 * COPIES)
            sp.sem_inc(zeroed, 1)

            def table(k, to):
                sp.wait_ge(table_ready, k + 1)
                sp.dma_start(by_window(to), g[:, :, :]).then_inc(table_out[k], 16)

            def feed(name, index_of, attr_of=None, width=F):
                def body(c, s, use):
                    sp.wait_ge(rows_free[name][s], use + 1)
                    sp.dma_start(index[s][:, :], by_chunk(index_of)[bass.ds(c, 1), :, :]
                                 .rearrange("a p j -> (a p) j")).then_inc(index_in[name][s], 16)
                    if attr_of is not None:
                        sp.dma_start(attr[s][:, :, 0:width], attr_of.rearrange("(c p j) k -> c p j k", p=P, j=TILES)
                                     [bass.ds(c, 1), :, :, :].rearrange("a p j k -> (a p) j k"))\
                            .then_inc(attr_in[name][s], 16)
                chunks(sp, body)

            table(0, tab1)
            feed("conv1", src)
            table(1, tab2)
            feed("conv2", src)

            with sp.Fori(0, NW // 2) as i:
                for s in range(2):
                    sp.wait_ge(rel_copied[s], i * 2 + 3)
                    sp.dma_start(tab_rel.rearrange("(n r) f -> n (r f)", r=RELS)[bass.ds((i * 2 + s) * P, P), :],
                                 rel_out[s]).then_inc(rel_stored[s], 16)
            for s in range(2):
                sp.wait_ge(rel_stored[s], 16 * NW // 2 + 16)
            sp.wait_ge(relidx_out, 16)
            sp.sem_inc(table_out[2], 16)
            feed("rel", rel_index, edge_attr_16)

            for k in range(2):
                for s in range(2):
                    sp.wait_ge(net_copied[s], 1 + (k + 1) * TILES)
                    sp.dma_start(by_window(tab_net)[:, 2 * TILES * k + s:2 * TILES * (k + 1):2, :], rows[s][:, :, :])\
                        .then_inc(net_stored, 16)
                sp.wait_ge(net_stored, 32 * (k + 1))
            sp.sem_inc(table_out[3], 16)
            feed("net", src, edge_attr_4, KE)

            sp.wait_ge(table_ready, 3)
            sp.dma_start(by_window(tab3), g[:, :, :]).then_inc(table_out[4], 16)

            def feed_rational(c, s, use):
                sp.wait_ge(rows_free["rat"][s], use + 1)
                sp.dma_start(index[s][:, :], by_chunk(src)[bass.ds(c, 1), :, :]
                             .rearrange("a p j -> (a p) j")).then_inc(index_in["rat"][s], 16)
                sp.dma_start(weight[s][:, :], by_chunk(edge_weight)[bass.ds(c, 1), :, :]
                             .rearrange("a p j -> (a p) j")).then_inc(weight_in[s], 16)
                sp.dma_start(src_row[s][:, :], src.rearrange("(c e) -> c e", e=CE)[bass.ds(c, 1), :]
                             .broadcast_to([P, CE])).then_inc(src_row_in[s], 16)
                sp.wait_ge(dst_row_free, c + 1)
                sp.dma_start(dst_row[:, :], dst.rearrange("(c e) -> c e", e=CE)[bass.ds(c, 1), :]
                             .broadcast_to([P, CE])).then_inc(dst_row_in, 16)
            chunks(sp, feed_rational)

            sp.wait_ge(sums_ready, 1)
            for k in range(COPIES):
                sp.wait_ge(scattered[k], 16 * CHUNKS * TILES // COPIES)
            loads = (acc[:, 0:NW, 0:F], acc[:, 0:NW, F:2 * F], tmp[:, :, :], h[:, :, :], g[:, :, :])
            for k in range(COPIES):
                sp.dma_start(loads[k][:, 0:NWIN - 1, :], by_window(sums[k][0:(NWIN - 1) * P, :])).then_inc(sums_in, 16)
                sp.dma_start(loads[k][0:LAST, NWIN - 1, :], sums[k][(NWIN - 1) * P:N, :]).then_inc(sums_in, 16)
            sp.wait_ge(out_ready, 1)
            sp.dma_start(by_window(out[0:(NWIN - 1) * P, :]), xs[:, 0:NWIN - 1, :]).then_inc(stored, 16)
            sp.dma_start(out[(NWIN - 1) * P:N, :], xs[0:LAST, NWIN - 1, :]).then_inc(stored, 16)
            sp.wait_ge(stored, 32)

        @block.gpsimd
        def _(pool):
            pool.memset(before[:, :], 1.0)
            pool.memset(earlier[:, :], 1.0)
            pool.memset(identity[:, :], 0.0)
            pool.memset(ones_f[:, :], 1.0)
            pool.memset(ones_b[:, :], 1.0)
            pool.iota(iota_span[:, :], pattern=[[1, SPAN]], base=0, channel_multiplier=0,
                      allow_small_or_imprecise_dtypes=True)
            pool.iota(counting, pattern=[[1, P], [0, PADDED]], base=0, channel_multiplier=0,
                      allow_small_or_imprecise_dtypes=True)
            pool.iota(spare[:, :], pattern=[[0, 1]], base=N, channel_multiplier=1,
                      allow_small_or_imprecise_dtypes=True)
            pool.iota(node_ids[:, :], pattern=[[P, WIN]], base=0, channel_multiplier=1,
                      allow_small_or_imprecise_dtypes=True)
            pool.iota(valid[:, :], pattern=[[P, NW]], base=0, channel_multiplier=1,
                      allow_small_or_imprecise_dtypes=True)
            pool.drain()
            pool.affine_select(out=before[:, :], in_=before[:, :], compare_op=ALU.is_gt, fill=0.0, base=0,
                               pattern=[[1, P]], channel_multiplier=-1)
            pool.affine_select(out=earlier[:, :], in_=earlier[:, :], compare_op=ALU.is_gt, fill=0.0, base=0,
                               pattern=[[-1, P]], channel_multiplier=1)
            pool.affine_select(out=identity[:, :], in_=identity[:, :], compare_op=ALU.not_equal, fill=1.0, base=0,
                               pattern=[[-1, P]], channel_multiplier=1)
            pool.memset(identity_b[:, :], 0.0)
            pool.drain()
            pool.affine_select(out=identity_b[:, :], in_=identity_b[:, :], compare_op=ALU.not_equal, fill=1.0, base=0,
                               pattern=[[-1, P]], channel_multiplier=1)
            pool.drain().then_inc(consts, 1)

            def alone():
                pool.sem_inc(pool_turns, 1)

            def gather(name, table, width, number):
                pool.wait_ge(table_out[number], 16)

                def body(c, s, use):
                    pool.wait_ge(index_in[name][s], use * 16 + 16)
                    pool.wait_ge(rows_free[name][s], use + 1)
                    alone()
                    for j in range(TILES - DENSE.get(name, 0)):
                        pool.indirect_dma_start(
                            out=rows[s][:, j, 0:width], out_offset=None, in_=table,
                            in_offset=bass.IndirectOffsetOnAxis(ap=index[s][:, j:j + 1], axis=0),
                        ).then_inc(gathered[name][s], 16)
                chunks(pool, body)

            gather("conv1", tab1, F, 0)
            gather("conv2", tab2, F, 1)
            gather("rel", tab_rel, RW, 2)
            gather("net", tab_net, NETW, 3)

            pool.wait_ge(table_out[4], 16)
            pool.wait_ge(zeroed, 2 + 48 * COPIES)

            def gather_sources(s, use):
                pool.wait_ge(index_in["rat"][s], use * 16 + 16)
                pool.wait_ge(rows_free["rat"][s], use + 1)
                alone()
                for j in range(TILES - DENSE["rat"]):
                    pool.indirect_dma_start(
                        out=rows[s][:, j, 0:F], out_offset=None, in_=tab3,
                        in_offset=bass.IndirectOffsetOnAxis(ap=index[s][:, j:j + 1], axis=0),
                    ).then_inc(gathered["rat"][s], 16)

            def scatter(c, s, use, first=False):
                pool.wait_ge(scat_ready[s], use + 1)
                for j in range(TILES):
                    k = j % COPIES
                    if not (first and j < COPIES):
                        pool.wait_ge(scattered[k], c * (16 * TILES // COPIES) + 16 * (j // COPIES))
                    alone()
                    pool.indirect_dma_start(
                        out=sums[k], out_offset=bass.IndirectOffsetOnAxis(ap=scat_index[s][:, j:j + 1], axis=0),
                        in_=scat[s][:, j, :], in_offset=None, compute_op=ALU.add,
                        bounds_check=N + P - 1,
                    ).then_inc(scattered[k], 16)

            gather_sources(0, 0)
            gather_sources(1, 0)
            scatter(0, 0, 0, first=True)
            gather_sources(0, 1)
            scatter(1, 1, 0)
            with pool.Fori(1, PAIRS) as i:
                gather_sources(1, i)
                scatter(i * 2, 0, i)
                gather_sources(0, i + 1)
                scatter(i * 2 + 1, 1, i)
            scatter(CHUNKS - 1, 0, PAIRS)

        @block.scalar
        def _(act):
            def root(k):
                act.wait_ge(var_ready, k)
                act.activation(row_b[:, :], row_a[:, :], ACT.Sqrt)
                act.drain().then_inc(root_done, 1)

            def turn(name, i):
                of = g if name == "hidden" else h
                act.activation(stage[:, :, :], of[:, bass.ds(i * GROUP, GROUP), :], ACT.Copy)
                act.drain().then_inc(staged[name], 1)
                act.wait_ge(turned_ps_ready[name], i + 1)
                act.activation(turned[:, :, :].rearrange("k w r -> k (w r)"), turn_ps[0:F, :], ACT.Copy)
                act.drain().then_inc(turned_ready[name], 1)

            def pick(name):
                dense = DENSE[name]
                for b in range(F // FPB):
                    act.sem_inc(near_free[name][b], 1)

                def body(c, s, use):
                    act.wait_ge(rows_free[name][s], use + 1)
                    for d in range(dense):
                        for b in range(F // FPB):
                            act.wait_ge(near_ready[name][b], c * dense + (d + 1))
                            for f in range(FPB):
                                act.activation(unused[:, f, :], near_banks[name][b][:, f * NWIN:(f + 1) * NWIN],
                                               ACT.Relu, accum_out=rows[s][:, TILES - dense + d,
                                                                           b * FPB + f:b * FPB + f + 1])
                            act.drain().then_inc(near_free[name][b], 1)
                    act.drain().then_inc(picked[name][s], 1)
                chunks(act, body)

            root(1)
            root(2)
            pick("conv1")
            act.wait_ge(node_ready, 1)
            act.wait_ge(in_small, 16 * (13 + KE))
            with act.Fori(0, NGRP) as i:
                turn("hidden", i)
                act.wait_ge(hid_ps_ready, i + 1)
                act.activation(hid[:, :], big_ps[0][0:HID, 0, :], ACT.Relu, bias=b1[:, 0:1])
                act.drain().then_inc(hid_ready, 1)
                act.wait_ge(product_ready["hidden"], i + 1)
                act.activation(tmp[:, bass.ds(i * GROUP, GROUP), :],
                               big_ps[1][:, 0, 0:GROUP * F].rearrange("p (w f) -> p w f", f=F), ACT.Copy)
                act.drain()
            act.drain().then_inc(node_done, 1)
            root(3)
            act.wait_ge(node_ready, 2)
            for s in range(2):
                act.sem_inc(rel_stored[s], 16)

            def take_turned(name, s, i):
                act.wait_ge(stack_ps_ready[name][s], i + 1)
                act.activation(turned_b[s][:, :], stack_ps[s], ACT.Copy)
                act.drain().then_inc(stack_ready[name][s], 1)
            take_turned("rel", 0, 0)
            take_turned("rel", 1, 0)

            def empty(i, more=True):
                for s in range(2):
                    act.wait_ge(rows_ready["rel"][s], i + 1)
                    act.wait_ge(rel_stored[s], i * 16 + 16)
                    for b in range(RBANKS - 1 - s):
                        act.activation(rel_out[s][:, b * RPB * RW:(b + 1) * RPB * RW], big_ps[s][:, b, 0:RPB * RW],
                                       ACT.Copy)
                    act.drain().then_inc(rel_copied[s], 1)
                    if more:
                        take_turned("rel", s, i + 1)
            with act.Fori(0, NW // 2 - 1) as i:
                empty(i)
            empty(NW // 2 - 1, more=False)
            root(4)
            act.wait_ge(node_ready, 3)
            take_turned("net", 0, 0)
            take_turned("net", 1, 0)
            with act.Fori(0, NW // 2 - 1) as i:
                for s in range(2):
                    act.wait_ge(rows_ready["net"][s], i + 1)
                    take_turned("net", s, i + 1)
            act.wait_ge(bn_ready, 3)
            act.activation(scale[:, :], col_sum[:, :], ACT.Sqrt)
            act.drain().then_inc(root_done, 1)
            root(5)
            pick("rat")

        @block.tensor
        def _(pe):
            pe.wait_ge(consts, 1)
            pe.wait_ge(setup_pe, 1)
            pe.matmul(turn_ps[0:CHUNKS, 0:1], before[0:CHUNKS, 0:CHUNKS], passes_f[:, :], start=True, stop=True)
            pe.drain().then_inc(setup_pe, 1)
            pe.wait_ge(in_small, 16 * (13 + KE))
            pe.wait_ge(setup_pe, 3)
            pe.matmul(big_ps[0][0:RELS, 0, 0:F * F], comp[:, :], bases[:, :, :].rearrange("b i o -> b (i o)"),
                      start=True, stop=True)
            for t in range(3):
                pe.matmul(big_ps[0][:, 1, t * F:t * F + F], wa_wide[:, t, :], ws[:, :], start=(t == 0), stop=(t == 2),
                          skip_group_check=True)
            pe.matmul(big_ps[0][0:F, 2, 0:1], ws[:, :], wa[:, 0:1], start=True, stop=True)
            pe.drain().then_inc(setup_pe, 1)
            pe.wait_ge(meta_in, 32)

            def near_rows(name, c):
                dense = DENSE[name]
                pe.wait_ge(near_split[name], c + 1)
                rounds = (dense + 1) // 2
                for d in range(0, dense, 2):
                    if d:
                        pe.wait_ge(near_hot_ready[name], c * rounds + d // 2)
                    tiles = min(2, dense - d)
                    for e in range(tiles):
                        for q in range(2):
                            at = (2 * e + q) * P
                            pe.matmul(turn_ps[:, at:at + P], near_b[:, q, d + e:d + e + 1].broadcast_to([P, P]),
                                      identity_b[:, :], start=(e == 0 and q == 0), stop=(e == tiles - 1 and q == 1),
                                      skip_group_check=True)
                    pe.drain().then_inc(near_rows_ps[name], 1)
                pe.wait_ge(near_hot_ready[name], (c + 1) * rounds)

            def near(name, c, tiles):
                for d in tiles:
                    for b in range(F // FPB):
                        pe.wait_ge(near_free[name][b], c * DENSE[name] + (d + 1))
                        out = near_banks[name][b][:, 0:FPB * NWIN]
                        for q in range(PARTS):
                            pe.matmul(out, near_hot[:, d, 0, :],
                                      near_table[name][:, q * F + b * FPB:q * F + (b + 1) * FPB, 0:NWIN],
                                      start=(q == 0), stop=False)
                        pe.matmul(out, near_hot[:, d, 1, :], near_mask[:, :, :], start=False, stop=True)
                        pe.drain().then_inc(near_ready[name][b], 1)

            def sum_windows(name, width):
                def body(c, more):
                    if more:
                        near_rows(name, c + 1)
                        near(name, c + 1, range(2))
                    passes = pe.value_load(meta_row[0:1, bass.ds(c * 4 + 1, 1)], min_val=1, max_val=NWIN)
                    first = pe.value_load(meta_row[0:1, bass.ds(c * 4 + 2, 1)], min_val=0, max_val=NWIN * CHUNKS)
                    with pe.Fori(0, passes) as k:
                        pe.wait_ge(hot_ready[name], first + k + 1)
                        for j in range(TILES):
                            for w in range(WIN):
                                rhs = parts_view(width)[:, j * PARTS * width:(j + 1) * PARTS * width]
                                n = rhs.shape[1]
                                pe.matmul(pass_ps[:, w * n:w * n + n], hot[:, j, w * P:w * P + P], rhs,
                                          start=(j == 0 and w == 0), stop=(j == TILES - 1),
                                          skip_group_check=True)
                        pe.drain().then_inc(pass_done[name], 1)
                    if more:
                        near(name, c + 1, range(2, DENSE[name]))
                if name in DENSE:
                    pe.wait_ge(near_table_ready[name], 1)
                    near_rows(name, 0)
                    near(name, 0, range(DENSE[name]))
                    with pe.Fori(0, CHUNKS - 1) as c:
                        body(c, True)
                    body(CHUNKS - 1, False)
                else:
                    with pe.Fori(0, CHUNKS) as c:
                        body(c, False)

            def turn(name, i):
                pe.wait_ge(staged[name], i + 1)
                for w in range(GROUP):
                    pe.transpose(turn_ps[0:F, w * P:w * P + P], stage[:, w, :], identity[:, :])
                pe.drain().then_inc(turned_ps_ready[name], 1)
                pe.wait_ge(turned_ready[name], i + 1)

            def degrees(c, s, use, first=False):
                pe.wait_ge(place_ready[s], use + 1)
                for j in range(TILES):
                    pe.matmul(pass_ps[:, 0:NWIN], hot_place(s)[:, :, j], hot_window(s)[:, :, j],
                              start=(first and s == 0 and j == 0), stop=True, skip_group_check=True)
                pe.drain().then_inc(degree_done[s], 1)
            chunks_after_first(pe, degrees)
            sum_windows("conv1", F)
            with pe.Fori(0, NGRP) as i:
                turn("hidden", i)
                pe.matmul(big_ps[0][0:HID, 0, :], w1[:, :], turned[:, :, :].rearrange("k w r -> k (w r)"),
                          start=True, stop=True)
                pe.drain().then_inc(hid_ps_ready, 1)
                pe.wait_ge(hid_ready, i + 1)
                for w in range(GROUP):
                    pe.matmul(big_ps[1][:, 0, w * F:w * F + F], hid[:, w * P:w * P + P], w2[:, :],
                              start=(w == 0), stop=(w == GROUP - 1), skip_group_check=True)
                pe.drain().then_inc(product_ready["hidden"], 1)
            sum_windows("conv2", F)
            def turn_stack(name, s, i):
                pe.transpose(stack_ps[s], h_stack[:, bass.ds(i * 2 + s, 1), :, :].rearrange("p a q f -> p (a q f)"),
                             identity_b[:, :])
                pe.drain().then_inc(stack_ps_ready[name][s], 1)

            def product(name, copied, stack, low, banks, width):
                def pair(i, more=True):
                    for s in range(2):
                        pe.wait_ge(stack_ready[name][s], i + 1)
                        pe.wait_ge(copied[s], i * (2 if name == "rel" else 1) + 1)
                        for b in range(banks):
                            pe.matmul(big_ps[s][:, b, 0:width], turned_b[s][:, :],
                                      stack[:, b * width:(b + 1) * width], start=True, stop=False)
                        for b in range(banks):
                            pe.matmul(big_ps[s][:, b, 0:width], turned_b[s][LOW:LOW + F, :],
                                      low[LOW:LOW + F, b * width:(b + 1) * width], start=False, stop=True)
                        pe.drain().then_inc(rows_ready[name][s], 1)
                        if more:
                            turn_stack(name, s, i + 1)
                pe.wait_ge(mat_stacked[name], 16 * (len(MATE_ORDER) + 1))
                turn_stack(name, 0, 0)
                turn_stack(name, 1, 0)
                with pe.Fori(0, NW // 2 - 1) as i:
                    pair(i)
                pair(NW // 2 - 1, more=False)

            pe.wait_ge(node_ready, 2)
            product("rel", rel_copied, rel_stack, rel_low, RBANKS, RPB * RW)
            sum_windows("rel", 2 * F)
            pe.wait_ge(node_ready, 3)
            product("net", net_copied, net_stack, net_low, 1, NODEW)
            sum_windows("net", F)
            for k in range(2):
                pe.wait_ge(bn_ready, k + 1)
                pe.matmul(turn_ps[:, 0:F], ones_f[:, :], col_sum[:, :], start=True, stop=True)
                pe.drain().then_inc(bn_sum, 1)
            width = PARTS * F
            per = BANK // width
            def rational(c, more):
                if more:
                    near_rows("rat", c + 1)
                    near("rat", c + 1, range(2))
                low = pe.value_load(meta_row[0:1, bass.ds(c * 4, 1)], min_val=0, max_val=NWIN - 1)
                passes = pe.value_load(meta_row[0:1, bass.ds(c * 4 + 1, 1)], min_val=1, max_val=NWIN)
                before_c = pe.value_load(meta_row[0:1, bass.ds(c * 4 + 2, 1)], min_val=0, max_val=NWIN * CHUNKS)
                with pe.Fori(0, passes) as k:
                    place = nc.s_assert_within(low + k * WIN, 0, NW, skip_runtime_bounds_check_because=
                                               "a pass begins at a window that the chunk touches")
                    pe.wait_ge(hot_ready["rat"], before_c + k + 1)
                    for j in range(TILES):
                        b, a = j // per, j % per
                        for w in range(WIN):
                            pe.matmul(big_ps[1][:, b, a * width:(a + 1) * width],
                                      hot_t[:, w, j:CE:TILES],
                                      near_table["rat"][:, :, bass.ds(place + w, 1)].rearrange("p f a -> p (f a)"),
                                      start=(a == 0 and w == 0), stop=(w == WIN - 1), skip_group_check=True)
                    pe.drain().then_inc(pass_done["rat"], 1)
                if more:
                    near("rat", c + 1, range(2, 5))
                pe.wait_ge(equal_ready, c + 1)
                for j in range(TILES):
                    b, a = j // per, j % per
                    pe.matmul(big_ps[1][:, b, a * width:(a + 1) * width], equal[:, j, :],
                              parts_view(F)[:, j * width:(j + 1) * width],
                              start=(a == 0), stop=(a == per - 1 or j == TILES - 1), skip_group_check=True)
                pe.drain().then_inc(equal_done, 1)
                if more:
                    near("rat", c + 1, range(5, DENSE["rat"]))
            pe.wait_ge(near_table_ready["rat"], 1)
            near_rows("rat", 0)
            near("rat", 0, range(DENSE["rat"]))
            with pe.Fori(0, CHUNKS - 1) as c:
                rational(c, True)
            rational(CHUNKS - 1, False)

        @block.vector
        def _(dve):
            dve.memset(xs[:, NWIN - 1:NW, :], 0.0)
            dve.drain().then_inc(setup, 1)
            dve.memset(acc[:, :, :], 0.0)
            dve.drain().then_inc(zeroed, 1)
            dve.wait_ge(in_dst, 16)
            dve.tensor_copy(dst_f[:, :], int_a)
            dve.drain().then_inc(setup, 1)
            dve.wait_ge(in_span, 16)
            dve.tensor_reduce(span[:, 0:1], span_in, AX.X, ALU.min)
            dve.tensor_reduce(span[:, 1:2], span_in, AX.X, ALU.max)
            dve.memset(meta[:, :], 0)
            dve.drain()
            shift = P.bit_length() - 1
            dve.tensor_scalar(span[:, 2:4], span[:, 0:2], shift, None, ALU.logical_shift_right)
            dve.drain()
            dve.tensor_copy(meta[:, 0:1], span[:, 2:3])
            dve.tensor_scalar(base_f[:, :], span[:, 2:3], float(P), None, ALU.mult)
            dve.tensor_tensor(span[:, 0:1], span[:, 3:4], span[:, 2:3], ALU.subtract)
            dve.drain()
            dve.tensor_scalar(span[:, 1:2], span[:, 0:1], float(WIN), None, ALU.add)
            dve.drain()
            dve.tensor_scalar(meta[:, 1:2], span[:, 1:2], WIN.bit_length() - 1, None, ALU.logical_shift_right)
            dve.drain()
            dve.tensor_copy(passes_f[:, :], meta[:, 1:2])
            dve.drain().then_inc(setup_pe, 1)
            dve.wait_ge(setup_pe, 2)
            dve.tensor_copy(meta[:, 2:3], turn_ps[0:CHUNKS, 0:1])
            dve.drain().then_inc(setup, 1)
            dve.wait_ge(in_srctype, 32)
            dve.scalar_tensor_tensor(out=int_b, in0=int_a, scalar=float(RELS), in1=int_b,
                                     op0=ALU.mult, op1=ALU.add)
            dve.drain().then_inc(setup, 1)
            dve.memset(dst_window[:, :, TILES:PADDED], NOWHERE)
            dve.memset(dst_place[:, :, TILES:PADDED], NOWHERE)
            dve.tensor_copy(int_a, dst_f[:, :])
            dve.drain()
            dve.tensor_scalar(int_c, int_a, shift, None, ALU.logical_shift_right)
            dve.drain()
            dve.tensor_scalar(int_a, int_a, P - 1, None, ALU.bitwise_and)
            dve.tensor_copy(dst_window[:, :, 0:TILES], int_c.rearrange("p (c j) -> p c j", j=TILES))
            dve.drain()
            dve.tensor_copy(dst_place[:, :, 0:TILES], int_a.rearrange("p (c j) -> p c j", j=TILES))
            dve.drain()
            dve.wait_ge(in_small, 16 * (13 + KE))
            dve.tensor_copy(wa_wide[:, :, :], wa[:, :].unsqueeze(2).broadcast_to([F, 3, P]))
            dve.drain().then_inc(setup_pe, 1)
            dve.wait_ge(setup_pe, 4)
            dve.tensor_copy(w_rel_sb[:, :], big_ps[0][0:RELS, 0, 0:F * F])
            dve.drain().then_inc(setup, 1)
            dve.tensor_copy(a_rows[:, :, :].rearrange("p t f -> p (t f)"), big_ps[0][:, 1, 0:3 * F])
            dve.tensor_copy(a_col[:, :], big_ps[0][0:F, 2, 0:1])
            dve.wait_ge(w_rel_in, 16)
            dve.drain()
            dve.tensor_copy(rel_rhs[:, :, F:RW], a_col[:, :].unsqueeze(2).broadcast_to([F, RELS, 1]))
            dve.drain()

            def split_matrix(name, flat, to):
                dve.tensor_copy(to[:, 0, :], flat)
                dve.drain()
                dve.tensor_tensor(flat, flat, to[:, 0, :], ALU.subtract)
                dve.drain()
                dve.tensor_copy(to[:, 1, :], flat)
                dve.drain()
                dve.tensor_tensor(to[:, 2, :], flat, to[:, 1, :], ALU.subtract)
                dve.drain().then_inc(mat_split[name], 1)
            split_matrix("rel", rel_rhs[:, :, :].rearrange("i r o -> i (r o)"), mat_parts)
            dve.wait_ge(mat_stacked["rel"], 16 * (len(MATE_ORDER) + 1))
            split_matrix("net", net_rhs[:, :, :].rearrange("i k o -> i (k o)"), net_parts)
            dve.wait_ge(consts, 1)
            dve.tensor_scalar(valid[:, :], valid[:, :], float(N), None, ALU.is_lt)
            dve.drain()

            def wide(v):
                return v.unsqueeze(2).broadcast_to([P, NW, F])

            def per_feature(v):
                return v.unsqueeze(1).broadcast_to([P, NW, F])

            def norm(k):
                dve.tensor_reduce(row_a[:, :], xs[:, :, :], AX.X, ALU.add)
                dve.drain()
                dve.tensor_scalar(row_a[:, :], row_a[:, :], 1.0 / F, None, ALU.mult)
                dve.drain()
                dve.tensor_tensor(h[:, :, :], xs[:, :, :], wide(row_a[:, :]), ALU.subtract)
                dve.drain()
                dve.tensor_tensor(tmp[:, :, :], h[:, :, :], h[:, :, :], ALU.mult)
                dve.drain()
                dve.tensor_reduce(row_a[:, :], tmp[:, :, :], AX.X, ALU.add)
                dve.drain()
                dve.tensor_scalar(row_a[:, :], row_a[:, :], 1.0 / F, EPS, ALU.mult, ALU.add)
                dve.drain().then_inc(var_ready, 1)
                dve.wait_ge(root_done, k)
                dve.reciprocal(row_a[:, :], row_b[:, :])
                dve.drain()
                dve.tensor_tensor(h[:, :, :], h[:, :, :], wide(row_a[:, :]), ALU.mult)
                dve.drain()
                dve.tensor_scalar(h[:, :, :], h[:, :, :], 0.0, None, ALU.max)
                dve.drain()

            def split(of, width):
                v = parts_view(width).rearrange("p (j s f) -> p j s f", j=TILES, s=PARTS)
                r = rest[:, :, 0:width]
                dve.tensor_copy(v[:, :, 0, :], of)
                dve.drain()
                dve.tensor_tensor(r, of, v[:, :, 0, :], ALU.subtract)
                dve.drain()
                dve.tensor_copy(v[:, :, 1, :], r)
                dve.drain()
                dve.tensor_tensor(v[:, :, 2, :], r, v[:, :, 1, :], ALU.subtract)
                dve.drain()

            def passes_of(name, c, width):
                low = dve.value_load(meta_row[0:1, bass.ds(c * 4, 1)], min_val=0, max_val=NWIN - 1)
                passes = dve.value_load(meta_row[0:1, bass.ds(c * 4 + 1, 1)], min_val=1, max_val=NWIN)
                first = dve.value_load(meta_row[0:1, bass.ds(c * 4 + 2, 1)], min_val=0, max_val=NWIN * CHUNKS)
                dve.tensor_tensor(dst_rel[:, :], dst_f[:, bass.ds(c * TILES, TILES)],
                                  base_all[:, bass.ds(c, 1)].broadcast_to([P, TILES]), ALU.subtract)
                dve.drain()
                with dve.Fori(0, passes) as k:
                    for j in range(TILES):
                        dve.tensor_scalar(hot[:, j, :], iota_span[:, :], dst_rel[:, j:j + 1], None, ALU.is_equal)
                    dve.drain().then_inc(hot_ready[name], 1)
                    dve.tensor_scalar(dst_rel[:, :], dst_rel[:, :], -float(SPAN), None, ALU.add)
                    dve.wait_ge(pass_done[name], first + k + 1)
                    place = nc.s_assert_within(low + k * WIN, 0, NW, skip_runtime_bounds_check_because=
                                               "a pass begins at a window that the chunk touches")
                    dve.tensor_reduce(part_sum[:, :, 0:width],
                                      pass_ps[:, 0:WIN * PARTS * width]
                                      .rearrange("p (w s f) -> p w f s", w=WIN, s=PARTS), AX.X, ALU.add)
                    dve.drain()
                    at = acc[:, bass.ds(place, WIN), 0:width]
                    dve.tensor_tensor(at, at, part_sum[:, :, 0:width], ALU.add)
                    dve.drain()

            def clear_sums(width):
                dve.memset(acc[:, :, 0:width], 0.0)
                dve.drain()

            def split_table(name, of):
                t = near_table[name]
                dve.memset(t[:, :, NW:AW], 0.0)
                hi, mid, lo = (t[:, q * F:(q + 1) * F, 0:NW].rearrange("p f w -> p w f") for q in range(PARTS))
                dve.tensor_copy(hi, of)
                dve.drain()
                dve.tensor_tensor(tmp[:, :, :], of, hi, ALU.subtract)
                dve.drain()
                dve.tensor_copy(mid, tmp[:, :, :])
                dve.drain()
                dve.tensor_tensor(lo, tmp[:, :, :], mid, ALU.subtract)
                dve.drain().then_inc(near_table_ready[name], 1)

            def near_sources(name, c, s, use):
                dense = DENSE[name]
                last = index[s][:, TILES - dense:TILES]
                dve.wait_ge(index_in[name][s], use * 16 + 16)
                dve.tensor_scalar(near_int[:, 0, 0:dense], last, P - 1, None, ALU.bitwise_and)
                dve.tensor_scalar(near_int[:, 1, 0:dense], last, shift, None, ALU.logical_shift_right)
                dve.drain()
                dve.tensor_copy(near_b[:, :, 0:dense], near_int[:, :, 0:dense])
                dve.drain().then_inc(near_split[name], 1)
                for d in range(0, dense, 2):
                    tiles = min(2, dense - d)
                    dve.wait_ge(near_rows_ps[name], c * ((dense + 1) // 2) + (d // 2 + 1))
                    dve.tensor_scalar(near_hot[:, d:d + tiles, :, :].rearrange("p d q e -> p (d q e)"),
                                      turn_ps[:, 0:2 * tiles * P],
                                      node_ids[:, 0:1], None, ALU.is_equal)
                    dve.drain().then_inc(near_hot_ready[name], 1)

            def near_used(name, c):
                dve.wait_ge(near_ready[name][F // FPB - 1], c * DENSE[name] + DENSE[name])

            def chunks_and_next(body):
                with dve.Fori(0, PAIRS) as i:
                    body(i * 2, 0, i, i)
                    body(i * 2 + 1, 1, i, i + 1)
                body(CHUNKS - 1, 0, PAIRS, None)

            def edges(name, width, message):
                for s in range(2):
                    dve.sem_inc(rows_free[name][s], 1)
                if name in DENSE:
                    near_sources(name, 0, 0, 0)

                def body(c, s, use, next_use=None):
                    if name in DENSE:
                        if next_use is not None:
                            near_used(name, c)
                            near_sources(name, c + 1, 1 - s, next_use)
                        dve.wait_ge(picked[name][s], use + 1)
                    dve.wait_ge(gathered[name][s], use * land(name) + land(name))
                    message(s, use)
                    dve.drain().then_inc(rows_free[name][s], 1)
                    passes_of(name, c, width)
                if name in DENSE:
                    chunks_and_next(body)
                else:
                    chunks(dve, body)

            def plain(s, use):
                split(rows[s][:, :, 0:F], F)

            dve.wait_ge(in_x, 32)
            norm(1)
            dve.wait_ge(meta_in, 32)
            dve.wait_ge(relidx_out, 16)

            def places(c, s, use, first=False):
                if not first:
                    dve.wait_ge(degree_done[s], use)
                for to, of, n in ((hot_place(s), dst_place, P), (hot_window(s), dst_window, NWIN)):
                    dve.tensor_tensor(to, counting[:, 0:n, :], of[:, bass.ds(c, 1), :].broadcast_to([P, n, PADDED]),
                                      ALU.is_equal)
                dve.drain().then_inc(place_ready[s], 1)
            chunks_after_first(dve, places)
            dve.memset(deg[:, :], 0.0)
            for s in range(2):
                dve.wait_ge(degree_done[s], PAIRS + 1 - s)
            dve.drain()
            dve.tensor_copy(deg[:, 0:NWIN], pass_ps[:, 0:NWIN])
            dve.drain()
            dve.tensor_scalar(row_a[:, :], deg[:, :], 1.0, None, ALU.add)
            dve.drain().then_inc(var_ready, 1)
            dve.wait_ge(root_done, 2)
            dve.reciprocal(dinv[:, :], row_b[:, :])
            dve.drain()
            dve.tensor_tensor(g[:, :, :], h[:, :, :], wide(dinv[:, :]), ALU.mult)
            dve.drain().then_inc(table_ready, 1)
            dve.tensor_copy(near_mask[:, :, :], iota_span[:, 0:NWIN].unsqueeze(1).broadcast_to([P, FPB, NWIN]))
            dve.drain()
            dve.tensor_scalar(unused[:, :, :], near_mask[:, :, :], node_ids[:, 0:1], None, ALU.is_equal)
            dve.drain()
            dve.tensor_scalar(near_mask[:, :, :], unused[:, :, :], -1.0, FAR, ALU.add, ALU.mult)
            split_table("conv1", g[:, :, :])
            dve.wait_ge(zeroed, 2 + 48 * COPIES)
            edges("conv1", F, plain)
            dve.tensor_tensor(g[:, :, :], g[:, :, :], acc[:, 0:NW, 0:F], ALU.add)
            dve.drain()
            dve.tensor_tensor(g[:, :, :], g[:, :, :], wide(dinv[:, :]), ALU.mult)
            dve.drain().then_inc(node_ready, 1)
            dve.wait_ge(node_done, 1)
            dve.tensor_tensor(g[:, :, :], tmp[:, :, :], wide(dinv[:, :]), ALU.mult)
            dve.drain().then_inc(table_ready, 1)
            clear_sums(F)
            edges("conv2", F, plain)
            dve.tensor_tensor(g[:, :, :], g[:, :, :], acc[:, 0:NW, 0:F], ALU.add)
            dve.drain()
            dve.tensor_tensor(g[:, :, :], g[:, :, :], wide(dinv[:, :]), ALU.mult)
            dve.drain()
            dve.tensor_tensor(xs[:, :, :], xs[:, :, :], g[:, :, :], ALU.add)
            dve.drain()
            dve.tensor_tensor(xs[:, :, :], xs[:, :, :], per_feature(b2[:, :]), ALU.add)
            dve.drain()

            def stack_rows():
                hi, mid, lo = (PAIR_ORDER.index(q) for q in range(PARTS))
                dve.tensor_copy(h_stack[:, :, hi, :], h[:, :, :])
                dve.drain()
                dve.tensor_tensor(tmp[:, :, :], h[:, :, :], h_stack[:, :, hi, :], ALU.subtract)
                dve.drain()
                dve.tensor_copy(h_stack[:, :, mid, :], tmp[:, :, :])
                dve.drain()
                dve.tensor_tensor(h_stack[:, :, lo, :], tmp[:, :, :], h_stack[:, :, mid, :], ALU.subtract)
                dve.drain()
                for q, part in enumerate(PAIR_ORDER):
                    if q != PAIR_ORDER.index(part):
                        dve.tensor_copy(h_stack[:, :, q, :], h_stack[:, :, PAIR_ORDER.index(part), :])

            norm(3)
            for s in range(2):
                dve.sem_inc(rel_copied[s], 1)
            stack_rows()
            dve.drain().then_inc(node_ready, 1)
            with dve.Fori(0, NW // 2) as i:
                for s in range(2):
                    dve.wait_ge(rows_ready["rel"][s], i + 1)
                    dve.wait_ge(rel_stored[s], i * 16 + 16)
                    for b in range(RBANKS - 1 - s, RBANKS):
                        dve.tensor_copy(rel_out[s][:, b * RPB * RW:(b + 1) * RPB * RW], big_ps[s][:, b, 0:RPB * RW])
                    dve.drain().then_inc(rel_copied[s], 1)
            clear_sums(2 * F)

            def relational(s, use):
                dve.wait_ge(attr_in["rel"][s], use * 16 + 16)
                dve.tensor_tensor(msg[:, :, 0:F], attr[s][:, :, :],
                                  a_rows[:, 1, :].unsqueeze(1).broadcast_to([P, TILES, F]), ALU.mult)
                dve.drain()
                dve.tensor_reduce(score[:, :], msg[:, :, 0:F], AX.X, ALU.add)
                dve.drain()
                dve.tensor_tensor(score[:, :], score[:, :], rows[s][:, :, F], ALU.add)
                dve.drain()
                dve.tensor_tensor(msg[:, :, 0:F], rows[s][:, :, 0:F],
                                  score[:, :].unsqueeze(2).broadcast_to([P, TILES, F]), ALU.mult)
                dve.tensor_copy(msg[:, :, F:2 * F], rows[s][:, :, 0:F])
                dve.drain()
                split(msg[:, :, :], 2 * F)
            edges("rel", 2 * F, relational)
            dve.tensor_tensor(tmp[:, :, :], h[:, :, :], per_feature(a_rows[:, 2, :]), ALU.mult)
            dve.drain()
            dve.tensor_reduce(row_a[:, :], tmp[:, :, :], AX.X, ALU.add)
            dve.drain()
            dve.tensor_tensor(tmp[:, :, :], acc[:, 0:NW, F:2 * F], wide(row_a[:, :]), ALU.mult)
            dve.drain()
            dve.tensor_tensor(tmp[:, :, :], tmp[:, :, :], acc[:, 0:NW, 0:F], ALU.add)
            dve.drain()
            dve.tensor_tensor(xs[:, :, :], xs[:, :, :], tmp[:, :, :], ALU.add)
            dve.drain()

            norm(4)
            for s in range(2):
                dve.sem_inc(net_copied[s], 1)
            stack_rows()
            dve.drain().then_inc(node_ready, 1)
            for k in range(2):
                if k:
                    dve.wait_ge(net_stored, 32 * k)
                with dve.Fori(0, TILES) as i:
                    for s in range(2):
                        dve.wait_ge(rows_ready["net"][s], i + (k * TILES + 1))
                        dve.tensor_copy(rows[s][:, bass.ds(i, 1), :].rearrange("p a k -> p (a k)"),
                                        big_ps[s][:, 0, 0:NETW])
                        dve.tensor_copy(own[:, bass.ds(i * 2 + (2 * TILES * k + s), 1), :]
                                        .rearrange("p a k -> p (a k)"), big_ps[s][:, 0, NETW:NODEW])
                        dve.drain().then_inc(net_copied[s], 1)
            clear_sums(F)

            def network(s, use):
                dve.wait_ge(attr_in["net"][s], use * 16 + 16)
                for k in range(KE):
                    dve.tensor_tensor(work[:, :, k * F:k * F + F], rows[s][:, :, k * F:k * F + F],
                                      attr[s][:, :, k:k + 1].broadcast_to([P, TILES, F]), ALU.mult)
                dve.drain()
                dve.tensor_tensor(work[:, :, 0:2 * F], work[:, :, 0:2 * F], work[:, :, 2 * F:4 * F], ALU.add)
                dve.drain()
                dve.tensor_tensor(work[:, :, 0:F], work[:, :, 0:F], work[:, :, F:2 * F], ALU.add)
                dve.drain()
                dve.tensor_tensor(msg[:, :, 0:F], work[:, :, 0:F], rows[s][:, :, KE * F:NETW], ALU.add)
                dve.drain()
                split(msg[:, :, 0:F], F)
            edges("net", F, network)
            dve.tensor_scalar(row_a[:, :], deg[:, :], 1.0, None, ALU.max)
            dve.drain()
            dve.reciprocal(row_a[:, :], row_a[:, :])
            dve.drain()
            dve.tensor_tensor(tmp[:, :, :], acc[:, 0:NW, 0:F], wide(row_a[:, :]), ALU.mult)
            dve.drain()
            dve.tensor_tensor(tmp[:, :, :], tmp[:, :, :], own[:, :, :], ALU.add)
            dve.drain()
            dve.tensor_tensor(tmp[:, :, :], tmp[:, :, :], per_feature(bias[:, :]), ALU.add)
            dve.drain()

            def over_nodes(k):
                dve.tensor_reduce(col_sum[:, :], g[:, :, :].rearrange("p w f -> p f w"), AX.X, ALU.add)
                dve.drain().then_inc(bn_ready, 1)
                dve.wait_ge(bn_sum, k)
            dve.tensor_tensor(g[:, :, :], tmp[:, :, :], wide(valid[:, :]), ALU.mult)
            dve.drain()
            over_nodes(1)
            dve.tensor_scalar(mean[:, :], turn_ps[:, 0:F], 1.0 / N, None, ALU.mult)
            dve.drain()
            dve.tensor_tensor(tmp[:, :, :], tmp[:, :, :], per_feature(mean[:, :]), ALU.subtract)
            dve.drain()
            dve.tensor_tensor(g[:, :, :], tmp[:, :, :], wide(valid[:, :]), ALU.mult)
            dve.drain()
            dve.tensor_tensor(g[:, :, :], g[:, :, :], g[:, :, :], ALU.mult)
            dve.drain()
            over_nodes(2)
            dve.tensor_scalar(col_sum[:, :], turn_ps[:, 0:F], 1.0 / N, EPS, ALU.mult, ALU.add)
            dve.drain().then_inc(bn_ready, 1)
            dve.wait_ge(root_done, 4 + 1)
            dve.reciprocal(scale[:, :], scale[:, :])
            dve.drain()
            dve.tensor_tensor(scale[:, :], scale[:, :], gamma[:, :], ALU.mult)
            dve.drain()
            dve.tensor_tensor(tmp[:, :, :], tmp[:, :, :], per_feature(scale[:, :]), ALU.mult)
            dve.drain()
            dve.tensor_tensor(tmp[:, :, :], tmp[:, :, :], per_feature(beta[:, :]), ALU.add)
            dve.drain()
            dve.tensor_scalar(g[:, :, :], tmp[:, :, :], SLOPE, None, ALU.mult)
            dve.drain()
            dve.tensor_tensor(tmp[:, :, :], tmp[:, :, :], g[:, :, :], ALU.max)
            dve.drain()
            dve.tensor_tensor(xs[:, :, :], xs[:, :, :], tmp[:, :, :], ALU.add)
            dve.drain()

            norm(6)
            dve.tensor_copy(g[:, :, :], h[:, :, :])
            dve.drain().then_inc(table_ready, 1)
            dve.tensor_scalar(tmp[:, :, :], h[:, :, :], -1.0 / FK, 1.0, ALU.mult, ALU.add)
            dve.tensor_scalar(own[:, :, :], h[:, :, :], 1.0 / FC, -1.0, ALU.mult, ALU.add)
            dve.drain()
            dve.tensor_tensor(tmp[:, :, :], tmp[:, :, :], h[:, :, :], ALU.mult)
            dve.drain()
            dve.tensor_tensor(own[:, :, :], tmp[:, :, :], own[:, :, :], ALU.mult)
            dve.drain()
            dve.tensor_scalar(own[:, :, :], own[:, :, :], FB, None, ALU.add)
            dve.drain()
            dve.tensor_tensor(xs[:, :, :], xs[:, :, :], own[:, :, :], ALU.add)
            split_table("rat", h[:, :, :])
            for s in range(2):
                dve.sem_inc(rows_free["rat"][s], 1)
            dve.sem_inc(dst_row_free, 1)
            per = BANK // (PARTS * F)

            def tile_rows(ps, to):
                for b in range((TILES + per - 1) // per):
                    n = min(per, TILES - b * per)
                    dve.tensor_reduce(to[:, b * per:b * per + n, :], ps[:, b, 0:n * PARTS * F]
                                      .rearrange("p (a q f) -> p a f q", a=n, q=PARTS), AX.X, ALU.add)

            def targets(c):
                passes = dve.value_load(meta_row[0:1, bass.ds(c * 4 + 1, 1)], min_val=1, max_val=NWIN)
                before_c = dve.value_load(meta_row[0:1, bass.ds(c * 4 + 2, 1)], min_val=0, max_val=NWIN * CHUNKS)
                dve.wait_ge(dst_row_in, c * 16 + 16)
                dve.memset(xj[:, :, :], 0.0)
                dve.tensor_tensor(node_of[:, :], node_ids[:, :], base_all[:, bass.ds(c, 1)].broadcast_to([P, WIN]),
                                  ALU.add)
                dve.drain()
                with dve.Fori(0, passes) as k:
                    for w in range(WIN):
                        dve.tensor_scalar(hot_t[:, w, :], dst_row[:, :], node_of[:, w:w + 1], None, ALU.is_equal)
                    dve.drain().then_inc(hot_ready["rat"], 1)
                    dve.tensor_scalar(node_of[:, :], node_of[:, :], float(SPAN), None, ALU.add)
                    dve.wait_ge(pass_done["rat"], before_c + k + 1)
                    tile_rows(big_ps[1], rest[:, :, 0:F])
                    dve.drain()
                    dve.tensor_tensor(xj[:, :, :], xj[:, :, :], rest[:, :, 0:F], ALU.add)
                    dve.drain()
                dve.drain().then_inc(dst_row_free, 1)

            def rational(c, s, use, next_use, first=False):
                if next_use is not None:
                    near_used("rat", c)
                    near_sources("rat", c + 1, 1 - s, next_use)
                targets(c)
                dve.wait_ge(picked["rat"][s], use + 1)
                dve.wait_ge(gathered["rat"][s], use * land("rat") + land("rat"))
                dve.wait_ge(weight_in[s], use * 16 + 16)
                xi = rows[s][:, :, 0:F]
                den, top = work[:, :, 0:F], work[:, :, F:2 * F]
                dve.tensor_scalar(den, xi, FE, FD, ALU.mult, ALU.add)
                dve.tensor_tensor(top, xi, xj[:, :, :], ALU.mult)
                dve.drain()
                dve.scalar_tensor_tensor(out=den, in0=xj[:, :, :], scalar=FH, in1=den, op0=ALU.mult, op1=ALU.add)
                dve.tensor_tensor(top, top, weight[s][:, :].unsqueeze(2)
                                  .broadcast_to([P, TILES, F]), ALU.mult)
                dve.drain()
                dve.reciprocal(msg[:, :, 0:F], den)
                dve.drain()
                dve.tensor_tensor(msg[:, :, 0:F], msg[:, :, 0:F], top, ALU.mult)
                dve.drain()
                split(msg[:, :, 0:F], F)
                dve.wait_ge(src_row_in[s], use * 16 + 16)
                dve.tensor_tensor(equal, src_row[s][:, :].rearrange("q (p j) -> q j p", j=TILES),
                                  index[s][:, :].unsqueeze(2).broadcast_to([P, TILES, P]), ALU.is_equal)
                dve.drain().then_inc(equal_ready, 1)
                before_row = src_row[s][:, 0:CE // 2].bitcast(BF16).rearrange("p (j q) -> p j q", q=P)
                dve.tensor_tensor(before_row, equal,
                                  earlier[:, :].unsqueeze(1).broadcast_to([P, TILES, P]), ALU.mult)
                dve.drain()
                dve.tensor_reduce(seen[:, :], before_row, AX.X, ALU.add)
                dve.drain()
                dve.tensor_scalar(seen[:, :], seen[:, :], 0.5, None, ALU.is_gt)
                dve.tensor_scalar(score[:, :], index[s][:, :], -1.0, spare[:, 0:1], ALU.mult, ALU.add)
                dve.drain()
                dve.tensor_tensor(score[:, :], score[:, :], seen[:, :], ALU.mult)
                dve.drain()
                if not first:
                    for k in range(COPIES):
                        dve.wait_ge(scattered[k], (c - 1) * (16 * TILES // COPIES))
                dve.tensor_tensor(scat_index[s][:, :], score[:, :], index[s][:, :], ALU.add)
                dve.drain().then_inc(rows_free["rat"][s], 1)
                dve.wait_ge(equal_done, c + 1)
                tile_rows(big_ps[1], scat[s])
                dve.drain().then_inc(scat_ready[s], 1)
            near_sources("rat", 0, 0, 0)
            rational(0, 0, 0, 0, first=True)
            rational(1, 1, 0, 1, first=True)
            with dve.Fori(1, PAIRS) as i:
                rational(i * 2, 0, i, i)
                rational(i * 2 + 1, 1, i, i + 1)
            rational(CHUNKS - 1, 0, PAIRS, None)
            dve.drain().then_inc(sums_ready, 1)
            dve.wait_ge(sums_in, 32 * COPIES)
            for v in (acc[:, 0:NW, 0:F], acc[:, 0:NW, F:2 * F], tmp[:, :, :], h[:, :, :], g[:, :, :]):
                dve.tensor_tensor(xs[:, 0:NWIN, :], xs[:, 0:NWIN, :], v[:, 0:NWIN, :], ALU.add)
                dve.drain()
            dve.drain().then_inc(out_ready, 1)


_INS = ['x', 'src', 'dst', 'edge_attr_16', 'edge_attr_4', 'edge_type_90', 'edge_weight', 'L0_gnn_W1', 'L0_gnn_b1',
        'L0_gnn_W2', 'L0_gnn_b2', 'L1_gnn_Ws', 'L1_gnn_Wa', 'L1_gnn_weight', 'L1_gnn_w_comp', 'L2_gnn_enet_w',
        'L2_gnn_enet_b', 'L2_gnn_root', 'L2_gnn_bias', 'L2_gnn_gamma', 'L2_gnn_beta']


def kernel(**inputs):
    import numpy as np
    import concourse.bacc as bacc
    from concourse.bass_utils import run_bass_kernel_spmd

    nc = bacc.Bacc("TRN2", target_bir_lowering=False, num_devices=1)
    arrays, args = {}, []
    for name in _INS:
        a = np.ascontiguousarray(inputs[name])
        arrays[f"in_{name}"] = a
        args.append(nc.dram_tensor(f"in_{name}", a.shape, mybir.dt.from_np(a.dtype), kind="ExternalInput").ap())
    result = nc.dram_tensor("out_x", inputs["x"].shape, F32, kind="ExternalOutput").ap()
    build_program(nc, *args, result)
    r = run_bass_kernel_spmd(nc, [arrays], core_ids=[0])
    return r.results[0]["out_x"]
```
